# Optimizing a Trainium2 kernel written in Bass

```python
import numpy as np
import jax
import jax.numpy as jnp

def _softmax(x, axis=-1):
    return jax.nn.softmax(x, axis=axis)

def _gelu(x):
    return jax.nn.gelu(x, approximate=True)

def _silu(x):
    return jax.nn.silu(x)

def _sigmoid(x):
    return jax.nn.sigmoid(x)

def _layernorm(x, axis=-1, eps=1e-05):
    m = jnp.mean(x, axis=axis, keepdims=True)
    v = jnp.var(x, axis=axis, keepdims=True)
    return (x - m) / jnp.sqrt(v + eps)

def _scatter_add(tgt, idx, src, axis=0):
    return tgt.at[idx].add(src)

def _segment_sum(src, seg, n):
    return jax.ops.segment_sum(src, seg, n)
kernel_name = 'mk_prb_d2_jaxref_r8_9a049a'

def setup_inputs(seed: int=0):
    np.random.seed(seed)
    _w = jnp.asarray

    def _L0_attn_setup():
        import jax, jax.numpy as jnp
        import numpy as np
        EMB_DIM = 33
        FREQ = 10.0
        ORDER = 2

        def _hyena_filter(L, D, w1, b1, w2, b2, filt_bias, filt_decay):
            t = jnp.linspace(0.0, 1.0, L)[:, None]
            bands = jnp.linspace(0.0, EMB_DIM - 1.0, EMB_DIM)[None, :]
            pe = jnp.sin(t * bands * FREQ)
            h = jnp.sin(FREQ * (pe @ w1.T + b1)) @ w2.T + b2
            h = h.reshape(L, ORDER, D).transpose(1, 2, 0)
            t_window = jnp.linspace(0.0, 1.0, L)[None, None, :]
            decay = jnp.exp(-jnp.exp(filt_decay)[..., None] * t_window)
            h = h * decay + filt_bias[..., None]
            return h * (1.0 / L)

        def _depthwise_conv3(x, w, b):
            xp = jnp.pad(x, ((0, 0), (0, 0), (1, 1)))
            return w[:, 0, None] * xp[:, :, :-2] + w[:, 1, None] * xp[:, :, 1:-1] + w[:, 2, None] * xp[:, :, 2:] + b[:, None]
        key = jax.random.key(seed)
        ks = jax.random.split(key, 8)
        B, L, D = (2, 512, 128)
        OD = (ORDER + 1) * D
        std = 0.02
        return {'u': jax.random.normal(ks[0], (B, L, D), jnp.float32), 'w_in': jax.random.normal(ks[1], (OD, D), jnp.float32) * std, 'b_in': jnp.zeros((OD,), jnp.float32), 'conv_w': jax.random.normal(ks[2], (OD, 3), jnp.float32) * std, 'conv_b': jnp.zeros((OD,), jnp.float32), 'w1': jax.random.normal(ks[3], (64, EMB_DIM), jnp.float32) * std, 'b1': jnp.zeros((64,), jnp.float32), 'w2': jax.random.normal(ks[4], (ORDER * D, 64), jnp.float32) * std, 'b2': jnp.zeros((ORDER * D,), jnp.float32), 'filt_bias': jnp.zeros((ORDER, D), jnp.float32), 'filt_decay': jnp.ones((ORDER, D), jnp.float32) * -3.0, 'w_out': jax.random.normal(ks[5], (D, D), jnp.float32) * std, 'b_out': jnp.zeros((D,), jnp.float32)}
    _L0_attn_in = _L0_attn_setup()

    def _L0_ffn_setup():
        import jax, jax.numpy as jnp
        import numpy as np
        K = 4
        ROUTED_SCALING = 1.0
        NORM_TOPK = True

        def _gate(hidden_states, router_w, router_bias):
            logits = jnp.einsum('bsh,he->bse', hidden_states, router_w).astype(jnp.float32)
            scores = jax.nn.softmax(logits, axis=-1)
            corrected = scores + router_bias
            _, top_k_indices = jax.lax.top_k(corrected, K)
            top_k_weights = jnp.take_along_axis(scores, top_k_indices, axis=-1)
            if NORM_TOPK:
                top_k_weights = top_k_weights / (top_k_weights.sum(-1, keepdims=True) + 1e-20)
            top_k_weights = top_k_weights * ROUTED_SCALING
            return (top_k_weights.astype(hidden_states.dtype), top_k_indices)
        key = jax.random.key(seed)
        ks = jax.random.split(key, 9)
        B, S, H, E, I, IS = (2, 128, 128, 8, 64, 256)
        sc = 0.02
        return {'hidden_states': jax.random.normal(ks[0], (B, S, H), jnp.float32), 'router_w': jax.random.normal(ks[1], (H, E), jnp.float32) * sc, 'router_bias': jnp.zeros((), jnp.float32), 'gate_w': jax.random.normal(ks[2], (E, H, I), jnp.float32) * sc, 'up_w': jax.random.normal(ks[3], (E, H, I), jnp.float32) * sc, 'down_w': jax.random.normal(ks[4], (E, I, H), jnp.float32) * sc, 's_gate_w': jax.random.normal(ks[5], (H, IS), jnp.float32) * sc, 's_up_w': jax.random.normal(ks[6], (H, IS), jnp.float32) * sc, 's_down_w': jax.random.normal(ks[7], (IS, H), jnp.float32) * sc}
    _L0_ffn_in = _L0_ffn_setup()

    def _L1_attn_setup():
        import jax, jax.numpy as jnp
        import numpy as np
        HEADS = 16

        def _fm(t):
            return jax.nn.elu(t) + 1.0
        key = jax.random.key(seed)
        ks = jax.random.split(key, 9)
        B, N, D = (4, 1024, 128)
        s = 1.0 / np.sqrt(D)
        return {'x': jax.random.normal(ks[0], (B, N, D), dtype=jnp.float32), 'wq': jax.random.normal(ks[1], (D, D), dtype=jnp.float32) * s, 'bq': jnp.zeros((D,), dtype=jnp.float32), 'wk': jax.random.normal(ks[2], (D, D), dtype=jnp.float32) * s, 'bk': jnp.zeros((D,), dtype=jnp.float32), 'wv': jax.random.normal(ks[3], (D, D), dtype=jnp.float32) * s, 'bv': jnp.zeros((D,), dtype=jnp.float32), 'wo': jax.random.normal(ks[4], (D, D), dtype=jnp.float32) * s, 'bo': jnp.zeros((D,), dtype=jnp.float32)}
    _L1_attn_in = _L1_attn_setup()

    def _L1_ffn_setup():
        import jax, jax.numpy as jnp
        import numpy as np
        E, K, H, F, R = (8, 2, 128, 256, 64)
        B, S = (2, 256)
        key = jax.random.key(seed)
        k0, k1, k2, k3, k4 = jax.random.split(key, 5)
        return {'hidden_states': jax.random.normal(k0, (B, S, H), dtype=jnp.float32), 'W_A': jax.random.normal(k1, (E, R, H), dtype=jnp.float32) * 0.02, 'W_B': jax.random.normal(k2, (E, F, R), dtype=jnp.float32) * 0.02, 'W_up': jax.random.normal(k3, (E, F, H), dtype=jnp.float32) * 0.02, 'W_down': jax.random.normal(k4, (E, H, F), dtype=jnp.float32) * 0.02}
    _L1_ffn_in = _L1_ffn_setup()
    _d = {'L0_attn_u': _L0_attn_in['u'], 'L0_attn_w_in': _L0_attn_in['w_in'], 'L0_attn_b_in': _L0_attn_in['b_in'], 'L0_attn_conv_w': _L0_attn_in['conv_w'], 'L0_attn_conv_b': _L0_attn_in['conv_b'], 'L0_attn_w1': _L0_attn_in['w1'], 'L0_attn_b1': _L0_attn_in['b1'], 'L0_attn_w2': _L0_attn_in['w2'], 'L0_attn_b2': _L0_attn_in['b2'], 'L0_attn_filt_bias': _L0_attn_in['filt_bias'], 'L0_attn_filt_decay': _L0_attn_in['filt_decay'], 'L0_attn_w_out': _L0_attn_in['w_out'], 'L0_attn_b_out': _L0_attn_in['b_out'], 'L0_ffn_router_w': _L0_ffn_in['router_w'], 'L0_ffn_router_bias': _L0_ffn_in['router_bias'], 'L0_ffn_gate_w': _L0_ffn_in['gate_w'], 'L0_ffn_up_w': _L0_ffn_in['up_w'], 'L0_ffn_down_w': _L0_ffn_in['down_w'], 'L0_ffn_s_gate_w': _L0_ffn_in['s_gate_w'], 'L0_ffn_s_up_w': _L0_ffn_in['s_up_w'], 'L0_ffn_s_down_w': _L0_ffn_in['s_down_w'], 'L1_attn_wq': _L1_attn_in['wq'], 'L1_attn_bq': _L1_attn_in['bq'], 'L1_attn_wk': _L1_attn_in['wk'], 'L1_attn_bk': _L1_attn_in['bk'], 'L1_attn_wv': _L1_attn_in['wv'], 'L1_attn_bv': _L1_attn_in['bv'], 'L1_attn_wo': _L1_attn_in['wo'], 'L1_attn_bo': _L1_attn_in['bo'], 'L1_ffn_W_A': _L1_ffn_in['W_A'], 'L1_ffn_W_B': _L1_ffn_in['W_B'], 'L1_ffn_W_up': _L1_ffn_in['W_up'], 'L1_ffn_W_down': _L1_ffn_in['W_down']}
    _x0 = _d['L0_attn_u']
    _d['L0_attn_u'] = jax.random.normal(jax.random.fold_in(jax.random.key(seed), 1), (2, 2048, 128), dtype=_x0.dtype)
    del _x0
    return _d

def reference(L0_attn_u, L0_attn_w_in, L0_attn_b_in, L0_attn_conv_w, L0_attn_conv_b, L0_attn_w1, L0_attn_b1, L0_attn_w2, L0_attn_b2, L0_attn_filt_bias, L0_attn_filt_decay, L0_attn_w_out, L0_attn_b_out, L0_ffn_router_w, L0_ffn_router_bias, L0_ffn_gate_w, L0_ffn_up_w, L0_ffn_down_w, L0_ffn_s_gate_w, L0_ffn_s_up_w, L0_ffn_s_down_w, L1_attn_wq, L1_attn_bq, L1_attn_wk, L1_attn_bk, L1_attn_wv, L1_attn_bv, L1_attn_wo, L1_attn_bo, L1_ffn_W_A, L1_ffn_W_B, L1_ffn_W_up, L1_ffn_W_down):

    def _L0_attn_ref(u, w_in, b_in, conv_w, conv_b, w1, b1, w2, b2, filt_bias, filt_decay, w_out, b_out):
        import jax, jax.numpy as jnp
        import numpy as np
        EMB_DIM = 33
        FREQ = 10.0
        ORDER = 2

        def _hyena_filter(L, D, w1, b1, w2, b2, filt_bias, filt_decay):
            t = jnp.linspace(0.0, 1.0, L)[:, None]
            bands = jnp.linspace(0.0, EMB_DIM - 1.0, EMB_DIM)[None, :]
            pe = jnp.sin(t * bands * FREQ)
            h = jnp.sin(FREQ * (pe @ w1.T + b1)) @ w2.T + b2
            h = h.reshape(L, ORDER, D).transpose(1, 2, 0)
            t_window = jnp.linspace(0.0, 1.0, L)[None, None, :]
            decay = jnp.exp(-jnp.exp(filt_decay)[..., None] * t_window)
            h = h * decay + filt_bias[..., None]
            return h * (1.0 / L)

        def _depthwise_conv3(x, w, b):
            xp = jnp.pad(x, ((0, 0), (0, 0), (1, 1)))
            return w[:, 0, None] * xp[:, :, :-2] + w[:, 1, None] * xp[:, :, 1:-1] + w[:, 2, None] * xp[:, :, 2:] + b[:, None]
        B, L, D = u.shape
        res = u @ w_in.T + b_in
        res = res.transpose(0, 2, 1)
        res = _depthwise_conv3(res, conv_w, conv_b)
        res = res.reshape(B, ORDER + 1, D, L)
        x = res[:, :-1]
        v = res[:, -1]
        h = _hyena_filter(L, D, w1, b1, w2, b2, filt_bias, filt_decay)
        n_fft = 2 * L
        for n in range(ORDER):
            v_fft = jnp.fft.rfft(v, n=n_fft, axis=-1)
            h_fft = jnp.fft.rfft(h[n], n=n_fft, axis=-1)
            y = jnp.fft.irfft(v_fft * h_fft, n=n_fft, axis=-1)[..., :L]
            v = y * x[:, n]
        return v.transpose(0, 2, 1) @ w_out.T + b_out

    def _L0_ffn_ref(hidden_states, router_w, router_bias, gate_w, up_w, down_w, s_gate_w, s_up_w, s_down_w):
        import jax, jax.numpy as jnp
        import numpy as np
        K = 4
        ROUTED_SCALING = 1.0
        NORM_TOPK = True

        def _gate(hidden_states, router_w, router_bias):
            logits = jnp.einsum('bsh,he->bse', hidden_states, router_w).astype(jnp.float32)
            scores = jax.nn.softmax(logits, axis=-1)
            corrected = scores + router_bias
            _, top_k_indices = jax.lax.top_k(corrected, K)
            top_k_weights = jnp.take_along_axis(scores, top_k_indices, axis=-1)
            if NORM_TOPK:
                top_k_weights = top_k_weights / (top_k_weights.sum(-1, keepdims=True) + 1e-20)
            top_k_weights = top_k_weights * ROUTED_SCALING
            return (top_k_weights.astype(hidden_states.dtype), top_k_indices)
        B, S, H = hidden_states.shape
        tk_w, tk_i = _gate(hidden_states, router_w, router_bias)
        hf = hidden_states.reshape(-1, H)
        tk_w = tk_w.reshape(-1, K)
        tk_i = tk_i.reshape(-1, K)
        gate_all = jnp.einsum('nh,ehi->nei', hf, gate_w)
        up_all = jnp.einsum('nh,ehi->nei', hf, up_w)
        act = jax.nn.silu(gate_all) * up_all
        down_all = jnp.einsum('nei,eih->neh', act, down_w)
        sel = jnp.take_along_axis(down_all, tk_i[:, :, None], axis=1)
        routed = (sel * tk_w[:, :, None]).sum(axis=1).reshape(B, S, H)
        g = jnp.einsum('bsh,hm->bsm', hidden_states, s_gate_w)
        u = jnp.einsum('bsh,hm->bsm', hidden_states, s_up_w)
        shared = jnp.einsum('bsm,mh->bsh', jax.nn.silu(g) * u, s_down_w)
        return routed + shared

    def _L1_attn_ref(x, wq, bq, wk, bk, wv, bv, wo, bo):
        import jax, jax.numpy as jnp
        import numpy as np
        HEADS = 16

        def _fm(t):
            return jax.nn.elu(t) + 1.0
        B, N, D = x.shape
        H = HEADS
        Dh = D // H
        q = _fm((x @ wq + bq).reshape(B, N, H, Dh))
        k = _fm((x @ wk + bk).reshape(B, N, H, Dh))
        v = (x @ wv + bv).reshape(B, N, H, Dh)
        kv = jnp.einsum('bnhd,bnhe->bhde', k, v)
        z = 1.0 / (jnp.einsum('bnhd,bhd->bnh', q, k.sum(axis=1)) + 1e-06)
        scores = jnp.einsum('bnhd,bhde,bnh->bnhe', q, kv, z)
        out = scores.reshape(B, N, D) @ wo + bo
        return out

    def _L1_ffn_ref(hidden_states, W_A, W_B, W_up, W_down):
        import jax, jax.numpy as jnp
        import numpy as np
        E, K, H, F, R = (8, 2, 128, 256, 64)
        B, S = (2, 256)
        orig_shape = hidden_states.shape
        x = hidden_states.reshape(-1, orig_shape[-1])
        num_experts = W_A.shape[0]
        gate_hidden = jnp.einsum('nh,erh->ner', x, W_A)
        scores = jnp.sqrt(jnp.sum(gate_hidden * gate_hidden, axis=-1))
        topk_scores, topk_idx = jax.lax.top_k(scores, K)
        topk_w = jax.nn.softmax(topk_scores, axis=-1)
        w_full = jnp.sum(jax.nn.one_hot(topk_idx, num_experts, dtype=topk_w.dtype) * topk_w[..., None], axis=1)
        g = jnp.einsum('ner,efr->nef', gate_hidden, W_B)
        up = jnp.einsum('nh,efh->nef', x, W_up)
        y = jnp.einsum('nef,ehf->neh', jax.nn.silu(g) * up, W_down)
        out = jnp.einsum('neh,ne->nh', y, w_full)
        return out.reshape(orig_shape)
    x = L0_attn_u
    xn = _layernorm(x, axis=-1)
    x = x + _L0_attn_ref(xn, L0_attn_w_in, L0_attn_b_in, L0_attn_conv_w, L0_attn_conv_b, L0_attn_w1, L0_attn_b1, L0_attn_w2, L0_attn_b2, L0_attn_filt_bias, L0_attn_filt_decay, L0_attn_w_out, L0_attn_b_out) + _L0_ffn_ref(xn, L0_ffn_router_w, L0_ffn_router_bias, L0_ffn_gate_w, L0_ffn_up_w, L0_ffn_down_w, L0_ffn_s_gate_w, L0_ffn_s_up_w, L0_ffn_s_down_w)
    xn = _layernorm(x, axis=-1)
    x = x + _L1_attn_ref(xn, L1_attn_wq, L1_attn_bq, L1_attn_wk, L1_attn_bk, L1_attn_wv, L1_attn_bv, L1_attn_wo, L1_attn_bo) + _L1_ffn_ref(xn, L1_ffn_W_A, L1_ffn_W_B, L1_ffn_W_up, L1_ffn_W_down)
    return x

_drawn_inputs = setup_inputs


def setup_inputs(seed=0):
    import zlib

    import numpy as np

    out = dict(_drawn_inputs(seed))
    spreads = {'L0_attn_b_in': (0.0, 0.8),
     'L0_attn_conv_b': (0.0, 0.8),
     'L0_attn_b1': (0.0, 0.8),
     'L0_attn_b2': (0.0, 0.8),
     'L0_attn_filt_bias': (0.0, 0.8),
     'L0_attn_filt_decay': (-3.0, 0.6),
     'L0_attn_b_out': (0.0, 0.1),
     'L1_attn_bq': (0.0, 2.0),
     'L1_attn_bk': (0.0, 2.0),
     'L1_attn_bv': (0.0, 0.549),
     'L1_attn_bo': (0.0, 0.634)}
    factors = {'L0_attn_w_in': 8.0,
     'L0_attn_conv_w': 8.0,
     'L0_attn_w1': 8.0,
     'L0_attn_w2': 8.0,
     'L0_attn_w_out': 8.0,
     'L0_ffn_router_w': 8.0,
     'L0_ffn_gate_w': 8.0,
     'L0_ffn_up_w': 8.0,
     'L0_ffn_down_w': 8.0,
     'L0_ffn_s_gate_w': 6.995,
     'L0_ffn_s_up_w': 6.896,
     'L0_ffn_s_down_w': 6.924,
     'L1_attn_wq': 34.76,
     'L1_ffn_W_A': 8.0,
     'L1_ffn_W_B': 8.0,
     'L1_ffn_W_up': 8.0,
     'L1_ffn_W_down': 8.0,
     'L1_attn_wk': 8.0,
     'L1_attn_wv': 5.173,
     'L1_attn_wo': 2.687}
    for name, (base, spread) in spreads.items():
        noise = np.random.default_rng([zlib.crc32(name.encode()), seed]).standard_normal(out[name].shape)
        drawn = base * np.exp(spread * noise) if base else spread * noise
        out[name] = jnp.asarray(drawn.astype(out[name].dtype))
    for name, factor in factors.items():
        out[name] = (out[name] * factor).astype(out[name].dtype)
    return out
```

```python
import math

import numpy as np

import concourse.bass as bass
from concourse import mybir
from contextlib import ExitStack

F32 = mybir.dt.float32
ALU = mybir.AluOpType
ACT = mybir.ActivationFunctionType
AX = mybir.AxisListType

P = 128
B, L, D = 2, 2048, 128
NI = L // P
T = B * NI
TOK = B * L
CH = 512
NCH = TOK // CH
TPC = CH // P
OD = 3 * D
K1 = 2 * NI
NK = K1 // 2 + 1
EMB, FH = 33, 64
E0, I0, IS = 8, 64, 256
M0 = E0 * I0 // P
N0 = M0 + IS // P
E1, R1, F1W = 8, 64, 256
M1 = E1 * F1W // P
PAIRS = E1 // 2
EPS = 1e-5
MAGIC = 12582912.0
PI2_HI = 6.28125
PI2_LO = 2 * math.pi - PI2_HI
PI_IN = 3.1415925


def hyena_moe_program(nc, x, w_inT, conv_w, conv_b, b_in, peT, w1T, b1, w2b, fdec, fbias, w_outT, b_out,
                      rout_w, rout_b, gate0, up0, down0, wq, wkv, bkv, bq, wo, bo, w_a, w_b, w_up, w_dn,
                      dft_f, dft_i, dft_b, idft_b, negt, ident, before, heads, expert_of, edges,
                      out):
    wexp = [nc.dram_tensor(f"expert_weights_{n}", (T, 8, P), F32, kind="Internal").ap() for n in range(2)]
    ctx = ExitStack()
    with ctx:
        words = [0]
        arena = ctx.enter_context(nc.sbuf_tensor("arena", [P, 53000], F32))

        def region(n):
            at = words[0]
            words[0] += n
            assert words[0] <= 53000, words[0]
            return at

        def view(at, *dims, parts=P):
            n = int(np.prod(dims))
            v = arena[0:parts, at:at + n]
            if len(dims) == 1:
                return v
            names = "abcd"[:len(dims)]
            return v.rearrange("p (%s) -> p %s" % (" ".join(names), " ".join(names)),
                               **{c: d for c, d in zip(names, dims)})

        IDENT = view(region(P), P)
        DFTB = view(region(K1 * 8), K1 * 8)
        IDFTB = view(region(NI * 4), NI * 4)
        NEGT = view(region(NI), NI)
        BEFORE = view(region(64), 8, 8)
        HEADS = view(region(P), P)
        EXPOF = view(region(E1 * PAIRS), PAIRS, E1)
        EDGES = view(region(2), 2)
        ROUTB = view(region(1), 1)
        B1 = view(region(1), 1, parts=FH)
        BQ = view(region(1), 1)
        BO = view(region(1), 1)
        BOUT = view(region(D), D)
        ROUTW = view(region(E0), E0)
        MV = view(region(2 * T), T, 2)
        RSTD = view(region(T), T)
        STAT = view(region(6 * T), T, 6)
        SHIFT = view(region(2 * P), 2, P)

        rX = region(T * D)
        rG = region(T * 2 * D)
        rV = region(T * D)
        rH = region(NK * 2 * 2 * D)
        rA = region(K1 * 2 * D + 8)
        rY = region(4096)
        rF = region(NK * 3 * P)
        rI = region(NK * 3 * P)

        X = view(rX, T, D)
        G = view(rG, T, 2, D)
        V = view(rV, T, D)
        VG = view(rV, B * 16, NI, 8)
        H = view(rH, NK, 2, 2 * D)
        A = view(rA, 2 * D // 4, K1, 4)
        XNT = view(rA, TOK + 2)
        XN = view(rY, T, D)
        MF = view(rF, NK, 3, P)
        MI = view(rI, NK, 3, P)
        FT = view(rY, 2, CH)
        ZT = view(rY, 2, CH)
        T1 = view(rY + 1024, 2, 2, 2 * D)
        T2 = view(rY + 2048, 2, 2, 2 * D)
        YS = view(rY + 3072, 2, 2, 2 * D)
        WRES = view(rH + 4096, 3, OD)
        RBIAS = view(rH + 4096 + 3 * OD, 3, OD)
        CWB = view(rH + 4096 + 6 * OD, 3, OD)
        BINB = view(rH + 4096 + 9 * OD, OD)
        CBB = view(rH + 4096 + 10 * OD, OD)
        WIN = view(rH + 3712, OD)
        PET = view(rH, L, parts=EMB)
        SINT = view(rH + L, L, parts=FH + 1)
        SIN64 = view(rH + L, L, parts=FH)
        DEC = view(rH + 2 * L, NI, 2 * D)
        ZF = view(rA, L, parts=FH)
        ZN = view(rA + L, L, parts=FH)
        HT = view(rY, 2 * D // 8, NI, 8)
        r0 = rA + TOK + 6
        GW0 = view(r0, N0, P)
        UW0 = view(r0 + N0 * P, N0, P)
        DW0 = view(r0 + 2 * N0 * P, N0, P)
        WB0 = view(r0 + 3 * N0 * P, M0, CH)
        SG0 = view(r0 + 3 * N0 * P + M0 * CH, 2, CH)
        AM0 = view(r0 + 3 * N0 * P + (M0 + 2) * CH, 3, CH)
        assert r0 + 3 * N0 * P + (M0 + 5) * CH <= rF
        small = region(2 * 2 * D + FH + 2 * D + D)
        FDB = view(small, 2 * D)
        FBB = view(small + 2 * D, 2 * D)
        W1S = view(small + 4 * D, FH, parts=EMB)
        W2S = view(small + 4 * D + FH, 2 * D, parts=FH + 1)
        WOUT = view(small + 6 * D + FH, D)

        def router_scratch(at):
            return (view(at, T, 8), view(at + 256, T, 8), view(at + 512, T, 8), view(at + 768, T, 8),
                    view(at + 1024, T * 8), view(at + 1024, T, 8), view(at + 1280, 2, P), view(at + 1536, T),
                    view(at + 1536 + T, T))

        ROUTER = [router_scratch(rH + L), router_scratch(rA + TOK + 8)]
        CMP = [(view(rI, T, 8, 8), view(rI + 2048, T, 8, 8)), (view(rY, T, 8, 8), view(rY + 2048, T, 8, 8))]
        XNT1 = view(rA, TOK)
        GH = view(rG, PAIRS, TOK)
        assert rG + PAIRS * TOK <= rH + 4096
        ATT = view(rH + 4096, TOK)
        WBC1 = view(rY, E1, CH)
        rW = rF
        WA1 = view(rW, PAIRS, P)
        WB1 = view(rW + 512, M1, P)
        UP1 = view(rW + 512 + 2048, M1, P)
        DN1 = view(rW + 512 + 4096, M1, P)
        WQ = view(rW + 6656, P)
        WKV = view(rW + 6784, 2 * P)
        WO = view(rW + 7040, P)
        BKV = view(rW + 7168, 2 * P)
        rr = rW + 7424
        assert rr + 5632 <= rI + NK * 3 * P + 0
        SG1 = view(rr, 2, CH)
        AM1 = view(rr + 1024, 3, CH)
        OT1 = view(rr + 2560, CH)
        ST1 = view(rr + 3072, 2, TPC, D)
        KVS = view(rr, 3, 2, 2 * P + 1)
        KEX = view(rr + 1542 + 2, 3, 2, P)
        SQ1 = view(rr, 2, CH)
        QMN = view(rr, 2, CH)
        QEX = view(rr + 1024, 2, CH)
        QPS = view(rr + 2048, 2, CH)
        DEN = view(rr + 3072, CH)
        KVB = view(rr + 4096, B, P)
        KSB = view(rr + 4096 + 256, B, P)
        KSC = view(rr + 4096 + 512, B, 1)

        PS = [ctx.enter_context(nc.psum_tensor(f"bank{n}", [P, CH], F32)) for n in range(8)]

        def bank(n, *dims, at=0):
            n_words = int(np.prod(dims))
            v = PS[n][:, at:at + n_words]
            names = "abcd"[:len(dims)]
            return v if len(dims) == 1 else v.rearrange(
                "p (%s) -> p %s" % (" ".join(names), " ".join(names)), **{c: d for c, d in zip(names, dims)})

        def sem(name):
            return ctx.enter_context(nc.semaphore(name))

        ld_const = sem("ld_const")
        ld_x = sem("ld_x")
        ld_res = sem("ld_res")
        ld_w0 = sem("ld_w0")
        ld_filt = sem("ld_filt")
        ld_pe = sem("ld_pe")
        ld_dft = sem("ld_dft")
        ld_idft = sem("ld_idft")
        ld_w1 = sem("ld_w1")
        ld_wexp0 = [sem(f"ld_wexp0_{m}") for m in range(M0)]
        ld_wexp1 = [sem(f"ld_wexp1_{e}") for e in range(E1)]
        st_wexp = sem("st_wexp")
        st_out = sem("st_out")
        ln_stat = sem("ln_stat")
        ln_var = sem("ln_var")
        ln_std = sem("ln_std")
        ln_xn = sem("ln_xn")
        lnt_done = sem("lnt_done")
        lnt_dve = sem("lnt_dve")
        lnt_act = sem("lnt_act")
        rt_logit = sem("rt_logit")
        rt_sub = sem("rt_sub")
        rt_exp = sem("rt_exp")
        rt_w = sem("rt_w")
        rt_tr = sem("rt_tr")
        rt_out = sem("rt_out")
        dve_chain = sem("dve_chain")
        res_w = sem("res_w")
        pool_chain = sem("pool_chain")
        edge_set = sem("edge_set")
        res_mm = sem("res_mm")
        res_out = sem("res_out")
        bout_in = sem("bout_in")
        g_mm = sem("g_mm")
        u_mm = sem("u_mm")
        silu_done = sem("silu_done")
        mult_done = sem("mult_done")
        weighted = sem("weighted")
        down_mm = sem("down_mm")
        x_added = sem("x_added")
        z_mm = sem("z_mm")
        z_wrapped = sem("z_wrapped")
        sin_done = sem("sin_done")
        ones_row = sem("ones_row")
        dec_exp = sem("dec_exp")
        h_mm = sem("h_mm")
        h_dec = sem("h_dec")
        h_ready = sem("h_ready")
        spec_act = sem("spec_act")
        spec_dve = sem("spec_dve")
        f0_mm = sem("f0_mm")
        ft_in = sem("ft_in")
        f1_mm = sem("f1_mm")
        a_in = [sem("a_in_dve"), sem("a_in_act")]
        f2_mm = sem("f2_mm")
        prod_in = sem("prod_in")
        y_in = sem("y_in")
        i1_mm = sem("i1_mm")
        z_in = sem("z_in")
        i2_mm = sem("i2_mm")
        zt_in = sem("zt_in")
        i3_mm = sem("i3_mm")
        gated = sem("gated")
        vt_mm = sem("vt_mm")
        vt_in = sem("vt_in")
        o_mm = sem("o_mm")
        o_added = sem("o_added")
        wb_zero = sem("wb_zero")
        one_set = sem("one_set")
        kv_mm = sem("kv_mm")
        kv_bias = sem("kv_bias")
        k_min = sem("k_min")
        k_exp = sem("k_exp")
        k_fm = sem("k_fm")
        kvs_mm = sem("kvs_mm")
        kv_mask = sem("kv_mask")
        gh_mm = sem("gh_mm")
        gh_in = sem("gh_in")
        sq_in = sem("sq_in")
        sc_mm = sem("sc_mm")
        q_mm = sem("q_mm")
        q_min = sem("q_min")
        q_relu = sem("q_relu")
        q_exp = sem("q_exp")
        q_fm = sem("q_fm")
        nd_mm = sem("nd_mm")
        att_in = sem("att_in")
        g1_mm = sem("g1_mm")
        u1_mm = sem("u1_mm")
        silu1 = sem("silu1")
        mult1 = sem("mult1")
        weighted1 = sem("weighted1")
        down1_mm = sem("down1_mm")
        ot_in = sem("ot_in")
        y_mm = sem("y_mm")
        y_sum = sem("y_sum")

        N_CONST = 14 * 16
        block = ctx.enter_context(nc.Block())

        def a_bank(K):
            return PS[2 + K % 4][:, :]

        def a_slot(n):
            return arena[:, rA + CH * n:rA + CH * (n + 1)]

        def a_rows(s, n):
            return A[:, :, s:s + n, :].rearrange("p g s c -> p s g c")

        def h_blocks(j):
            return HT[:, :, 2 * j:2 * j + 2, :].rearrange("p g i c -> p i g c")

        def z_slots(k):
            return (0, 1) if k == 0 else (1, 1) if k == NK - 1 else (2 * k, 2)

        def add_down(dve, ck):
            dve.wait_ge(down_mm, N0 * (ck + 1))
            xs = X[:, TPC * ck:TPC * (ck + 1), :]
            nc.vector.tensor_tensor(out=xs, in0=bank(4 + ck % 2, TPC, D), in1=xs, op=ALU.add).then_inc(x_added, 1)

        outv = out.rearrange("b (i a) c -> a (b i) c", a=P)

        def store(sp, ck):
            sp.wait_ge(y_sum, ck + 1)
            sp.dma_start(outv[:, TPC * ck:TPC * (ck + 1), :], ST1[:, ck % 2]).then_inc(st_out, 16)

        @block.sync
        def _(sp):
            xv = x.rearrange("b (i a) c -> a (b i) c", a=P)
            for n in range(4):
                sp.dma_start(X[:, 8 * n:8 * n + 8, :], xv[:, 8 * n:8 * n + 8, :]).then_inc(ld_x, 16)
            for dst, src in ((IDENT, ident), (ROUTW, rout_w), (ROUTB, rout_b.partition_broadcast(P)),
                             (BEFORE, before), (EDGES, edges), (BOUT, b_out.partition_broadcast(P)), (DFTB, dft_b),
                             (IDFTB, idft_b), (NEGT, negt), (HEADS, heads), (EXPOF, expert_of), (B1, b1), (BQ, bq),
                             (BO, bo)):
                sp.dma_start(dst, src).then_inc(ld_const, 16)
            for dst, src in ((W1S, w1T), (W2S, w2b), (FDB, fdec.partition_broadcast(P)),
                             (FBB, fbias.partition_broadcast(P)), (WOUT, w_outT)):
                sp.dma_start(dst, src).then_inc(ld_filt, 16)
            sp.dma_start(PET, peT).then_inc(ld_pe, 16)
            sp.wait_ge(lnt_done, NCH)
            for dst, src in ((GW0, gate0), (UW0, up0), (DW0, down0)):
                sp.dma_start(dst, src).then_inc(ld_w0, 16)
            sp.dma_start(MF, dft_f).then_inc(ld_dft, 16)
            sp.wait_ge(rt_out, 2)
            sp.dma_start(wexp[0].rearrange("(n t) e a -> (t e) n a", n=2), ROUTER[0][6]).then_inc(st_wexp, 16)
            sp.wait_ge(st_wexp, 16)
            sp.dma_start(MI, dft_i).then_inc(ld_idft, 16)
            for ck in range(NCH):
                for m in range(M0):
                    if ck:
                        sp.wait_ge(weighted, M0 * (ck - 1) + m + 1)
                    for e2 in range(2):
                        src = wexp[0][TPC * ck:TPC * (ck + 1), 2 * m + e2, :]
                        sp.dma_start(WB0[64 * e2:64 * e2 + 64, m, :].rearrange("p (t a) -> p t a", a=P),
                                     src.partition_broadcast(64)).then_inc(ld_wexp0[m], 16)
            sp.wait_ge(i1_mm, 2 * NK)
            sp.wait_ge(wb_zero, 1)
            for e in range(E1):
                h0 = 64 * (e % 2)
                sp.dma_start(WB1[h0:h0 + 64, 2 * e:2 * e + 2, :], w_b[e]).then_inc(ld_w1, 16)
            for dst, src in ((WA1, w_a), (UP1, w_up), (DN1, w_dn), (WQ, wq), (WKV, wkv), (WO, wo),
                             (BKV, bkv.partition_broadcast(P))):
                sp.dma_start(dst, src).then_inc(ld_w1, 16)
            sp.wait_ge(rt_out, 4)
            sp.dma_start(wexp[1].rearrange("(n t) e a -> (t e) n a", n=2), ROUTER[1][6]).then_inc(st_wexp, 16)
            sp.wait_ge(st_wexp, 32)
            for ck in range(NCH):
                for e in range(E1):
                    if ck:
                        sp.wait_ge(weighted1, M1 * (ck - 1) + 2 * e + 2)
                    sp.dma_start(WBC1[:, e, :].rearrange("p (t a) -> p t a", a=P),
                                 wexp[1][TPC * ck:TPC * (ck + 1), e, :].partition_broadcast(P))\
                      .then_inc(ld_wexp1[e], 16)
                if ck:
                    store(sp, ck - 1)
            store(sp, NCH - 1)
            sp.wait_ge(st_out, 16 * NCH)

        @block.gpsimd
        def _(pool):
            done = [0]

            def link(ins):
                done[0] += 1
                ins.then_inc(pool_chain, 1)
                pool.wait_ge(pool_chain, done[0])

            for dst, src in ((WIN, w_inT), (CWB, conv_w.rearrange("k o -> (k o)").partition_broadcast(P)
                                            .rearrange("p (k o) -> p k o", k=3)),
                             (BINB, b_in.partition_broadcast(P)), (CBB, conv_b.partition_broadcast(P))):
                pool.dma_start(dst, src).then_inc(ld_res, 16)
            pool.wait_ge(ld_res, 64)
            pool.wait_ge(ld_const, N_CONST)
            for d in range(3):
                link(nc.gpsimd.tensor_tensor(out=WRES[:, d, :], in0=WIN, in1=CWB[:, d, :], op=ALU.mult))
            for d in range(3):
                link(nc.gpsimd.tensor_tensor(out=CWB[:, d, :], in0=BINB, in1=CWB[:, d, :], op=ALU.mult))
            link(nc.gpsimd.tensor_tensor(out=RBIAS[:, 0, :], in0=CWB[:, 0, :], in1=CWB[:, 1, :], op=ALU.add))
            link(nc.gpsimd.tensor_tensor(out=RBIAS[:, 0, :], in0=RBIAS[:, 0, :], in1=CWB[:, 2, :], op=ALU.add))
            link(nc.gpsimd.tensor_tensor(out=RBIAS[:, 0, :], in0=RBIAS[:, 0, :], in1=CBB, op=ALU.add))
            for n, d in ((1, 0), (2, 2)):
                link(nc.gpsimd.tensor_scalar(out=CWB[:, d, :], in0=CWB[:, d, :], scalar1=EDGES[:, n - 1:n],
                                             scalar2=None, op0=ALU.mult))
                link(nc.gpsimd.tensor_tensor(out=RBIAS[:, n, :], in0=RBIAS[:, 0, :], in1=CWB[:, d, :],
                                             op=ALU.subtract))
            nc.gpsimd.memset(SHIFT[:, :, :], 0.0).then_inc(res_w, 1)
            pool.wait_ge(ln_xn, 1)
            for n in range(NCH):
                ins = nc.gpsimd.tensor_tensor(out=X[:, TPC * n:TPC * (n + 1), :], in0=X[:, TPC * n:TPC * (n + 1), :],
                                              in1=BOUT.unsqueeze(1).broadcast_to((P, TPC, D)), op=ALU.add)
            ins.then_inc(bout_in, 1)

            for ck in range(NCH):
                for m in range(M0):
                    n = N0 * ck + m
                    pool.wait_ge(mult_done, n + 1)
                    pool.wait_ge(ld_wexp0[m], 32 * (ck + 1))
                    nc.gpsimd.tensor_tensor(out=AM0[:, n % 3, :], in0=AM0[:, n % 3, :], in1=WB0[:, m, :],
                                            op=ALU.mult).then_inc(weighted, 1)
            for j in range(NI // 2):
                pool.wait_ge(h_dec, j + 1)
                hv = h_blocks(j)
                nc.gpsimd.tensor_tensor(out=hv, in0=hv, in1=FBB.rearrange("p (g c) -> p g c", c=8).unsqueeze(1)
                                        .broadcast_to((P, 2, 2 * D // 8, 8)),
                                        op=ALU.add).then_inc(h_ready, 1)
            for c in range(2):
                for k in range(NK):
                    q = NK * c + k
                    pool.wait_ge(prod_in, q + 1)
                    if q >= 2:
                        pool.wait_ge(i1_mm, q - 1)
                    s = q % 2
                    nc.gpsimd.tensor_tensor(out=YS[:, s, 0, :], in0=T1[:, s, 0, :], in1=T2[:, s, 1, :],
                                            op=ALU.subtract)
                    nc.gpsimd.tensor_tensor(out=YS[:, s, 1, :], in0=T1[:, s, 1, :], in1=T2[:, s, 0, :],
                                            op=ALU.add).then_inc(y_in, 1)
            pool.wait_ge(i1_mm, 2 * NK)
            nc.gpsimd.memset(WB1[:, :, :], 0.0).then_inc(wb_zero, 1)
            nc.gpsimd.memset(KVS[:, :, :, 2 * P:2 * P + 1], 1.0).then_inc(one_set, 1)
            for j in range(T // 2):
                pool.wait_ge(kv_bias, j + 1)
                if j >= 3:
                    pool.wait_ge(k_fm, j - 2)
                nc.gpsimd.tensor_scalar(out=KEX[:, j % 3], in0=KVS[:, j % 3, :, 0:P], scalar1=0.0, scalar2=None,
                                        op0=ALU.min).then_inc(k_min, 1)
            for n in range(NCH * M1):
                ck, m = divmod(n, M1)
                pool.wait_ge(mult1, n + 1)
                pool.wait_ge(ld_wexp1[m // 2], 16 * (ck + 1))
                nc.gpsimd.tensor_tensor(out=AM1[:, n % 3, :], in0=AM1[:, n % 3, :], in1=WBC1[:, m // 2, :],
                                        op=ALU.mult).then_inc(weighted1, 1)

        @block.scalar
        def _(act):
            def norm_std(layer):
                act.wait_ge(ln_var, layer + 1)
                nc.scalar.activation(RSTD, RSTD, ACT.Sqrt).then_inc(ln_std, 1)

            def norm_copies(layer, dst):
                for j in range(1, NCH, 2):
                    act.wait_ge(lnt_done, NCH * layer + j + 1)
                    nc.scalar.activation(dst[:, CH * j:CH * (j + 1)], PS[j % 4][:, :], ACT.Copy)\
                      .then_inc(lnt_act, 1)

            norm_std(0)
            norm_copies(0, XNT[:, 1:1 + TOK])
            act.wait_ge(rt_sub, 1)
            nc.scalar.activation(ROUTER[0][1], ROUTER[0][1], ACT.Exp).then_inc(rt_exp, 1)
            for n in range(NCH * N0):
                act.wait_ge(g_mm, n + 1)
                if n >= 2:
                    act.wait_ge(mult_done, n - 1)
                nc.scalar.activation(SG0[:, n % 2, :], PS[n % 2][:, :], ACT.Silu).then_inc(silu_done, 1)
            act.wait_ge(ld_filt, 80)
            act.wait_ge(res_out, T)
            nc.scalar.activation(FDB, FDB, ACT.Exp).then_inc(dec_exp, 1)
            act.wait_ge(dec_exp, 1)
            for i in range(NI):
                nc.scalar.activation(DEC[:, i, :], FDB, ACT.Exp, scale=NEGT[:, i:i + 1]).then_inc(dec_exp, 1)
            act.wait_ge(z_wrapped, 1)
            nc.scalar.activation(SIN64, ZF, ACT.Sin).then_inc(sin_done, 1)

            def block_copies(t):
                def ft(j):
                    J = 8 * t + j
                    act.wait_ge(f0_mm, J + 1)
                    if J >= 2:
                        act.wait_ge(f1_mm, 2 * (J - 1))
                    if t and j < 2:
                        act.wait_ge(i3_mm, 16 * (t - 1))
                    nc.scalar.activation(FT[:, J % 2, :], PS[J % 2][:, :], ACT.Copy).then_inc(ft_in, 1)

                def a(j):
                    K = 16 * t + 2 * j + 1
                    act.wait_ge(f1_mm, K + 1)
                    nc.scalar.activation(a_slot(2 * j + 1), a_bank(K), ACT.Copy).then_inc(a_in[1], 1)

                ft(0)
                for j in range(8):
                    if j < 7:
                        ft(j + 1)
                    a(j)

            block_copies(0)
            for k in range(1, NK, 2):
                act.wait_ge(f2_mm, k + 1)
                nc.scalar.activation(H[:, k], bank(k % 3, 2, 2 * D), ACT.Copy).then_inc(spec_act, 1)
            for c in range(2):
                block_copies(c + 1)
                for k in range(NK):
                    q = NK * c + k
                    act.wait_ge(i1_mm, q + 1)
                    s, n = z_slots(k)
                    nc.scalar.activation(a_rows(s, n), bank(3 + q % 3, n, 2 * D // 4, 4), ACT.Copy).then_inc(z_in, 1)
                for p in range(16):
                    q = 16 * c + p
                    act.wait_ge(i2_mm, q + 1)
                    if q >= 2:
                        act.wait_ge(i3_mm, q - 1)
                    nc.scalar.activation(ZT[:, q % 2, :], PS[6 + q % 2][:, :], ACT.Copy).then_inc(zt_in, 1)
            for j in range(NCH):
                act.wait_ge(vt_mm, j + 1)
                if j >= 2:
                    act.wait_ge(o_mm, j - 1)
                nc.scalar.activation(FT[:, j % 2, :], PS[j % 2][:, :], ACT.Copy).then_inc(vt_in, 1)
            norm_std(1)
            norm_copies(1, XNT1)
            for j in range(T // 2):
                act.wait_ge(k_min, j + 1)
                nc.scalar.activation(KEX[:, j % 3], KEX[:, j % 3], ACT.Exp).then_inc(k_exp, 1)
            for n in range(NCH * PAIRS):
                ck, m = divmod(n, PAIRS)
                act.wait_ge(gh_mm, n + 1)
                nc.scalar.activation(GH[:, m, CH * ck:CH * (ck + 1)], PS[n % 3][:, :], ACT.Copy).then_inc(gh_in, 1)
            for ck in range(NCH):
                act.wait_ge(q_min, ck + 1)
                if ck >= 2:
                    act.wait_ge(q_fm, ck - 1)
                nc.scalar.activation(QPS[:, ck % 2, :], PS[ck % 2][:, :], ACT.Relu, bias=BQ).then_inc(q_relu, 1)
                nc.scalar.activation(QEX[:, ck % 2, :], QMN[:, ck % 2, :], ACT.Exp).then_inc(q_exp, 1)
            LOG, SCO = ROUTER[1][:2]
            act.wait_ge(rt_sub, 2)
            nc.scalar.activation(SCO, LOG, ACT.Sqrt).then_inc(rt_exp, 1)
            act.wait_ge(rt_sub, 3)
            nc.scalar.activation(SCO, SCO, ACT.Exp).then_inc(rt_exp, 1)

            def finish(ck):
                act.wait_ge(down1_mm, M1 * (ck + 1))
                if ck:
                    act.wait_ge(y_mm, ck)
                nc.scalar.activation(OT1, PS[4 + ck % 2][:, :], ACT.Identity, bias=BO).then_inc(ot_in, 1)

            for ck in range(NCH):
                for m in range(M1):
                    n = M1 * ck + m
                    act.wait_ge(g1_mm, n + 1)
                    if n >= 2:
                        act.wait_ge(mult1, n - 1)
                    nc.scalar.activation(SG1[:, n % 2, :], PS[n % 2][:, :], ACT.Silu).then_inc(silu1, 1)
                    if ck and m == 3:
                        finish(ck - 1)
            finish(NCH - 1)

        @block.vector
        def _(dve):
            done = [0]

            def link(ins):
                done[0] += 1
                ins.then_inc(dve_chain, 1)
                dve.wait_ge(dve_chain, done[0])

            def norm(layer):
                for t in range(T):
                    ins = nc.vector.bn_stats(out=STAT[:, t, :], in_=X[:, t, :])
                link(ins)
                for t in range(T):
                    ins = nc.vector.bn_aggr(out=MV[:, t, :], in_=STAT[:, t, :])
                link(ins)
                nc.vector.tensor_scalar(out=RSTD, in0=MV[:, :, 1], scalar1=EPS, scalar2=None, op0=ALU.add)\
                  .then_inc(ln_var, 1)
                dve.wait_ge(ln_std, layer + 1)
                link(nc.vector.reciprocal(RSTD, RSTD))
                for t in range(T):
                    ins = nc.vector.tensor_scalar(out=XN[:, t, :], in0=X[:, t, :], scalar1=MV[:, t, 0:1],
                                                  scalar2=RSTD[:, t:t + 1], op0=ALU.subtract, op1=ALU.mult)
                ins.then_inc(ln_xn, 1)

            def norm_copies(layer, dst):
                for j in range(0, NCH, 2):
                    dve.wait_ge(lnt_done, NCH * layer + j + 1)
                    nc.vector.tensor_copy(dst[:, CH * j:CH * (j + 1)], PS[j % 4][:, :]).then_inc(lnt_dve, 1)

            def rank(values, ge, gt):
                vj = values.unsqueeze(2).broadcast_to((P, T, 8, 8))
                ve = values.unsqueeze(3).broadcast_to((P, T, 8, 8))
                link(nc.vector.tensor_tensor(out=ge, in0=vj, in1=ve, op=ALU.is_ge))
                link(nc.vector.tensor_tensor(out=ge, in0=ge, in1=BEFORE.unsqueeze(1).broadcast_to((P, T, 8, 8)),
                                             op=ALU.mult))
                link(nc.vector.tensor_tensor(out=gt, in0=vj, in1=ve, op=ALU.is_gt))
                link(nc.vector.tensor_tensor(out=ge, in0=ge, in1=gt, op=ALU.max))
                link(nc.vector.tensor_reduce(out=RNK, in_=ge, axis=AX.X, op=ALU.add))

            def per_tile(v):
                return v.unsqueeze(2).broadcast_to((P, T, 8))

            def normalise(src, tiny):
                link(nc.vector.tensor_reduce(out=RED, in_=src, axis=AX.X, op=ALU.add))
                if tiny:
                    link(nc.vector.tensor_scalar(out=RED, in0=RED, scalar1=tiny, scalar2=None, op0=ALU.add))
                link(nc.vector.reciprocal(RED2, RED))
                return nc.vector.tensor_tensor(out=WGT3, in0=src, in1=per_tile(RED2), op=ALU.mult)

            def weights_out(layer):
                for n in range(2):
                    dve.wait_ge(rt_tr, 2 * layer + n + 1)
                    nc.vector.tensor_copy(WTT[:, n, :], PS[6 + n][:, 0:P]).then_inc(rt_out, 1)

            nc.vector.memset(XNT[:, 0:1], 0.0)
            nc.vector.memset(XNT[:, TOK + 1:TOK + 2], 0.0)
            dve.wait_ge(ld_x, 64)
            norm(0)
            norm_copies(0, XNT[:, 1:1 + TOK])
            dve.wait_ge(res_w, 1)
            dve.wait_ge(lnt_act, 4)
            dve.wait_ge(lnt_dve, 4)
            nc.vector.tensor_copy(SHIFT[:, 0, 1:P], XNT[:, 1 + L:L + P])
            nc.vector.tensor_copy(SHIFT[:, 1, 0:P - 1], XNT[:, L - P + 2:L + 1]).then_inc(edge_set, 1)
            LOG, SCO, COR, RNK, WGT, WGT3, WTT, RED, RED2 = ROUTER[0]
            dve.wait_ge(rt_logit, 1)
            link(nc.vector.tensor_copy(LOG, bank(4, T, 8)))
            link(nc.vector.tensor_reduce(out=RED, in_=LOG, axis=AX.X, op=ALU.max))
            nc.vector.tensor_tensor(out=SCO, in0=LOG, in1=per_tile(RED), op=ALU.subtract).then_inc(rt_sub, 1)
            dve.wait_ge(rt_exp, 1)
            link(normalise(SCO, None))
            link(nc.vector.tensor_copy(SCO, WGT3))
            link(nc.vector.tensor_scalar(out=COR, in0=SCO, scalar1=ROUTB, scalar2=None, op0=ALU.add))
            rank(COR, *CMP[0])
            link(nc.vector.tensor_scalar(out=RNK, in0=RNK, scalar1=4.0, scalar2=None, op0=ALU.is_lt))
            link(nc.vector.tensor_tensor(out=COR, in0=RNK, in1=SCO, op=ALU.mult))
            normalise(COR, 1e-20).then_inc(rt_w, 1)
            for t in range(T):
                if t == 0:
                    weights_out(0)
                dve.wait_ge(res_mm, t + 1)
                kind = 1 if t % NI == 0 else 2 if t % NI == NI - 1 else 0
                nc.vector.tensor_tensor(out=G[:, t, :, :], in0=bank(t % 4, 2, D),
                                        in1=RBIAS[:, kind, 0:2 * D].rearrange("p (g c) -> p g c", g=2), op=ALU.add)
                nc.vector.tensor_tensor(out=VG[:, 16 * (t // NI):16 * (t // NI) + 16, t % NI, :],
                                        in0=bank(t % 4, 16, 8, at=2 * D),
                                        in1=RBIAS[:, kind, 2 * D:OD].rearrange("p (g c) -> p g c", c=8),
                                        op=ALU.add).then_inc(res_out, 1)
            dve.wait_ge(bout_in, 1)
            for ck in range(NCH):
                for m in range(N0):
                    n = N0 * ck + m
                    dve.wait_ge(silu_done, n + 1)
                    dve.wait_ge(u_mm, n + 1)
                    if n >= 3:
                        dve.wait_ge(down_mm, n - 2)
                    nc.vector.tensor_tensor(out=AM0[:, n % 3, :], in0=PS[2 + n % 2][:, :], in1=SG0[:, n % 2, :],
                                            op=ALU.mult).then_inc(mult_done, 1)
                    if ck and m == 2:
                        add_down(dve, ck - 1)
            add_down(dve, NCH - 1)

            dve.wait_ge(res_out, T)
            nc.vector.memset(arena[FH:FH + 1, rH + L:rH + 2 * L], 1.0).then_inc(ones_row, 1)
            for n in range(4):
                dve.wait_ge(z_mm, n + 1)
                ins = nc.vector.tensor_scalar(out=ZF[:, CH * n:CH * (n + 1)], in0=PS[n][0:FH, :], scalar1=B1,
                                              scalar2=10.0, op0=ALU.add, op1=ALU.mult)
            link(ins)
            link(nc.vector.tensor_scalar(out=ZN, in0=ZF, scalar1=1 / (2 * math.pi), scalar2=MAGIC, op0=ALU.mult,
                                         op1=ALU.add))
            link(nc.vector.tensor_scalar(out=ZN, in0=ZN, scalar1=-MAGIC, scalar2=None, op0=ALU.add))
            link(nc.vector.scalar_tensor_tensor(out=ZF, in0=ZN, scalar=-PI2_HI, in1=ZF, op0=ALU.mult, op1=ALU.add))
            link(nc.vector.scalar_tensor_tensor(out=ZF, in0=ZN, scalar=-PI2_LO, in1=ZF, op0=ALU.mult, op1=ALU.add))
            nc.vector.tensor_scalar(out=ZF, in0=ZF, scalar1=PI_IN, scalar2=-PI_IN, op0=ALU.min, op1=ALU.max)\
              .then_inc(z_wrapped, 1)
            dve.wait_ge(dec_exp, 1 + NI)
            for j in range(NI // 2):
                dve.wait_ge(h_mm, j + 1)
                nc.vector.tensor_tensor(out=h_blocks(j), in0=bank(4 + j % 4, 2, 2 * D // 8, 8),
                                        in1=DEC[:, 2 * j:2 * j + 2, :].rearrange("p i (g c) -> p i g c", c=8),
                                        op=ALU.mult).then_inc(h_dec, 1)

            def block_copies(t):
                for j in range(8):
                    K = 16 * t + 2 * j
                    dve.wait_ge(f1_mm, K + 1)
                    nc.vector.tensor_copy(a_slot(2 * j), a_bank(K)).then_inc(a_in[0], 1)

            block_copies(0)
            for k in range(0, NK, 2):
                dve.wait_ge(f2_mm, k + 1)
                nc.vector.tensor_copy(H[:, k], bank(k % 3, 2, 2 * D)).then_inc(spec_dve, 1)
            for c in range(2):
                block_copies(c + 1)
                if c == 0:
                    dve.wait_ge(spec_act, NK // 2)
                    dve.wait_ge(spec_dve, NK - NK // 2)
                for k in range(NK):
                    q = NK * c + k
                    dve.wait_ge(f2_mm, NK + q + 1)
                    if q >= 2:
                        dve.wait_ge(y_in, q - 1)
                    xs = bank(q % 3, 2, B, D)
                    for part, dst in ((0, T1), (1, T2)):
                        h = H[:, k, part, D * c:D * (c + 1)].unsqueeze(1).unsqueeze(1).broadcast_to((P, 2, B, D))
                        ins = nc.vector.tensor_tensor(out=dst[:, q % 2].rearrange("p r (b c) -> p r b c", b=B),
                                                      in0=xs, in1=h, op=ALU.mult)
                    ins.then_inc(prod_in, 1)
                for r in range(8):
                    R = 8 * c + r
                    dve.wait_ge(i3_mm, 2 * (R + 1))
                    b, c0 = r // 4, 32 * (r % 4)
                    gate = G[:, NI * b:NI * (b + 1), c, c0:c0 + 32].rearrange("p i (g s) -> p g i s", s=4)
                    if c:
                        dst = V[:, NI * b:NI * (b + 1), c0:c0 + 32].rearrange("p i (g s) -> p g i s", s=4)
                        nc.vector.tensor_tensor(out=dst, in0=bank(R % 2, 8, NI, 4), in1=gate, op=ALU.mult)\
                          .then_inc(gated, 1)
                        continue
                    for h in range(2):
                        dst = VG[:, 16 * b + 4 * (r % 4):16 * b + 4 * (r % 4) + 4, :, 4 * h:4 * h + 4]
                        ins = nc.vector.tensor_tensor(out=dst, in0=bank(R % 2, 8, NI, 4)[:, h:8:2],
                                                      in1=gate[:, h:8:2], op=ALU.mult)
                    ins.then_inc(gated, 1)
            for j in range(NCH):
                dve.wait_ge(o_mm, j + 1)
                xs = X[:, TPC * j:TPC * (j + 1), :]
                ins = nc.vector.tensor_tensor(out=xs, in0=bank(2 + j % 2, TPC, D), in1=xs, op=ALU.add)
                ins.then_inc(o_added, 1)
            dve.wait_ge(o_added, NCH)
            norm(1)
            norm_copies(1, XNT1)
            dve.wait_ge(ld_w1, 15 * 16)
            dve.wait_ge(one_set, 1)
            for j in range(T // 2 + 2):
                if j < T // 2:
                    dve.wait_ge(kv_mm, j + 1)
                    if j >= 3:
                        dve.wait_ge(kvs_mm, 2 * (j - 2))
                    nc.vector.tensor_tensor(out=KVS[:, j % 3, :, 0:2 * P], in0=bank(j % 4, 2, 2 * P),
                                            in1=BKV.unsqueeze(1).broadcast_to((P, 2, 2 * P)), op=ALU.add)\
                      .then_inc(kv_bias, 1)
                if j >= 2:
                    i = j - 2
                    dve.wait_ge(k_exp, i + 1)
                    k = KVS[:, i % 3, :, 0:P]
                    nc.vector.scalar_tensor_tensor(out=k, in0=k, scalar=0.0, in1=KEX[:, i % 3], op0=ALU.max,
                                                   op1=ALU.add).then_inc(k_fm, 1)
            for b in range(B):
                dve.wait_ge(kvs_mm, NI * (b + 1))
                nc.vector.tensor_tensor(out=KVB[:, b, :], in0=PS[4 + b][:, 0:P], in1=HEADS, op=ALU.mult)
                link(nc.vector.tensor_copy(KSC[:, b, :], PS[4 + b][:, P:P + 1]))
                nc.vector.tensor_scalar(out=KSB[:, b, :], in0=HEADS, scalar1=KSC[:, b, :], scalar2=None,
                                        op0=ALU.mult).then_inc(kv_mask, 1)
            dve.wait_ge(kvs_mm, T)
            LOG, SCO, COR, RNK, WGT, WGT3, WTT, RED, RED2 = ROUTER[1]
            for n in range(NCH * PAIRS):
                ck, m = divmod(n, PAIRS)
                dve.wait_ge(gh_in, n + 1)
                if n >= 2:
                    dve.wait_ge(sc_mm, n - 1)
                g = GH[:, m, CH * ck:CH * (ck + 1)]
                nc.vector.tensor_tensor(out=SQ1[:, n % 2, :], in0=g, in1=g, op=ALU.mult).then_inc(sq_in, 1)
            dve.wait_ge(sc_mm, NCH * PAIRS)
            link(nc.vector.tensor_copy(LOG, bank(7, T, 8)))
            for ck in range(NCH):
                dve.wait_ge(q_mm, ck + 1)
                if ck >= 2:
                    dve.wait_ge(q_exp, ck - 1)
                nc.vector.tensor_scalar(out=QMN[:, ck % 2, :], in0=PS[ck % 2][:, :], scalar1=BQ, scalar2=0.0,
                                        op0=ALU.add, op1=ALU.min).then_inc(q_min, 1)
                dve.wait_ge(q_exp, ck + 1)
                if ck:
                    dve.wait_ge(nd_mm, ck)
                q = QPS[:, ck % 2, :]
                nc.vector.tensor_tensor(out=q, in0=q, in1=QEX[:, ck % 2, :], op=ALU.add).then_inc(q_fm, 1)
                dve.wait_ge(nd_mm, ck + 1)
                link(nc.vector.tensor_scalar(out=DEN, in0=PS[4 + ck % 2][:, :], scalar1=1e-6, scalar2=None,
                                             op0=ALU.add))
                link(nc.vector.reciprocal(DEN, DEN))
                nc.vector.tensor_tensor(out=ATT[:, CH * ck:CH * (ck + 1)], in0=PS[2 + ck % 2][:, :], in1=DEN,
                                        op=ALU.mult).then_inc(att_in, 1)
            rank(LOG, *CMP[1])
            nc.vector.tensor_scalar(out=RNK, in0=RNK, scalar1=2.0, scalar2=None, op0=ALU.is_lt).then_inc(rt_sub, 1)
            dve.wait_ge(rt_exp, 2)
            link(nc.vector.tensor_reduce(out=RED, in_=SCO, axis=AX.X, op=ALU.max))
            nc.vector.tensor_tensor(out=SCO, in0=SCO, in1=per_tile(RED), op=ALU.subtract).then_inc(rt_sub, 1)
            dve.wait_ge(rt_exp, 3)
            link(nc.vector.tensor_tensor(out=COR, in0=RNK, in1=SCO, op=ALU.mult))
            normalise(COR, None).then_inc(rt_w, 1)
            weights_out(1)

            def finish(ck):
                dve.wait_ge(y_mm, ck + 1)
                if ck >= 2:
                    dve.wait_ge(st_out, 16 * (ck - 1))
                nc.vector.tensor_tensor(out=ST1[:, ck % 2], in0=bank(6 + ck % 2, TPC, D),
                                        in1=X[:, TPC * ck:TPC * (ck + 1), :], op=ALU.add).then_inc(y_sum, 1)

            for ck in range(NCH):
                for m in range(M1):
                    n = M1 * ck + m
                    dve.wait_ge(silu1, n + 1)
                    dve.wait_ge(u1_mm, n + 1)
                    if n >= 3:
                        dve.wait_ge(down1_mm, n - 2)
                    nc.vector.tensor_tensor(out=AM1[:, n % 3, :], in0=PS[2 + n % 2][:, :], in1=SG1[:, n % 2, :],
                                            op=ALU.mult).then_inc(mult1, 1)
                    if ck and m == 6:
                        finish(ck - 1)
            finish(NCH - 1)

        @block.tensor
        def _(pe):
            mm = nc.tensor.matmul

            def norm_transposes(layer):
                pe.wait_ge(ln_xn, layer + 1)
                for j in range(NCH):
                    if j >= 4:
                        pe.wait_ge(lnt_act if j % 2 else lnt_dve, 4 * layer + (j - 4) // 2 + 1)
                    for t in range(TPC):
                        ins = nc.tensor.transpose(PS[j % 4][:, P * t:P * (t + 1)], XN[:, TPC * j + t, :], IDENT)
                    ins.then_inc(lnt_done, 1)

            def weight_transposes(layer):
                pe.wait_ge(rt_w, layer + 1)
                for n in range(2):
                    nc.tensor.transpose(PS[6 + n][:, 0:P], ROUTER[layer][4][:, P * n:P * (n + 1)], IDENT).then_inc(rt_tr, 1)

            pe.wait_ge(ld_const, N_CONST)
            norm_transposes(0)
            pe.wait_ge(lnt_act, 4)
            pe.wait_ge(lnt_dve, 4)
            for t in range(T):
                ins = mm(bank(4, T, 8)[:, t, :], XNT[:, 1 + P * t:1 + P * (t + 1)], ROUTW, start=True, stop=True)
            ins.then_inc(rt_logit, 1)
            pe.wait_ge(res_w, 1)
            pe.wait_ge(edge_set, 1)
            for t in range(T):
                if t == 4:
                    weight_transposes(0)
                if t >= 4:
                    pe.wait_ge(res_out, t - 3)
                for d in range(3):
                    xt = XNT[:, P * t + d:P * (t + 1) + d]
                    if t == NI and d == 0:
                        xt = SHIFT[:, 0, :]
                    if t == NI - 1 and d == 2:
                        xt = SHIFT[:, 1, :]
                    ins = mm(PS[t % 4][:, 0:OD], xt, WRES[:, d, :], start=(d == 0), stop=(d == 2))
                ins.then_inc(res_mm, 1)
            pe.wait_ge(ld_w0, 48)
            pe.wait_ge(res_out, T)

            def down0_step(n):
                ck, m = divmod(n, N0)
                if m < M0:
                    pe.wait_ge(weighted, M0 * ck + m + 1)
                else:
                    pe.wait_ge(mult_done, n + 1)
                if m == 0 and ck >= 2:
                    pe.wait_ge(x_added, ck - 1)
                for t in range(TPC):
                    ins = mm(PS[4 + ck % 2][:, D * t:D * (t + 1)], AM0[:, n % 3, P * t:P * (t + 1)],
                             DW0[:, m, :], start=(m == 0 and t == 0), stop=(m == N0 - 1), skip_group_check=True)
                ins.then_inc(down_mm, 1)

            for n in range(NCH * N0 + 2):
                if n < NCH * N0:
                    ck, m = divmod(n, N0)
                    xc = XNT[:, 1 + CH * ck:1 + CH * (ck + 1)]
                    if n >= 2:
                        pe.wait_ge(silu_done, n - 1)
                    mm(PS[n % 2][:, :], GW0[:, m, :], xc, start=True, stop=True).then_inc(g_mm, 1)
                    if n >= 2:
                        pe.wait_ge(mult_done, n - 1)
                    mm(PS[2 + n % 2][:, :], UW0[:, m, :], xc, start=True, stop=True).then_inc(u_mm, 1)
                if n >= 2:
                    down0_step(n - 2)

            pe.wait_ge(ld_filt, 80)
            pe.wait_ge(ld_pe, 16)
            pe.wait_ge(silu_done, NCH * N0)
            pe.wait_ge(mult_done, NCH * N0)
            for n in range(4):
                mm(PS[n][0:FH, :], W1S, PET[:, CH * n:CH * (n + 1)], start=True, stop=True).then_inc(z_mm, 1)
            pe.wait_ge(x_added, NCH)
            pe.wait_ge(sin_done, 1)
            pe.wait_ge(ones_row, 1)
            for j in range(NI // 2):
                if j >= 4:
                    pe.wait_ge(h_dec, j - 3)
                for i in range(2):
                    t = 2 * j + i
                    ins = mm(PS[4 + j % 4][:, 2 * D * i:2 * D * (i + 1)], SINT[:, P * t:P * (t + 1)], W2S,
                             start=True, stop=True)
                ins.then_inc(h_mm, 1)

            def block_dft(t, src):
                def transposes(j):
                    J = 8 * t + j
                    if J >= 2:
                        pe.wait_ge(ft_in, J - 1)
                    for n in range(4):
                        g = 4 * j + n
                        ins = nc.tensor.transpose(PS[J % 2][:, P * n:P * (n + 1)], src[:, g], IDENT)
                    ins.then_inc(f0_mm, 1)

                def rows(j):
                    J = 8 * t + j
                    pe.wait_ge(ft_in, J + 1)
                    for h in range(2):
                        K = 2 * J + h
                        if K >= 4:
                            pe.wait_ge(a_in[K % 2], (K - 4) // 2 + 1)
                        for n in range(2):
                            m = 2 * h + n
                            ins = mm(PS[2 + K % 4][:, 256 * n:256 * (n + 1)], FT[:, J % 2, P * m:P * (m + 1)],
                                     DFTB, start=True, stop=True)
                        ins.then_inc(f1_mm, 1)

                transposes(0)
                for j in range(8):
                    if j < 7:
                        transposes(j + 1)
                    rows(j)
                pe.wait_ge(a_in[0], 8 * (t + 1))
                pe.wait_ge(a_in[1], 8 * (t + 1))

            def inner_dft(k, n):
                o = bank(n, 2, 2 * D)
                s, rows = z_slots(k)
                if rows == 1:
                    mm(o[:, 0, :], MF[:, k, 0, :], a_rows(s, 1), start=True, stop=True)
                    return mm(o[:, 1, :], MF[:, k, 1, :], a_rows(s, 1), start=True, stop=True)
                mm(PS[n][:, :], MF[:, k, 0, :], a_rows(s, 2), start=True, stop=False, skip_group_check=True)
                mm(o[:, 1, :], MF[:, k, 1, :], a_rows(s, 1), start=False, stop=False, skip_group_check=True)
                return mm(o[:, 0, :], MF[:, k, 2, :], a_rows(s + 1, 1), start=False, stop=True, skip_group_check=True)

            def inner_idft(k, n, ys):
                o = bank(n, 2, 2 * D)
                if z_slots(k)[1] == 1:
                    mm(o[:, 0, :], MI[:, k, 0, :], ys[:, 0, :], start=True, stop=False)
                    return mm(o[:, 0, :], MI[:, k, 1, :], ys[:, 1, :], start=False, stop=True)
                mm(PS[n][:, :], MI[:, k, 0, :], ys, start=True, stop=False, skip_group_check=True)
                mm(o[:, 0, :], MI[:, k, 1, :], ys[:, 1, :], start=False, stop=False, skip_group_check=True)
                return mm(o[:, 1, :], MI[:, k, 2, :], ys[:, 0, :], start=False, stop=True, skip_group_check=True)

            pe.wait_ge(h_ready, NI // 2)
            pe.wait_ge(h_dec, NI // 2)
            block_dft(0, HT)
            pe.wait_ge(ld_dft, 16)
            for k in range(NK):
                if k >= 3:
                    pe.wait_ge(spec_act if (k - 3) % 2 else spec_dve, (k - 3) // 2 + 1)
                inner_dft(k, k % 3).then_inc(f2_mm, 1)
            pe.wait_ge(spec_act, NK // 2)
            pe.wait_ge(spec_dve, NK - NK // 2)
            pe.wait_ge(ld_idft, 16)
            for c in range(2):
                block_dft(c + 1, VG)
                for k in range(NK + 2):
                    if k < NK:
                        q = NK * c + k
                        if q >= 3:
                            pe.wait_ge(prod_in, q - 2)
                        inner_dft(k, q % 3).then_inc(f2_mm, 1)
                    if k >= 2:
                        q = NK * c + k - 2
                        pe.wait_ge(y_in, q + 1)
                        if q >= 3:
                            pe.wait_ge(z_in, q - 2)
                        inner_idft(k - 2, 3 + q % 3, YS[:, q % 2]).then_inc(i1_mm, 1)
                pe.wait_ge(z_in, NK * (c + 1))
                for p in range(17):
                    if p < 16:
                        q = 16 * c + p
                        if q >= 2:
                            pe.wait_ge(zt_in, q - 1)
                        for n in range(4):
                            ins = nc.tensor.transpose(PS[6 + q % 2][:, P * n:P * (n + 1)],
                                                      A[:, 4 * p + n], IDENT)
                        ins.then_inc(i2_mm, 1)
                    if p:
                        q = 16 * c + p - 1
                        pe.wait_ge(zt_in, q + 1)
                        R = q // 2
                        if q % 2 == 0 and R >= 2:
                            pe.wait_ge(gated, R - 1)
                        for n in range(4):
                            ins = mm(PS[R % 2][:, 256 * (q % 2) + 64 * n:256 * (q % 2) + 64 * (n + 1)],
                                     ZT[:, q % 2, P * n:P * (n + 1)], IDFTB, start=True, stop=True)
                        ins.then_inc(i3_mm, 1)
                pe.wait_ge(gated, 8 * (c + 1))
            for j in range(NCH + 1):
                if j < NCH:
                    if j >= 2:
                        pe.wait_ge(vt_in, j - 1)
                    for t in range(TPC):
                        ins = nc.tensor.transpose(PS[j % 2][:, P * t:P * (t + 1)], V[:, TPC * j + t, :], IDENT)
                    ins.then_inc(vt_mm, 1)
                if j:
                    i = j - 1
                    pe.wait_ge(vt_in, i + 1)
                    if i >= 2:
                        pe.wait_ge(o_added, i - 1)
                    for t in range(TPC):
                        ins = mm(PS[2 + i % 2][:, D * t:D * (t + 1)], FT[:, i % 2, P * t:P * (t + 1)], WOUT,
                                 start=True, stop=True)
                    ins.then_inc(o_mm, 1)
            norm_transposes(1)
            pe.wait_ge(lnt_act, 8)
            pe.wait_ge(lnt_dve, 8)
            pe.wait_ge(ld_w1, 15 * 16)
            for j in range(T // 2 + 3):
                if j < T // 2:
                    if j >= 4:
                        pe.wait_ge(kv_bias, j - 3)
                    for i in range(2):
                        t = 2 * j + i
                        ins = mm(PS[j % 4][:, 256 * i:256 * (i + 1)], XNT1[:, P * t:P * (t + 1)], WKV,
                                 start=True, stop=True)
                    ins.then_inc(kv_mm, 1)
                if j >= 3:
                    i = j - 3
                    pe.wait_ge(k_fm, i + 1)
                    for h in range(2):
                        t = 2 * i + h
                        mm(PS[4 + t // NI][:, 0:P + 1], KVS[:, i % 3, h, 0:P], KVS[:, i % 3, h, P:2 * P + 1],
                           start=(t % NI == 0), stop=(t % NI == NI - 1)).then_inc(kvs_mm, 1)
            pe.wait_ge(kv_bias, T // 2)
            for n in range(NCH * PAIRS + 2):
                if n < NCH * PAIRS:
                    ck, m = divmod(n, PAIRS)
                    if n >= 3:
                        pe.wait_ge(gh_in, n - 2)
                    mm(PS[n % 3][:, :], WA1[:, m, :], XNT1[:, CH * ck:CH * (ck + 1)], start=True, stop=True)\
                      .then_inc(gh_mm, 1)
                if n >= 2:
                    i = n - 2
                    ck, m = divmod(i, PAIRS)
                    pe.wait_ge(sq_in, i + 1)
                    for t in range(TPC):
                        ins = mm(bank(7, T, 8)[:, TPC * ck + t, :], SQ1[:, i % 2, P * t:P * (t + 1)], EXPOF[:, m, :],
                                 start=(i == 0 and t == 0), stop=(m == PAIRS - 1), skip_group_check=True)
                    ins.then_inc(sc_mm, 1)
            pe.wait_ge(gh_in, NCH * PAIRS)
            pe.wait_ge(kv_mask, B)
            for ck in range(NCH):
                b = ck // (NCH // B)
                if ck >= 2:
                    pe.wait_ge(q_fm, ck - 1)
                mm(PS[ck % 2][:, :], WQ, XNT1[:, CH * ck:CH * (ck + 1)], start=True, stop=True).then_inc(q_mm, 1)
                pe.wait_ge(q_fm, ck + 1)
                if ck >= 2:
                    pe.wait_ge(att_in, ck - 1)
                mm(PS[2 + ck % 2][:, :], KVB[:, b, :], QPS[:, ck % 2, :], start=True, stop=True)
                mm(PS[4 + ck % 2][:, :], KSB[:, b, :], QPS[:, ck % 2, :], start=True, stop=True).then_inc(nd_mm, 1)
            weight_transposes(1)
            pe.wait_ge(att_in, NCH)
            pe.wait_ge(rt_out, 4)

            def down1_step(n):
                ck, m = divmod(n, M1)
                if m == 0:
                    if ck >= 2:
                        pe.wait_ge(ot_in, ck - 1)
                    mm(PS[4 + ck % 2][:, :], WO, ATT[:, CH * ck:CH * (ck + 1)], start=True, stop=False)
                pe.wait_ge(weighted1, n + 1)
                ins = mm(PS[4 + ck % 2][:, :], DN1[:, m, :], AM1[:, n % 3, :], start=False, stop=(m == M1 - 1))
                ins.then_inc(down1_mm, 1)

            def back(ck):
                pe.wait_ge(ot_in, ck + 1)
                if ck >= 2:
                    pe.wait_ge(y_sum, ck - 1)
                for t in range(TPC):
                    ins = nc.tensor.transpose(PS[6 + ck % 2][:, P * t:P * (t + 1)], OT1[:, P * t:P * (t + 1)], IDENT)
                ins.then_inc(y_mm, 1)

            for n in range(NCH * M1 + 2):
                if n < NCH * M1:
                    ck, m = divmod(n, M1)
                    e = m // 2
                    if n >= 2:
                        pe.wait_ge(silu1, n - 1)
                    mm(PS[n % 2][:, :], WB1[:, m, :], GH[:, e // 2, CH * ck:CH * (ck + 1)], start=True, stop=True)\
                      .then_inc(g1_mm, 1)
                    if n >= 2:
                        pe.wait_ge(mult1, n - 1)
                    mm(PS[2 + n % 2][:, :], UP1[:, m, :], XNT1[:, CH * ck:CH * (ck + 1)], start=True, stop=True)\
                      .then_inc(u1_mm, 1)
                if n >= 2:
                    down1_step(n - 2)
                if n >= M1 and n % M1 == 5:
                    back(n // M1 - 1)
            back(NCH - 1)


_OUT = ((B, L, D), "float32")


def _constants():
    f32 = np.float32
    a, k2, i = np.arange(P), np.arange(P), np.arange(NI)
    mf = np.zeros((P, NK, 3, P))
    for k in range(NK):
        th = 2 * np.pi * (np.outer(a, k + K1 * k2) % (K1 * P)) / (K1 * P)
        mf[:, k, 0], mf[:, k, 1], mf[:, k, 2] = np.cos(th), -np.sin(th), np.sin(th)
    mi = mf.transpose(3, 1, 2, 0)
    slots = [(0, 0), (NK - 1, 0)] + [(k, r) for k in range(1, NK - 1) for r in range(2)]
    fw, iv = np.zeros((NI, 8, 2, K1, 4)), np.zeros((K1, 4, NI, 4))
    for s, (k, r) in enumerate(slots):
        th = 2 * np.pi * ((i * k) % K1) / K1
        row = -np.sin(th) if r else np.cos(th)
        weight = (1 if k in (0, NK - 1) else 2) / (K1 * P) / L
        for c in range(8):
            fw[:, c, c // 4, s, c % 4] = row
        for c in range(4):
            iv[s, c, :, c] = row * weight
    t = np.linspace(0.0, 1.0, L).astype(f32)
    bands = np.linspace(0.0, EMB - 1.0, EMB).astype(f32)
    pe = np.sin((t[:, None] * bands[None, :]).astype(f32) * f32(10.0)).astype(f32)
    ch = np.arange(D)
    expert_of = np.zeros((P, PAIRS, E1))
    for m in range(PAIRS):
        expert_of[:R1, m, 2 * m] = expert_of[R1:, m, 2 * m + 1] = 1
    edges = np.zeros((P, 2))
    edges[0, 0] = edges[P - 1, 1] = 1
    before = np.broadcast_to((np.arange(8)[None, :] < np.arange(8)[:, None]), (P, 8, 8))
    tables = {
        "dft_f": mf, "dft_i": mi, "dft_b": fw.reshape(P, K1 * 8), "idft_b": iv.reshape(P, NI * 4),
        "negt": -t.reshape(NI, P).T, "ident": np.eye(P), "before": before, "heads": (ch[:, None] // 8 == ch[None, :] // 8),
        "expert_of": expert_of, "edges": edges, "peT": pe.T,
    }
    return {k: np.ascontiguousarray(v, dtype=f32) for k, v in tables.items()}


def kernel(**inputs):
    import concourse.bacc as _bacc
    from concourse.bass_utils import run_bass_kernel_spmd as _run

    a = {k: np.asarray(v) for k, v in inputs.items()}
    g = lambda n: a["L0_attn_" + n]
    f = lambda n: a["L0_ffn_" + n]
    h = lambda n: a["L1_attn_" + n]
    w = lambda n: a["L1_ffn_" + n]
    c = _constants()

    def pairs(m):
        return m.transpose(1, 0, 2).reshape(D, M0, P)

    arrays = {
        "x": g("u"), "w_inT": g("w_in").T, "conv_w": g("conv_w").T, "conv_b": g("conv_b"), "b_in": g("b_in"),
        "peT": c["peT"], "w1T": g("w1").T, "b1": g("b1")[:, None], "w2b": np.concatenate([g("w2").T, g("b2")[None]]),
        "fdec": g("filt_decay").reshape(-1), "fbias": g("filt_bias").reshape(-1), "w_outT": g("w_out").T,
        "b_out": g("b_out"), "rout_w": f("router_w"), "rout_b": f("router_bias").reshape(1),
        "gate0": np.concatenate([pairs(f("gate_w")), f("s_gate_w").reshape(D, 2, P)], axis=1),
        "up0": np.concatenate([pairs(f("up_w")), f("s_up_w").reshape(D, 2, P)], axis=1),
        "down0": np.concatenate([f("down_w").reshape(M0, P, D), f("s_down_w").reshape(2, P, D)]).transpose(1, 0, 2),
        "wq": h("wq"), "wkv": np.concatenate([h("wk"), h("wv")], axis=1),
        "bkv": np.concatenate([h("bk"), h("bv")]), "bq": h("bq")[:, None], "wo": h("wo"), "bo": h("bo")[:, None],
        "w_a": w("W_A").transpose(2, 0, 1).reshape(D, PAIRS, P),
        "w_b": w("W_B").transpose(0, 2, 1).reshape(E1, R1, 2, P),
        "w_up": w("W_up").transpose(2, 0, 1).reshape(D, M1, P),
        "w_dn": w("W_down").transpose(0, 2, 1).reshape(M1, P, D).transpose(1, 0, 2),
    }
    for k in ("dft_f", "dft_i", "dft_b", "idft_b", "negt", "ident", "before", "heads", "expert_of", "edges"):
        arrays[k] = c[k]
    nc = _bacc.Bacc("TRN2", target_bir_lowering=False, num_devices=1)
    fed, args = {}, []
    for name, v in arrays.items():
        v = np.ascontiguousarray(v)
        fed[f"in_{name}"] = v
        args.append(nc.dram_tensor(f"in_{name}", v.shape, mybir.dt.from_np(v.dtype), kind="ExternalInput").ap())
    args.append(nc.dram_tensor("out_0", _OUT[0], F32, kind="ExternalOutput").ap())
    hyena_moe_program(nc, *args)
    r = _run(nc, [fed], core_ids=[0])
    return r.results[0]["out_0"]
```

```python
import math

import numpy as np

import concourse.bass as bass
from concourse import mybir
from contextlib import ExitStack

F32 = mybir.dt.float32
F32R = mybir.dt.float32r
ALU = mybir.AluOpType
ACT = mybir.ActivationFunctionType
AX = mybir.AxisListType

P = 128
B, L, D = 2, 2048, 128
NI = L // P
T = B * NI
TOK = B * L
CH = 512
NCH = TOK // CH
TPC = CH // P
OD = 3 * D
K1 = 2 * NI
NK = K1 // 2 + 1
EMB, FH = 33, 64
E0, I0, IS = 8, 64, 256
M0 = E0 * I0 // P
N0 = M0 + IS // P
E1, R1, F1W = 8, 64, 256
M1 = E1 * F1W // P
PAIRS = E1 // 2
EPS = 1e-5
XS_AT, GH_AT, RANK_AT, SUB_AT, EXP_AT, RW_AT, WT_AT = 0, 3, 8, 9, 11, 12, 14
Q_AT, QF_AT, ND_AT, WO_AT, OT_AT, BACK_AT, FIN_AT = 10, 12, 15, 2, 5, 7, 8
LAG = 3
XS0_AT, UP_AT, DN_AT, PREP_AT, COMP_AT = 4, 5, 9, 5, 5
W_PARTS = 4
STEPS = NCH + 5
ARENA_WORDS = 53000
ARENA_AT = 16640
Z_AT, SIN_AT = 12, 30
RT_STEPS = ((17, 19, 20, 21, 23, 24, 26, 28, 30), (0, 2, 3, 4, 5, 6, 7, 8, 10))
RT_EXP_AT, RT_BACK_AT = 1, (30, 9)
SPLIT0_AT = 1
MAGIC = 12582912.0
PI2_HI = 6.28125
PI2_LO = 2 * math.pi - PI2_HI
PI_IN = 3.1415925


def hyena_moe_program(nc, x, w_inT, conv_w, conv_b, b_in, peT, w1T, b1, w2b, fdec, fbias, w_outT, b_out,
                      rout_w, rout_b, gate0, up0, down0, wq, wkv, bkv, bq, wo, bo, w_a, w_at, w_b, w_up, w_dn,
                      dft_f, dft_i, dft_b, idft_b, negt, ident, before, heads, edges,
                      out):
    wexp = [nc.dram_tensor(f"expert_weights_{n}", (T, 8, P), F32, kind="Internal").ap() for n in range(2)]
    ctx = ExitStack()
    with ctx:
        words = [0]
        arena = nc.alloc_sbuf_tensor_at("arena", [P, ARENA_WORDS], F32, offset=ARENA_AT)

        def region(n):
            at = words[0]
            words[0] += -(-n // 8) * 8
            assert words[0] <= ARENA_WORDS, words[0]
            return at

        def view(at, *dims, parts=P):
            n = int(np.prod(dims))
            v = arena[0:parts, at:at + n]
            if len(dims) == 1:
                return v
            names = "abcd"[:len(dims)]
            return v.rearrange("p (%s) -> p %s" % (" ".join(names), " ".join(names)),
                               **{c: d for c, d in zip(names, dims)})

        def split_part(name, at, *dims):
            n = int(np.prod(dims))
            names = "abcd"[:len(dims)]
            t = nc.alloc_sbuf_tensor_at(name, [P, n], F32R, offset=ARENA_AT + 4 * at)
            return t[:, :].rearrange("p (%s) -> p %s" % (" ".join(names), " ".join(names)),
                                     **{c: d for c, d in zip(names, dims)})

        def split_view(name, at, *dims):
            return split_part(name + "_hi", at, *dims), split_part(name + "_lo", at + int(np.prod(dims)), *dims)

        IDENT = view(region(P), P)
        DFTB = view(region(K1 * 8), K1 * 8)
        IDFTB = view(region(NI * 4), NI * 4)
        NEGT = view(region(NI), NI)
        BEFORE = view(region(64), 8, 8)
        HEADS = view(region(P), P)
        EDGES = view(region(2), 2)
        ROUTB = view(region(1), 1)
        B1 = view(region(1), 1, parts=FH)
        BQ = view(region(1), 1)
        NBQ = view(region(1), 1)
        BO = view(region(1), 1)
        BOUT = view(region(D), D)
        MV = view(region(2 * T), T, 2)
        RSTD = view(region(T), T)
        STAT = view(region(6 * T), T, 6)
        HALF = view(region(16), 2, 8)
        SHIFT = view(region(2 * P), 2, P)

        rX = region(T * D)
        rG = region(T * 2 * D)
        rV = region(T * D)
        rH = region(NK * 2 * 2 * D)
        rA = region(K1 * 2 * D + 8)
        rY = region(4096)
        rF = region(NK * 3 * P)
        rI = region(NK * 3 * P)

        X = view(rX, T, D)
        G = view(rG, T, 2, D)
        V = view(rV, T, D)
        VG = view(rV, B * 16, NI, 8)
        H = view(rH, NK, 2, 2 * D)
        A = view(rA, 2 * D // 4, K1, 4)
        XNT = view(rA, TOK + 2)
        XN = view(rY, T, D)
        MF = view(rF, NK, 3, P)
        MI = view(rI, NK, 3, P)
        FT = view(rY, 2, CH)
        ZT = view(rY, 4, CH)
        T1 = view(rY + 1024, 2, 2, 2 * D)
        T2 = view(rY + 2048, 2, 2, 2 * D)
        YS = view(rY + 3072, 2, 2, 2 * D)
        WRES = view(rH + 4096, 3, OD + E0)
        rB = rH + 4096 + 3 * (OD + E0)
        RBIAS = view(rB, 3, OD)
        CWB = view(rB + 3 * OD, 3, OD)
        BINB = view(rB + 6 * OD, OD)
        CBB = view(rB + 7 * OD, OD)
        WIN = view(rH + 3712, OD)
        assert rB + 8 * OD <= rA
        PET = view(rH, L, parts=EMB)
        SINT = view(rH + L, L, parts=FH + 1)
        SIN64 = view(rH + L, L, parts=FH)
        DEC = view(rH + 2 * L, NI, 2 * D)
        ZF = SIN64
        ZN = view(rH + 2 * L, L, parts=FH)
        HT = view(rY, 2 * D // 8, NI, 8)
        r0 = rA + TOK + 6
        GW0 = view(r0, N0, P)
        UW0 = view(r0 + N0 * P, N0, P)
        DW0 = view(r0 + 2 * N0 * P, N0, P)
        WB0 = view(r0 + 3 * N0 * P, M0, CH)
        SG0 = view(r0 + 3 * N0 * P + M0 * CH, 2, CH)
        AM0 = view(r0 + 3 * N0 * P + (M0 + 2) * CH, 3, CH)
        assert r0 + 3 * N0 * P + (M0 + 5) * CH <= rF
        GWH0, GWL0 = split_view("gate_weights0", rI, N0, P)
        UWH0, UWL0 = split_view("up_weights0", rI + 2 * N0 * P, N0, P)
        XHI0, XLO0 = split_view("x0", rI + 4 * N0 * P, 2, CH)
        assert 4 * N0 * P + 4 * CH <= NK * 3 * P
        small = region(2 * 2 * D + FH + 2 * D + D)
        FDB = view(small, 2 * D)
        FBB = view(small + 2 * D, 2 * D)
        W1S = view(small + 4 * D, FH, parts=EMB)
        W2S = view(small + 4 * D + FH, 2 * D, parts=FH + 1)
        WOUT = view(small + 6 * D + FH, D)

        def router_scratch(at):
            return (view(at, T, 8), view(at + 256, T, 8), view(at + 512, T, 8), view(at + 768, T, 8),
                    view(at + 1024, T * 8), view(at + 1024, T, 8), view(at + 1280, 2, P), view(at + 1536, T),
                    view(at + 1536 + T, T))

        LOG, SCO, COR, RNK, WGT, WGT3, WTT, RED, RED2 = router_scratch(rF)
        CMP0 = (view(rF + 2048, NI, 8, 8), view(rF + 3072, NI, 8, 8))
        VT = view(rY + 3072, 2, CH)
        assert rY + 4096 == rF
        XNR = view(rY + 2048, 2, TPC, D)
        KVS = view(rH, 3, 2, 2 * P + 1)
        KEX = view(rH + 1544, 3, 2, P)
        KVB = view(rH + 2400, B, P)
        KSB = view(rH + 2656, B, P)
        KSC = view(rH + 2912, B, 1)
        XNT1 = view(rG, TOK)
        XHI, XLO = split_view("x", rG + TOK, 2, CH)
        ACC1 = view(rG + TOK + 4 * CH, 2, CH)
        TMP1 = view(rG + TOK + 6 * CH, 2, CH)
        GWH, GWL = split_view("gate_weights", rH + 3072, M1, P)
        assert rH + 3072 + 2 * M1 * P <= rA
        WBC1 = view(rA, E1, CH)
        SQ1 = view(rA + 4096, TPC, E1, R1)
        q0 = rA + 6144
        LOG1, SCO1, COR1, RNK1 = (view(q0 + 32 * n, TPC, 8) for n in range(4))
        WGT1, WGT13 = view(q0 + 128, TPC * 8), view(q0 + 128, TPC, 8)
        WTT1 = view(q0 + 160, P, parts=TPC * 8)
        RED11, RED12 = view(q0 + 288, TPC), view(q0 + 292, TPC)
        CMP1 = (view(q0 + 320, TPC, 8, 8), view(q0 + 576, TPC, 8, 8))
        QEX, QPS, DEN, ATT = (view(rV + CH * n, CH) for n in range(4))
        rW = rF
        WA1 = view(rW, PAIRS, P)
        WAT = view(rW + 512, PAIRS, P)
        WB1 = view(rW + 1024, M1, P)
        UP1 = view(rW + 3072, M1, P)
        DN1 = view(rW + 5120, M1, P)
        UPH, UPL = split_view("up_weights", rW + 7168, M1, P)
        w0 = rW + 7168 + 2 * M1 * P
        WQ = view(w0, P)
        WKV = view(w0 + P, 2 * P)
        WO = view(w0 + 3 * P, P)
        BKV = view(w0 + 4 * P, 2 * P)
        WAH, WAL = split_view("router_weights", w0 + 6 * P, PAIRS, P)
        assert w0 + 14 * P <= rI + NK * 3 * P
        DNH, DNL = split_view("down_weights", rW + 1024, M1, P)
        SG1 = view(rY, 2, CH)
        AM1 = view(rY + 1024, 2, CH)
        AML = split_part("activations_lo", rY + 2048, 4, CH)
        AMH = split_part("activations_hi", rH, 4, CH)
        OT1 = view(rV + 4 * CH, CH)
        ST1 = view(q0 + 832, 2, TPC, D)
        assert q0 + 832 + 2 * CH <= rY

        PS = [ctx.enter_context(nc.psum_tensor(f"bank{n}", [P, CH], F32)) for n in range(8)]

        def bank(n, *dims, at=0):
            n_words = int(np.prod(dims))
            v = PS[n][:, at:at + n_words]
            names = "abcd"[:len(dims)]
            return v if len(dims) == 1 else v.rearrange(
                "p (%s) -> p %s" % (" ".join(names), " ".join(names)), **{c: d for c, d in zip(names, dims)})

        def sem(name):
            return ctx.enter_context(nc.semaphore(name))

        ld_const = sem("ld_const")
        ld_ident = sem("ld_ident")
        wo_mm = sem("wo_mm")
        ld_x = [sem(f"ld_x{n}") for n in range(4)]
        ld_res = sem("ld_res")
        ld_w0 = sem("ld_w0")
        ld_filt = sem("ld_filt")
        ld_pe = sem("ld_pe")
        ld_dft = sem("ld_dft")
        ld_idft = sem("ld_idft")
        ld_w1 = sem("ld_w1")
        ld_wexp0 = [sem(f"ld_wexp0_{m}") for m in range(M0)]
        ld_wexp1 = [sem(f"ld_wexp1_{e}") for e in range(E1)]
        st_wexp = sem("st_wexp")
        st_out = [sem("st_out_even"), sem("st_out_odd")]
        half_set = sem("half_set")
        ln_var = sem("ln_var")
        ln_rstd = sem("ln_rstd")
        ln_xn = [sem("ln_xn_dve"), sem("ln_xn_pool")]
        gw0_hi = sem("gw0_hi")
        gw0_lo = sem("gw0_lo")
        x0_hi = sem("x0_hi")
        x0_lo = sem("x0_lo")
        lnt_done = sem("lnt_done")
        lnt_dve = sem("lnt_dve")
        lnt_act = sem("lnt_act")
        rt_sub = sem("rt_sub")
        rt_exp = sem("rt_exp")
        rt_w = sem("rt_w")
        rt_tr = sem("rt_tr")
        rt_out = sem("rt_out")
        dve_chain = sem("dve_chain")
        pool_chain = sem("pool_chain")
        edge_set = sem("edge_set")
        res_mm = sem("res_mm")
        res_out = sem("res_out")
        bout_in = sem("bout_in")
        g_mm = sem("g_mm")
        u_mm = sem("u_mm")
        silu_done = sem("silu_done")
        mult_done = sem("mult_done")
        weighted = sem("weighted")
        down_mm = sem("down_mm")
        x_added = sem("x_added")
        z_mm = sem("z_mm")
        z_out = sem("z_out")
        z_wrapped = sem("z_wrapped")
        sin_done = sem("sin_done")
        ones_row = sem("ones_row")
        dec_exp = sem("dec_exp")
        h_mm = sem("h_mm")
        h_dec = sem("h_dec")
        h_ready = sem("h_ready")
        shift_zero = sem("shift_zero")
        spec_act = sem("spec_act")
        spec_dve = sem("spec_dve")
        f0_mm = sem("f0_mm")
        ft_in = sem("ft_in")
        f1_mm = sem("f1_mm")
        a_in = [sem("a_in_dve"), sem("a_in_act")]
        f2_mm = sem("f2_mm")
        prod_in = sem("prod_in")
        y_in = sem("y_in")
        i1_mm = sem("i1_mm")
        z_in = sem("z_in")
        i2_mm = sem("i2_mm")
        zt_in = sem("zt_in")
        i3_mm = sem("i3_mm")
        gated = sem("gated")
        vt_mm = sem("vt_mm")
        vt_in = sem("vt_in")
        o_mm = sem("o_mm")
        o_added = sem("o_added")
        ln1_var = sem("ln1_var")
        ln1_rstd = sem("ln1_rstd")
        ln1_xn = sem("ln1_xn")
        xnt1_mm = sem("xnt1_mm")
        xnt1_in = sem("xnt1_in")
        log1_in = sem("log1_in")
        sqrt1 = sem("sqrt1")
        sub1 = sem("sub1")
        exp1 = sem("exp1")
        w1_in = sem("w1_in")
        wt1_mm = sem("wt1_mm")
        wt1_in = sem("wt1_in")
        st_wexp1 = sem("st_wexp1")
        wb_zero = sem("wb_zero")
        one_set = sem("one_set")
        kv_mm = sem("kv_mm")
        kv_bias = sem("kv_bias")
        q_neg = sem("q_neg")
        k_exp = sem("k_exp")
        k_fm = sem("k_fm")
        k_neg = sem("k_neg")
        kvs_mm = sem("kvs_mm")
        kv_mask = sem("kv_mask")
        gh_mm = sem("gh_mm")
        sq_in = sem("sq_in")
        comp_mm = sem("comp_mm")
        gw_hi = sem("gw_hi")
        gw_lo = sem("gw_lo")
        up_hi = sem("up_hi")
        up_lo = sem("up_lo")
        dn_hi = sem("dn_hi")
        dn_lo = sem("dn_lo")
        wa_hi = sem("wa_hi")
        wa_lo = sem("wa_lo")
        summed = sem("summed")
        scaled = sem("scaled")
        am_in = sem("am_in")
        am_lo = sem("am_lo")
        x_hi = sem("x_hi")
        x_lo = sem("x_lo")
        q_mm = sem("q_mm")
        q_exp = sem("q_exp")
        q_fm = sem("q_fm")
        nd_mm = sem("nd_mm")
        att_in = sem("att_in")
        g1_mm = sem("g1_mm")
        u1_mm = sem("u1_mm")
        silu1 = sem("silu1")
        mult1 = sem("mult1")
        down1_mm = sem("down1_mm")
        ot_in = sem("ot_in")
        y_mm = sem("y_mm")
        y_sum = sem("y_sum")

        N_CONST = 12 * 16
        N_W1 = 16 * 16
        block = ctx.enter_context(nc.Block())

        F1_BANKS = (4, 5, 0, 1)

        def a_bank(K):
            return PS[F1_BANKS[K % 4]][:, :]

        def a_slot(n):
            return arena[:, rA + CH * n:rA + CH * (n + 1)]

        def a_rows(s, n):
            return A[:, :, s:s + n, :].rearrange("p g s c -> p s g c")

        def h_blocks(j):
            return HT[:, :, 2 * j:2 * j + 2, :].rearrange("p g i c -> p i g c")

        def z_slots(k):
            return (0, 1) if k == 0 else (1, 1) if k == NK - 1 else (2 * k, 2)

        def add_down(dve, ck):
            dve.wait_ge(down_mm, N0 * (ck + 1))
            xs = X[:, TPC * ck:TPC * (ck + 1), :]
            nc.vector.tensor_tensor(out=xs, in0=bank(4 + ck % 2, TPC, D), in1=xs, op=ALU.add).then_inc(x_added, 1)

        outv = out.rearrange("b (i a) c -> a (b i) c", a=P)

        def store(sp, ck):
            sp.wait_ge(y_sum, ck + 1)
            sp.dma_start(outv[:, TPC * ck:TPC * (ck + 1), :], ST1[:, ck % 2]).then_inc(st_out[ck % 2], 16)

        def gate_bank(ck, t):
            return 6 if ck else 3 + t % 2

        def router_bank(ck):
            return 7 if ck else 3

        def gate_square(act, ck, t):
            act.wait_ge(gh_mm, TPC * ck + t + 1)
            if ck and t == 0:
                act.wait_ge(log1_in, TPC * ck)
            nc.scalar.activation(SQ1[:, t, :, :], bank(gate_bank(ck, t), E1, R1), ACT.Square).then_inc(sq_in, 1)

        def split_hi(act, ck):
            if ck >= 2:
                act.wait_ge(u1_mm, M1 * (ck - 1))
            else:
                act.wait_ge(xnt1_in, ck + 1)
            nc.scalar.activation(XHI[:, ck % 2, :], XNT1[:, CH * ck:CH * (ck + 1)], ACT.Copy).then_inc(x_hi, 1)

        def split_lo(pool, ck):
            pool.wait_ge(x_hi, ck + 1)
            nc.gpsimd.tensor_tensor(out=XLO[:, ck % 2, :], in0=XNT1[:, CH * ck:CH * (ck + 1)],
                                    in1=XHI[:, ck % 2, :].bitcast(F32), op=ALU.subtract).then_inc(x_lo, 1)

        def router_root(pool, ck, t):
            pool.wait_ge(log1_in, TPC * ck + t + 1)
            nc.gpsimd.tensor_tensor(out=SCO1[:, t, :], in0=LOG1[:, t, :], in1=HALF[:, 1, :], op=ALU.pow)\
              .then_inc(sqrt1, 1)

        def router_exp(act, ck):
            act.wait_ge(sub1, ck + 1)
            nc.scalar.activation(SCO1, SCO1, ACT.Exp).then_inc(exp1, 1)

        @block.sync
        def _(sp):
            xv = x.rearrange("b (i a) c -> a (b i) c", a=P)
            sp.dma_start(IDENT, ident).then_inc(ld_ident, 16)
            for n in range(4):
                sp.dma_start(X[:, 8 * n:8 * n + 8, :], xv[:, 8 * n:8 * n + 8, :]).then_inc(ld_x[n], 16)
            for dst, src in ((WRES[:, 1, OD:OD + E0], rout_w), (ROUTB, rout_b.partition_broadcast(P)),
                             (BEFORE, before), (EDGES, edges), (BOUT, b_out.partition_broadcast(P)), (DFTB, dft_b),
                             (IDFTB, idft_b), (NEGT, negt), (HEADS, heads), (B1, b1), (BQ, bq),
                             (BO, bo)):
                sp.dma_start(dst, src).then_inc(ld_const, 16)
            for dst, src in ((W1S, w1T), (W2S, w2b), (FDB, fdec.partition_broadcast(P)),
                             (FBB, fbias.partition_broadcast(P)), (WOUT, w_outT)):
                sp.dma_start(dst, src).then_inc(ld_filt, 16)
            sp.dma_start(PET, peT).then_inc(ld_pe, 16)
            sp.wait_ge(lnt_done, NCH)
            for dst, src in ((GW0, gate0), (UW0, up0), (DW0, down0)):
                sp.dma_start(dst, src).then_inc(ld_w0, 16)
            def expert_weights(n):
                sp.wait_ge(rt_out, n + 1)
                sp.dma_start(wexp[0].rearrange("(n t) e a -> (t e) n a", n=2)[:, n, :], WTT[:, n, :])\
                  .then_inc(st_wexp, 16)
                sp.wait_ge(st_wexp, 16 * (n + 1))

            expert_weights(0)
            for ck in range(NCH):
                for m in range(M0):
                    if ck:
                        sp.wait_ge(weighted, M0 * (ck - 1) + m + 1)
                    for e2 in range(2):
                        src = wexp[0][TPC * ck:TPC * (ck + 1), 2 * m + e2, :]
                        sp.dma_start(WB0[64 * e2:64 * e2 + 64, m, :].rearrange("p (t a) -> p t a", a=P),
                                     src.partition_broadcast(64)).then_inc(ld_wexp0[m], 16)
                if ck == 1:
                    expert_weights(1)
                    sp.dma_start(MF, dft_f).then_inc(ld_dft, 16)
            sp.wait_ge(u_mm, NCH * N0)
            sp.dma_start(MI, dft_i).then_inc(ld_idft, 16)
            sp.wait_ge(i1_mm, 2 * NK)
            sp.wait_ge(wb_zero, 1)
            for e in range(E1):
                h0 = 64 * (e % 2)
                sp.dma_start(WB1[h0:h0 + 64, 2 * e:2 * e + 2, :], w_b[e]).then_inc(ld_w1, 16)
            for dst, src in ((WA1, w_a), (WAT, w_at), (UP1, w_up), (DN1, w_dn), (WQ, wq), (WKV, wkv), (WO, wo),
                             (BKV, bkv.partition_broadcast(P))):
                sp.dma_start(dst, src).then_inc(ld_w1, 16)
            for ck in range(NCH):
                sp.wait_ge(wt1_in, ck + 1)
                sp.dma_start(wexp[1][TPC * ck:TPC * (ck + 1)].rearrange("t e a -> (t e) a"), WTT1)\
                  .then_inc(st_wexp1, 16)
                sp.wait_ge(st_wexp1, 16 * (ck + 1))
                for e in range(E1):
                    if ck:
                        sp.wait_ge(scaled, E1 * (ck - 1) + e + 1)
                    sp.dma_start(WBC1[:, e, :].rearrange("p (t a) -> p t a", a=P),
                                 wexp[1][TPC * ck:TPC * (ck + 1), e, :].partition_broadcast(P))\
                      .then_inc(ld_wexp1[e], 16)
                if ck >= 2:
                    store(sp, ck - 2)
            store(sp, NCH - 2)
            store(sp, NCH - 1)
            sp.wait_ge(st_out[0], 16 * NCH // 2)
            sp.wait_ge(st_out[1], 16 * NCH // 2)

        @block.gpsimd
        def _(pool):
            done = [0]

            def link(ins):
                done[0] += 1
                ins.then_inc(pool_chain, 1)
                pool.wait_ge(pool_chain, done[0])

            for dst, src in ((WIN, w_inT), (CWB, conv_w.rearrange("k o -> (k o)").partition_broadcast(P)
                                            .rearrange("p (k o) -> p k o", k=3)),
                             (BINB, b_in.partition_broadcast(P)), (CBB, conv_b.partition_broadcast(P))):
                pool.dma_start(dst, src).then_inc(ld_res, 16)
            for n in range(4):
                pool.wait_ge(ln_var, n + 1)
                if n == 0:
                    pool.wait_ge(half_set, 2)
                rs = RSTD[:, 8 * n:8 * n + 8]
                nc.gpsimd.tensor_tensor(out=rs, in0=rs, in1=HALF[:, 0, :], op=ALU.pow).then_inc(ln_rstd, 1)
                pool.wait_ge(ln_rstd, n + 1)
                for t in range(8 * n + 4, 8 * n + 8):
                    ins = nc.gpsimd.tensor_scalar(out=XN[:, t, :], in0=X[:, t, :], scalar1=MV[:, t, 0:1],
                                                  scalar2=RSTD[:, t:t + 1], op0=ALU.subtract, op1=ALU.mult)
                ins.then_inc(ln_xn[1], 1)
                if n == 0:
                    pool.wait_ge(ld_res, 64)
                if n < 3:
                    link(nc.gpsimd.tensor_tensor(out=WRES[:, n, 0:OD], in0=WIN, in1=CWB[:, n, :], op=ALU.mult))
            pool.wait_ge(ld_const, N_CONST)
            nc.gpsimd.tensor_scalar(out=NBQ, in0=BQ, scalar1=-1.0, scalar2=None, op0=ALU.mult)
            for d in range(3):
                link(nc.gpsimd.tensor_tensor(out=CWB[:, d, :], in0=BINB, in1=CWB[:, d, :], op=ALU.mult))
            link(nc.gpsimd.tensor_tensor(out=RBIAS[:, 0, :], in0=CWB[:, 0, :], in1=CWB[:, 1, :], op=ALU.add))
            link(nc.gpsimd.tensor_tensor(out=RBIAS[:, 0, :], in0=RBIAS[:, 0, :], in1=CWB[:, 2, :], op=ALU.add))
            link(nc.gpsimd.tensor_tensor(out=RBIAS[:, 0, :], in0=RBIAS[:, 0, :], in1=CBB, op=ALU.add))
            for n, d in ((1, 0), (2, 2)):
                link(nc.gpsimd.tensor_scalar(out=CWB[:, d, :], in0=CWB[:, d, :], scalar1=EDGES[:, n - 1:n],
                                             scalar2=None, op0=ALU.mult))
                link(nc.gpsimd.tensor_tensor(out=RBIAS[:, n, :], in0=RBIAS[:, 0, :], in1=CWB[:, d, :],
                                             op=ALU.subtract))
            for n, (whole, hi, lo) in enumerate(((GW0, GWH0, GWL0), (UW0, UWH0, UWL0))):
                pool.wait_ge(gw0_hi, n + 1)
                nc.gpsimd.tensor_tensor(out=lo[:, :, :], in0=whole, in1=hi[:, :, :].bitcast(F32), op=ALU.subtract)\
                  .then_inc(gw0_lo, 1)

            def split0_lo(ck):
                pool.wait_ge(x0_hi, ck + 1)
                nc.gpsimd.tensor_tensor(out=XLO0[:, ck % 2, :], in0=XNT[:, 1 + CH * ck:1 + CH * (ck + 1)],
                                        in1=XHI0[:, ck % 2, :].bitcast(F32), op=ALU.subtract).then_inc(x0_lo, 1)

            split0_lo(0)
            pool.wait_ge(ln_xn[0], 4)
            for n in range(NCH):
                ins = nc.gpsimd.tensor_tensor(out=X[:, TPC * n:TPC * (n + 1), :], in0=X[:, TPC * n:TPC * (n + 1), :],
                                              in1=BOUT.unsqueeze(1).broadcast_to((P, TPC, D)), op=ALU.add)
            ins.then_inc(bout_in, 1)

            for ck in range(NCH):
                for m in range(M0):
                    n = N0 * ck + m
                    pool.wait_ge(mult_done, n + 1)
                    pool.wait_ge(ld_wexp0[m], 32 * (ck + 1))
                    nc.gpsimd.tensor_tensor(out=AM0[:, n % 3, :], in0=AM0[:, n % 3, :], in1=WB0[:, m, :],
                                            op=ALU.mult).then_inc(weighted, 1)
                    if m == SPLIT0_AT and ck + 1 < NCH:
                        split0_lo(ck + 1)
            for j in range(NI // 2):
                pool.wait_ge(h_dec, j + 1)
                hv = h_blocks(j)
                nc.gpsimd.tensor_tensor(out=hv, in0=hv, in1=FBB.rearrange("p (g c) -> p g c", c=8).unsqueeze(1)
                                        .broadcast_to((P, 2, 2 * D // 8, 8)),
                                        op=ALU.add).then_inc(h_ready, 1)
            for c in range(2):
                for k in range(NK):
                    q = NK * c + k
                    pool.wait_ge(prod_in, q + 1)
                    if q >= 2:
                        pool.wait_ge(i1_mm, q - 1)
                    s = q % 2
                    nc.gpsimd.tensor_tensor(out=YS[:, s, 0, :], in0=T1[:, s, 0, :], in1=T2[:, s, 1, :],
                                            op=ALU.subtract)
                    nc.gpsimd.tensor_tensor(out=YS[:, s, 1, :], in0=T1[:, s, 1, :], in1=T2[:, s, 0, :],
                                            op=ALU.add).then_inc(y_in, 1)
            pool.wait_ge(i1_mm, 2 * NK)
            nc.gpsimd.memset(WB1[:, :, :], 0.0).then_inc(wb_zero, 1)
            nc.gpsimd.memset(KVS[:, :, :, 2 * P:2 * P + 1], 1.0).then_inc(one_set, 1)
            for st in range(STEPS):
                if 1 <= st <= NCH:
                    pool.wait_ge(ln1_var, st)
                    rs = RSTD[:, TPC * (st - 1):TPC * st]
                    nc.gpsimd.tensor_tensor(out=rs, in0=rs, in1=HALF[:, 0, 0:TPC], op=ALU.pow).then_inc(ln1_rstd, 1)
                if 4 <= st < NCH + 4:
                    for j in (2 * (st - 4), 2 * (st - 4) + 1):
                        pool.wait_ge(k_exp, j + 1)
                        k = KVS[:, j % 3, :, 0:P]
                        nc.gpsimd.tensor_tensor(out=k, in0=k, in1=KEX[:, j % 3], op=ALU.add).then_inc(k_fm, 1)
                if st == XS0_AT:
                    pool.wait_ge(wa_hi, 1)
                    nc.gpsimd.tensor_tensor(out=WAL[:, :, :], in0=WA1, in1=WAH[:, :, :].bitcast(F32),
                                            op=ALU.subtract).then_inc(wa_lo, 1)
                    split_lo(pool, 0)
                if st in (PREP_AT + 1, PREP_AT + 2):
                    for t in (2 * (st - PREP_AT - 1), 2 * (st - PREP_AT - 1) + 1):
                        router_root(pool, 0, t)
                for at, whole, hi, lo, hi_in, lo_in in ((UP_AT, UP1, UPH, UPL, up_hi, up_lo),
                                                        (DN_AT, DN1, DNH, DNL, dn_hi, dn_lo)):
                    if at <= st < at + W_PARTS:
                        ms = slice(M1 // W_PARTS * (st - at), M1 // W_PARTS * (st - at + 1))
                        pool.wait_ge(hi_in, 1)
                        nc.gpsimd.tensor_tensor(out=lo[:, ms, :], in0=whole[:, ms, :], in1=hi[:, ms, :].bitcast(F32),
                                                op=ALU.subtract).then_inc(lo_in, 1)

            def accumulate(q):
                ck, e = divmod(q, E1)
                if e:
                    pool.wait_ge(scaled, q + 1)
                    acc = ACC1[:, ck % 2, :]
                    if e >= 2:
                        pool.wait_ge(summed, (E1 - 1) * ck + e - 1)
                    nc.gpsimd.tensor_tensor(out=acc, in0=acc, in1=TMP1[:, q % 2, :], op=ALU.add).then_inc(summed, 1)

            for n in range(NCH * M1 + LAG + 3):
                ck, m = divmod(n, M1)
                if n < NCH * M1:
                    pool.wait_ge(mult1, n + 1)
                    if n >= 4:
                        pool.wait_ge(down1_mm, n - 3)
                    nc.gpsimd.tensor_tensor(out=AML[:, n % 4, :], in0=AM1[:, n % 2, :],
                                            in1=AMH[:, n % 4, :].bitcast(F32), op=ALU.subtract).then_inc(am_lo, 1)
                if n >= LAG + 3 and (n - LAG - 3) % 2 == 0:
                    accumulate((n - LAG - 3) // 2)
                if ck + 1 < NCH:
                    if m == XS_AT:
                        split_lo(pool, ck + 1)
                    if GH_AT < m <= GH_AT + TPC:
                        router_root(pool, ck + 1, m - GH_AT - 1)

        @block.scalar
        def _(act):
            for j in range(1, NCH, 2):
                act.wait_ge(lnt_done, j + 1)
                nc.scalar.activation(XNT[:, 1 + CH * j:1 + CH * (j + 1)], PS[j % 4][:, :], ACT.Copy)\
                  .then_inc(lnt_act, 1)
            act.wait_ge(ld_w0, 48)
            nc.scalar.activation(GWH0[:, :, :], GW0, ACT.Copy).then_inc(gw0_hi, 1)
            nc.scalar.activation(UWH0[:, :, :], UW0, ACT.Copy).then_inc(gw0_hi, 1)

            def split0_hi(ck):
                if ck >= 2:
                    act.wait_ge(u_mm, N0 * (ck - 1))
                else:
                    act.wait_ge(lnt_dve, 4)
                nc.scalar.activation(XHI0[:, ck % 2, :], XNT[:, 1 + CH * ck:1 + CH * (ck + 1)], ACT.Copy)\
                  .then_inc(x0_hi, 1)

            def router0_exp(n):
                act.wait_ge(rt_sub, n + 1)
                sc = SCO[:, NI * n:NI * (n + 1), :]
                nc.scalar.activation(sc, sc, ACT.Exp).then_inc(rt_exp, 1)

            split0_hi(0)
            router0_exp(0)
            act.wait_ge(ld_filt, 80)
            for n in range(NCH * N0):
                act.wait_ge(g_mm, n + 1)
                if n >= 2:
                    act.wait_ge(mult_done, n - 1)
                nc.scalar.activation(SG0[:, n % 2, :], PS[n % 2][:, :], ACT.Silu).then_inc(silu_done, 1)
                if n == RT_EXP_AT:
                    router0_exp(1)
                if n % N0 == SPLIT0_AT and n // N0 + 1 < NCH:
                    split0_hi(n // N0 + 1)
                if n == SIN_AT:
                    act.wait_ge(z_wrapped, 2)
                    nc.scalar.activation(SIN64, ZF, ACT.Sin).then_inc(sin_done, 1)
                    act.wait_ge(sin_done, 1)
                if n == SIN_AT + 2:
                    nc.scalar.activation(FDB, FDB, ACT.Exp).then_inc(dec_exp, 1)
                    act.wait_ge(dec_exp, 1)
                    for i in range(NI):
                        nc.scalar.activation(DEC[:, i, :], FDB, ACT.Exp, scale=NEGT[:, i:i + 1]).then_inc(dec_exp, 1)

            def block_copies(t):
                def ft(j):
                    J = 8 * t + j
                    act.wait_ge(f0_mm, J + 1)
                    if J >= 2:
                        act.wait_ge(f1_mm, 2 * (J - 1))
                    if t and j < 2:
                        act.wait_ge(i3_mm, 16 * (t - 1))
                    nc.scalar.activation(FT[:, J % 2, :], PS[6 + J % 2][:, :], ACT.Copy).then_inc(ft_in, 1)

                def a(j):
                    K = 16 * t + 2 * j + 1
                    act.wait_ge(f1_mm, K + 1)
                    nc.scalar.activation(a_slot(2 * j + 1), a_bank(K), ACT.Copy).then_inc(a_in[1], 1)

                ft(0)
                for j in range(8):
                    if j < 7:
                        ft(j + 1)
                    a(j)

            block_copies(0)
            for k in range(1, NK, 2):
                act.wait_ge(f2_mm, k + 1)
                nc.scalar.activation(H[:, k], bank(k % 3, 2, 2 * D), ACT.Copy).then_inc(spec_act, 1)
            for c in range(2):
                block_copies(c + 1)
                for k in range(NK):
                    q = NK * c + k
                    act.wait_ge(i1_mm, q + 1)
                    s, n = z_slots(k)
                    nc.scalar.activation(a_rows(s, n), bank(3 + q % 3, n, 2 * D // 4, 4), ACT.Copy).then_inc(z_in, 1)
                for p in range(16):
                    q = 16 * c + p
                    act.wait_ge(i2_mm, q + 1)
                    if q >= 4:
                        act.wait_ge(i3_mm, q - 3)
                    nc.scalar.activation(ZT[:, q % 4, :], PS[4 + q % 4][:, :], ACT.Copy).then_inc(zt_in, 1)
            for st in range(STEPS):
                if st < NCH:
                    act.wait_ge(vt_mm, st + 1)
                    if st >= 2:
                        act.wait_ge(o_mm, st - 1)
                    nc.scalar.activation(VT[:, st % 2, :], PS[6][:, :], ACT.Copy).then_inc(vt_in, 1)
                if 3 <= st < NCH + 3:
                    j = st - 3
                    act.wait_ge(xnt1_mm, j + 1)
                    nc.scalar.activation(XNT1[:, CH * j:CH * (j + 1)], PS[0][:, :], ACT.Copy).then_inc(xnt1_in, 1)
                if 4 <= st < NCH + 4:
                    for j in (2 * (st - 4), 2 * (st - 4) + 1):
                        act.wait_ge(kv_bias, j + 1)
                        if j >= 3:
                            act.wait_ge(k_fm, j - 2)
                        k = KVS[:, j % 3, :, 0:P]
                        nc.scalar.activation(KEX[:, j % 3], k, ACT.Relu, scale=-1.0).then_inc(k_neg, 1)
                        act.wait_ge(k_neg, j + 1)
                        nc.scalar.activation(k, k, ACT.Relu)
                        nc.scalar.activation(KEX[:, j % 3], KEX[:, j % 3], ACT.Exp, scale=-1.0).then_inc(k_exp, 1)
                if st == XS0_AT:
                    act.wait_ge(ld_w1, N_W1)
                    nc.scalar.activation(WAH[:, :, :], WA1, ACT.Copy).then_inc(wa_hi, 1)
                    split_hi(act, 0)
                if st == DN_AT:
                    act.wait_ge(comp_mm, PAIRS)
                    act.wait_ge(up_lo, W_PARTS)
                    nc.scalar.activation(DNH[:, :, :], DN1[:, :, :], ACT.Copy).then_inc(dn_hi, 1)
                if st == UP_AT:
                    nc.scalar.activation(UPH[:, :, :], UP1[:, :, :], ACT.Copy).then_inc(up_hi, 1)
                if st == PREP_AT:
                    for t in range(TPC):
                        gate_square(act, 0, t)
                if COMP_AT <= st < COMP_AT + PAIRS:
                    q = st - COMP_AT
                    act.wait_ge(comp_mm, q + 1)
                    nc.scalar.activation(GWH[:, 4 * q:4 * q + 4, :], bank(4, 4, P), ACT.Copy).then_inc(gw_hi, 1)
                if st == PREP_AT + 5:
                    router_exp(act, 0)

            for ck in range(NCH):
                for m in range(M1):
                    n = M1 * ck + m
                    act.wait_ge(g1_mm, n + 1)
                    if n >= 2:
                        act.wait_ge(mult1, n - 1)
                    nc.scalar.activation(SG1[:, n % 2, :], PS[n % 2][:, :], ACT.Silu).then_inc(silu1, 1)
                    if ck + 1 < NCH:
                        if m == XS_AT:
                            split_hi(act, ck + 1)
                        if GH_AT <= m < GH_AT + TPC:
                            gate_square(act, ck + 1, m - GH_AT)
                        if m == EXP_AT:
                            router_exp(act, ck + 1)
                    if m == Q_AT + 1:
                        act.wait_ge(q_mm, ck + 1)
                        if ck:
                            act.wait_ge(nd_mm, ck)
                        nc.scalar.activation(QEX, PS[6][:, :], ACT.Relu, bias=NBQ, scale=-1.0).then_inc(q_neg, 1)
                        nc.scalar.activation(QPS, PS[6][:, :], ACT.Relu, bias=BQ)
                        act.wait_ge(q_neg, ck + 1)
                        nc.scalar.activation(QEX, QEX, ACT.Exp, scale=-1.0).then_inc(q_exp, 1)

        @block.vector
        def _(dve):
            done = [0]

            def link(ins):
                done[0] += 1
                ins.then_inc(dve_chain, 1)
                dve.wait_ge(dve_chain, done[0])

            def stats(t0, n):
                for t in range(t0, t0 + n):
                    ins = nc.vector.bn_stats(out=STAT[:, t, :], in_=X[:, t, :])
                link(ins)
                for t in range(t0, t0 + n):
                    ins = nc.vector.bn_aggr(out=MV[:, t, :], in_=STAT[:, t, :])
                link(ins)
                return nc.vector.tensor_scalar(out=RSTD[:, t0:t0 + n], in0=MV[:, t0:t0 + n, 1], scalar1=EPS,
                                               scalar2=None, op0=ALU.add)

            def normed(t, dst):
                return nc.vector.tensor_scalar(out=dst, in0=X[:, t, :], scalar1=MV[:, t, 0:1],
                                               scalar2=RSTD[:, t:t + 1], op0=ALU.subtract, op1=ALU.mult)

            def pairs_of(values, n):
                return (values.unsqueeze(2).broadcast_to((P, n, 8, 8)), values.unsqueeze(3).broadcast_to((P, n, 8, 8)))

            def rank_ties(values, ge, n):
                vj, ve = pairs_of(values, n)
                link(nc.vector.tensor_tensor(out=ge, in0=vj, in1=ve, op=ALU.is_ge))
                link(nc.vector.tensor_tensor(out=ge, in0=ge, in1=BEFORE.unsqueeze(1).broadcast_to((P, n, 8, 8)),
                                             op=ALU.mult))

            def rank_larger(values, ge, gt, n):
                vj, ve = pairs_of(values, n)
                link(nc.vector.tensor_tensor(out=gt, in0=vj, in1=ve, op=ALU.is_gt))
                link(nc.vector.tensor_tensor(out=ge, in0=ge, in1=gt, op=ALU.max))

            def chosen(ge, rnk, k):
                link(nc.vector.tensor_reduce(out=rnk, in_=ge, axis=AX.X, op=ALU.add))
                link(nc.vector.tensor_scalar(out=rnk, in0=rnk, scalar1=float(k), scalar2=None, op0=ALU.is_lt))

            def per_tile(v, n):
                return v.unsqueeze(2).broadcast_to((P, n, 8))

            def normalise(dst, src, red, inv, tiny, n):
                link(nc.vector.tensor_reduce(out=red, in_=src, axis=AX.X, op=ALU.add))
                if tiny:
                    link(nc.vector.tensor_scalar(out=red, in0=red, scalar1=tiny, scalar2=None, op0=ALU.add))
                link(nc.vector.reciprocal(inv, red))
                return nc.vector.tensor_tensor(out=dst, in0=src, in1=per_tile(inv, n), op=ALU.mult)

            nc.vector.memset(XNT[:, 0:1], 0.0)
            nc.vector.memset(XNT[:, TOK + 1:TOK + 2], 0.0)
            nc.vector.memset(HALF[:, 0, :], -0.5).then_inc(half_set, 1)
            nc.vector.memset(HALF[:, 1, :], 0.5).then_inc(half_set, 1)
            nc.vector.memset(SHIFT[:, :, :], 0.0).then_inc(shift_zero, 1)
            for q in range(5):
                if q < 4:
                    dve.wait_ge(ld_x[q], 16)
                    stats(8 * q, 8).then_inc(ln_var, 1)
                if q:
                    dve.wait_ge(ln_rstd, q)
                    for t in range(8 * (q - 1), 8 * (q - 1) + 4):
                        ins = normed(t, XN[:, t, :])
                    ins.then_inc(ln_xn[0], 1)
                if q >= 2:
                    j = 2 * (q - 2)
                    dve.wait_ge(lnt_done, j + 1)
                    nc.vector.tensor_copy(XNT[:, 1 + CH * j:1 + CH * (j + 1)], PS[j % 4][:, :]).then_inc(lnt_dve, 1)
            dve.wait_ge(lnt_done, 7)
            nc.vector.tensor_copy(XNT[:, 1 + CH * 6:1 + CH * 7], PS[2][:, :]).then_inc(lnt_dve, 1)
            dve.wait_ge(lnt_act, 4)
            dve.wait_ge(lnt_dve, 4)
            dve.wait_ge(shift_zero, 1)
            nc.vector.tensor_copy(SHIFT[:, 0, 1:P], XNT[:, 1 + L:L + P])
            nc.vector.tensor_copy(SHIFT[:, 1, 0:P - 1], XNT[:, L - P + 2:L + 1]).then_inc(edge_set, 1)

            def router0(n, step):
                half = slice(NI * n, NI * (n + 1))
                log, sco, cor, rnk, wgt = (v[:, half, :] for v in (LOG, SCO, COR, RNK, WGT3))
                red, red2 = RED[:, half], RED2[:, half]
                ge, gt = CMP0
                vj, ve = pairs_of(cor, NI)
                if step == 0:
                    link(nc.vector.tensor_reduce(out=red, in_=log, axis=AX.X, op=ALU.max))
                    nc.vector.tensor_tensor(out=sco, in0=log, in1=per_tile(red, NI), op=ALU.subtract)\
                      .then_inc(rt_sub, 1)
                if step == 1:
                    dve.wait_ge(rt_exp, n + 1)
                    link(normalise(wgt, sco, red, red2, None, NI))
                    link(nc.vector.tensor_scalar(out=cor, in0=wgt, scalar1=ROUTB, scalar2=None, op0=ALU.add))
                if step == 2:
                    link(nc.vector.tensor_tensor(out=ge, in0=vj, in1=ve, op=ALU.is_ge))
                if step == 3:
                    link(nc.vector.tensor_tensor(out=ge, in0=ge, in1=BEFORE.unsqueeze(1).broadcast_to((P, NI, 8, 8)),
                                                 op=ALU.mult))
                if step == 4:
                    link(nc.vector.tensor_tensor(out=gt, in0=vj, in1=ve, op=ALU.is_gt))
                if step == 5:
                    link(nc.vector.tensor_tensor(out=ge, in0=ge, in1=gt, op=ALU.max))
                if step == 6:
                    chosen(ge, rnk, 4)
                    link(nc.vector.tensor_tensor(out=cor, in0=rnk, in1=wgt, op=ALU.mult))
                if step == 7:
                    normalise(wgt, cor, red, red2, 1e-20, NI).then_inc(rt_w, 1)
                if step == 8:
                    dve.wait_ge(rt_tr, n + 1)
                    nc.vector.tensor_copy(WTT[:, n, :], PS[6 + n][:, 0:P]).then_inc(rt_out, 1)

            dve.wait_ge(pool_chain, 13)
            for t in range(T):
                dve.wait_ge(res_mm, t + 1)
                kind = 1 if t % NI == 0 else 2 if t % NI == NI - 1 else 0
                nc.vector.tensor_tensor(out=G[:, t, :, :], in0=bank(t % 4, 2, D),
                                        in1=RBIAS[:, kind, 0:2 * D].rearrange("p (g c) -> p g c", g=2), op=ALU.add)
                nc.vector.tensor_tensor(out=VG[:, 16 * (t // NI):16 * (t // NI) + 16, t % NI, :],
                                        in0=bank(t % 4, 16, 8, at=2 * D),
                                        in1=RBIAS[:, kind, 2 * D:OD].rearrange("p (g c) -> p g c", c=8),
                                        op=ALU.add)
                nc.vector.tensor_copy(LOG[:, t, :], PS[t % 4][:, OD:OD + E0]).then_inc(res_out, 1)
                if t == RT_STEPS[0][0] or t == T - 1:
                    dve.wait_ge(res_out, t + 1)
                if t in RT_STEPS[0]:
                    router0(0, RT_STEPS[0].index(t))
            dve.wait_ge(bout_in, 1)
            for ck in range(NCH):
                for m in range(N0):
                    n = N0 * ck + m
                    dve.wait_ge(silu_done, n + 1)
                    dve.wait_ge(u_mm, n + 1)
                    if n >= 3:
                        dve.wait_ge(down_mm, n - 2)
                    nc.vector.tensor_tensor(out=AM0[:, n % 3, :], in0=PS[2 + n % 2][:, :], in1=SG0[:, n % 2, :],
                                            op=ALU.mult).then_inc(mult_done, 1)
                    if ck and m == 2:
                        add_down(dve, ck - 1)
                    if n in RT_STEPS[1]:
                        router0(1, RT_STEPS[1].index(n))
                    if n == 0:
                        nc.vector.memset(arena[FH:FH + 1, rH + L:rH + 2 * L], 1.0).then_inc(ones_row, 1)
                    if Z_AT <= n < Z_AT + 4:
                        i = n - Z_AT
                        dve.wait_ge(z_mm, i + 1)
                        nc.vector.tensor_scalar(out=ZF[:, CH * i:CH * (i + 1)], in0=PS[6 + i % 2][0:FH, :],
                                                scalar1=B1, scalar2=10.0, op0=ALU.add, op1=ALU.mult)\
                          .then_inc(z_out, 1)
                    if n == Z_AT + 3:
                        dve.wait_ge(z_out, 4)
                    if Z_AT + 4 <= n < Z_AT + 12:
                        step, half = divmod(n - Z_AT - 4, 2)
                        zf, zn = ZF[:, L // 2 * half:L // 2 * (half + 1)], ZN[:, L // 2 * half:L // 2 * (half + 1)]
                        if step == 0:
                            link(nc.vector.tensor_scalar(out=zn, in0=zf, scalar1=1 / (2 * math.pi), scalar2=MAGIC,
                                                         op0=ALU.mult, op1=ALU.add))
                            link(nc.vector.tensor_scalar(out=zn, in0=zn, scalar1=-MAGIC, scalar2=None, op0=ALU.add))
                        if step == 1:
                            link(nc.vector.scalar_tensor_tensor(out=zf, in0=zn, scalar=-PI2_HI, in1=zf, op0=ALU.mult,
                                                                op1=ALU.add))
                        if step == 2:
                            link(nc.vector.scalar_tensor_tensor(out=zf, in0=zn, scalar=-PI2_LO, in1=zf, op0=ALU.mult,
                                                                op1=ALU.add))
                        if step == 3:
                            nc.vector.tensor_scalar(out=zf, in0=zf, scalar1=PI_IN, scalar2=-PI_IN, op0=ALU.min,
                                                    op1=ALU.max).then_inc(z_wrapped, 1)
            add_down(dve, NCH - 1)
            dve.wait_ge(dec_exp, 1 + NI)
            for j in range(NI // 2):
                dve.wait_ge(h_mm, j + 1)
                nc.vector.tensor_tensor(out=h_blocks(j), in0=bank(4 + j % 4, 2, 2 * D // 8, 8),
                                        in1=DEC[:, 2 * j:2 * j + 2, :].rearrange("p i (g c) -> p i g c", c=8),
                                        op=ALU.mult).then_inc(h_dec, 1)

            def block_copies(t):
                for j in range(8):
                    K = 16 * t + 2 * j
                    dve.wait_ge(f1_mm, K + 1)
                    nc.vector.tensor_copy(a_slot(2 * j), a_bank(K)).then_inc(a_in[0], 1)

            block_copies(0)
            for k in range(0, NK, 2):
                dve.wait_ge(f2_mm, k + 1)
                nc.vector.tensor_copy(H[:, k], bank(k % 3, 2, 2 * D)).then_inc(spec_dve, 1)
            for c in range(2):
                block_copies(c + 1)
                if c == 0:
                    dve.wait_ge(spec_act, NK // 2)
                    dve.wait_ge(spec_dve, NK - NK // 2)
                for k in range(NK):
                    q = NK * c + k
                    dve.wait_ge(f2_mm, NK + q + 1)
                    if q >= 2:
                        dve.wait_ge(y_in, q - 1)
                    xs = bank(q % 3, 2, B, D)
                    for part, dst in ((0, T1), (1, T2)):
                        h = H[:, k, part, D * c:D * (c + 1)].unsqueeze(1).unsqueeze(1).broadcast_to((P, 2, B, D))
                        ins = nc.vector.tensor_tensor(out=dst[:, q % 2].rearrange("p r (b c) -> p r b c", b=B),
                                                      in0=xs, in1=h, op=ALU.mult)
                    ins.then_inc(prod_in, 1)
                for r in range(8):
                    R = 8 * c + r
                    dve.wait_ge(i3_mm, 2 * (R + 1))
                    b, c0 = r // 4, 32 * (r % 4)
                    gate = G[:, NI * b:NI * (b + 1), c, c0:c0 + 32].rearrange("p i (g s) -> p g i s", s=4)
                    if c:
                        dst = V[:, NI * b:NI * (b + 1), c0:c0 + 32].rearrange("p i (g s) -> p g i s", s=4)
                        nc.vector.tensor_tensor(out=dst, in0=bank(R % 4, 8, NI, 4), in1=gate, op=ALU.mult)\
                          .then_inc(gated, 1)
                        continue
                    for h in range(2):
                        dst = VG[:, 16 * b + 4 * (r % 4):16 * b + 4 * (r % 4) + 4, :, 4 * h:4 * h + 4]
                        ins = nc.vector.tensor_tensor(out=dst, in0=bank(R % 4, 8, NI, 4)[:, h:8:2],
                                                      in1=gate[:, h:8:2], op=ALU.mult)
                    ins.then_inc(gated, 1)
            def norm_sum(ck, t):
                dve.wait_ge(sq_in, TPC * ck + t + 1)
                nc.vector.tensor_reduce(out=LOG1[:, t, :], in_=SQ1[:, t, :, :], axis=AX.X, op=ALU.add)\
                  .then_inc(log1_in, 1)

            def router_rank(ck):
                dve.wait_ge(log1_in, TPC * (ck + 1))
                rank_ties(LOG1, CMP1[0], TPC)
                rank_larger(LOG1, *CMP1, TPC)

            def router_sub(ck):
                chosen(CMP1[0], RNK1, 2)
                dve.wait_ge(sqrt1, TPC * (ck + 1))
                link(nc.vector.tensor_reduce(out=RED11, in_=SCO1, axis=AX.X, op=ALU.max))
                nc.vector.tensor_tensor(out=SCO1, in0=SCO1, in1=per_tile(RED11, TPC), op=ALU.subtract)\
                  .then_inc(sub1, 1)

            def router_weights(ck):
                dve.wait_ge(exp1, ck + 1)
                link(nc.vector.tensor_tensor(out=COR1, in0=RNK1, in1=SCO1, op=ALU.mult))
                normalise(WGT13, COR1, RED11, RED12, None, TPC).then_inc(w1_in, 1)

            def weights_out(ck):
                dve.wait_ge(wt1_mm, ck + 1)
                if ck:
                    dve.wait_ge(st_wexp1, 16 * ck)
                nc.vector.tensor_copy(WTT1, PS[router_bank(ck)][0:TPC * 8, 0:P]).then_inc(wt1_in, 1)

            dve.wait_ge(one_set, 1)
            for st in range(1, STEPS):
                if st <= NCH:
                    j = st - 1
                    dve.wait_ge(o_mm, j + 1)
                    xs = X[:, TPC * j:TPC * (j + 1), :]
                    nc.vector.tensor_tensor(out=xs, in0=bank(7, TPC, D), in1=xs, op=ALU.add).then_inc(o_added, 1)
                    dve.wait_ge(o_added, j + 1)
                    stats(TPC * j, TPC).then_inc(ln1_var, 1)
                if 4 <= st < NCH + 4:
                    for j in (2 * (st - 4), 2 * (st - 4) + 1):
                        dve.wait_ge(kv_mm, j + 1)
                        if j >= 3:
                            dve.wait_ge(kvs_mm, 2 * (j - 2))
                        nc.vector.tensor_tensor(out=KVS[:, j % 3, :, 0:2 * P], in0=bank(1 + j % 2, 2, 2 * P),
                                                in1=BKV.unsqueeze(1).broadcast_to((P, 2, 2 * P)), op=ALU.add)\
                          .then_inc(kv_bias, 1)
                if st <= NCH:
                    j = st - 1
                    dve.wait_ge(ln1_rstd, j + 1)
                    if j >= 2:
                        dve.wait_ge(xnt1_mm, j - 1)
                    for t in range(TPC):
                        ins = normed(TPC * j + t, XNR[:, j % 2, t, :])
                    ins.then_inc(ln1_xn, 1)
                if COMP_AT <= st < COMP_AT + PAIRS:
                    q = st - COMP_AT
                    dve.wait_ge(gw_hi, q + 1)
                    ms = slice(4 * q, 4 * q + 4)
                    nc.vector.tensor_tensor(out=GWL[:, ms, :], in0=bank(4, 4, P), in1=GWH[:, ms, :].bitcast(F32),
                                            op=ALU.subtract).then_inc(gw_lo, 1)
                if st == PREP_AT + 1:
                    for t in range(TPC):
                        norm_sum(0, t)
                if st == PREP_AT + 2:
                    router_rank(0)
                if st == PREP_AT + 4:
                    router_sub(0)
                if st == PREP_AT + 5:
                    router_weights(0)
                if st == PREP_AT + 7:
                    weights_out(0)
            dve.wait_ge(kvs_mm, T)
            for b in range(B):
                nc.vector.tensor_tensor(out=KVB[:, b, :], in0=PS[5][:, 256 * b:256 * b + P], in1=HEADS, op=ALU.mult)
                link(nc.vector.tensor_copy(KSC[:, b, :], PS[5][:, 256 * b + P:256 * b + P + 1]))
                nc.vector.tensor_scalar(out=KSB[:, b, :], in0=HEADS, scalar1=KSC[:, b, :], scalar2=None,
                                        op0=ALU.mult).then_inc(kv_mask, 1)


            def scale(q):
                ck, e = divmod(q, E1)
                dve.wait_ge(down1_mm, 2 * (q + 1))
                dve.wait_ge(ld_wexp1[e], 16 * (ck + 1))
                if e == 0 and ck >= 2:
                    dve.wait_ge(ot_in, ck - 1)
                if e and q >= 2:
                    dve.wait_ge(summed, (E1 - 1) * ck + max(e - 2, 0))
                nc.vector.tensor_tensor(out=TMP1[:, q % 2, :] if e else ACC1[:, ck % 2, :], in0=PS[4 + q % 2][:, :],
                                        in1=WBC1[:, e, :], op=ALU.mult).then_inc(scaled, 1)

            def total(ck):
                dve.wait_ge(wo_mm, ck + 1)
                dve.wait_ge(summed, (E1 - 1) * (ck + 1))
                if ck:
                    dve.wait_ge(y_mm, ck)
                nc.vector.scalar_tensor_tensor(out=OT1, in0=PS[7][:, :], scalar=BO, in1=ACC1[:, ck % 2, :],
                                               op0=ALU.add, op1=ALU.add).then_inc(ot_in, 1)

            def finish(ck):
                dve.wait_ge(y_mm, ck + 1)
                if ck >= 2:
                    dve.wait_ge(st_out[ck % 2], 16 * (ck // 2))
                nc.vector.tensor_tensor(out=ST1[:, ck % 2], in0=bank(7, TPC, D),
                                        in1=X[:, TPC * ck:TPC * (ck + 1), :], op=ALU.add).then_inc(y_sum, 1)

            for n in range(NCH * M1 + LAG + 2):
                ck, m = divmod(n, M1)
                if ck < NCH:
                    dve.wait_ge(silu1, n + 1)
                    dve.wait_ge(u1_mm, n + 1)
                    if n >= 2:
                        dve.wait_ge(am_lo, n - 1)
                    nc.vector.tensor_tensor(out=AM1[:, n % 2, :], in0=PS[2 + n % 2][:, :], in1=SG1[:, n % 2, :],
                                            op=ALU.mult)
                    if n >= 4:
                        dve.wait_ge(down1_mm, n - 3)
                    nc.vector.tensor_tensor(out=AMH[:, n % 4, :], in0=PS[2 + n % 2][:, :], in1=SG1[:, n % 2, :],
                                            op=ALU.mult).then_inc(mult1, 1)
                if n >= LAG + 2 and (n - LAG - 2) % 2 == 0:
                    scale((n - LAG - 2) // 2)
                if ck and m == OT_AT:
                    total(ck - 1)
                if ck and m == FIN_AT:
                    finish(ck - 1)
                if ck + 1 < NCH:
                    if GH_AT < m <= GH_AT + TPC:
                        norm_sum(ck + 1, m - GH_AT - 1)
                    if m == RANK_AT:
                        router_rank(ck + 1)
                    if m == SUB_AT:
                        router_sub(ck + 1)
                    if m == RW_AT:
                        router_weights(ck + 1)
                    if m == WT_AT:
                        weights_out(ck + 1)
                if ck < NCH:
                    if m == QF_AT:
                        dve.wait_ge(q_exp, ck + 1)
                        nc.vector.tensor_tensor(out=QPS, in0=QPS, in1=QEX, op=ALU.add).then_inc(q_fm, 1)
                    if m == ND_AT:
                        dve.wait_ge(nd_mm, ck + 1)
                        link(nc.vector.tensor_scalar(out=DEN, in0=PS[7][:, :], scalar1=1e-6, scalar2=None,
                                                     op0=ALU.add))
                        for h in range(2):
                            hs = slice(CH // 2 * h, CH // 2 * (h + 1))
                            ins = nc.vector.reciprocal(DEN[:, hs], DEN[:, hs])
                        link(ins)
                        if ck:
                            dve.wait_ge(wo_mm, ck)
                        nc.vector.tensor_tensor(out=ATT, in0=PS[6][:, :], in1=DEN, op=ALU.mult).then_inc(att_in, 1)
            total(NCH - 1)
            finish(NCH - 1)

        @block.tensor
        def _(pe):
            mm = nc.tensor.matmul

            pe.wait_ge(ld_ident, 16)
            for j in range(NCH):
                pe.wait_ge(ln_xn[j % 2], j // 2 + 1)
                if j >= 4:
                    pe.wait_ge(lnt_act if j % 2 else lnt_dve, (j - 4) // 2 + 1)
                for t in range(TPC):
                    ins = nc.tensor.transpose(PS[j % 4][:, P * t:P * (t + 1)], XN[:, TPC * j + t, :], IDENT)
                ins.then_inc(lnt_done, 1)
            pe.wait_ge(lnt_act, 4)
            pe.wait_ge(lnt_dve, 4)
            pe.wait_ge(ld_const, N_CONST)

            def router0_back(n):
                pe.wait_ge(rt_w, n + 1)
                nc.tensor.transpose(PS[6 + n][:, 0:P], WGT[:, P * n:P * (n + 1)], IDENT).then_inc(rt_tr, 1)

            pe.wait_ge(pool_chain, 3)
            pe.wait_ge(edge_set, 1)
            for t in range(T):
                if t == RT_BACK_AT[0]:
                    router0_back(0)
                if t >= 4:
                    pe.wait_ge(res_out, t - 3)
                for d in (1, 0, 2):
                    xt = XNT[:, P * t + d:P * (t + 1) + d]
                    if t == NI and d == 0:
                        xt = SHIFT[:, 0, :]
                    if t == NI - 1 and d == 2:
                        xt = SHIFT[:, 1, :]
                    n = OD + E0 if d == 1 else OD
                    ins = mm(PS[t % 4][:, 0:n], xt, WRES[:, d, 0:n], start=(d == 1), stop=(d == 2),
                             skip_group_check=True)
                ins.then_inc(res_mm, 1)
            pe.wait_ge(gw0_lo, 2)
            pe.wait_ge(res_out, T)

            def split_product(o, left, right, start=True, stop=True):
                (lh, ll), (rh, rl) = left, right
                mm(o, lh, rh, start=start, stop=False)
                mm(o, lh, rl, start=False, stop=False)
                return mm(o, ll, rh, start=False, stop=stop)

            def down0_step(n):
                ck, m = divmod(n, N0)
                if m < M0:
                    pe.wait_ge(weighted, M0 * ck + m + 1)
                else:
                    pe.wait_ge(mult_done, n + 1)
                if m == 0 and ck >= 2:
                    pe.wait_ge(x_added, ck - 1)
                for t in range(TPC):
                    ins = mm(PS[4 + ck % 2][:, D * t:D * (t + 1)], AM0[:, n % 3, P * t:P * (t + 1)],
                             DW0[:, m, :], start=(m == 0 and t == 0), stop=(m == N0 - 1), skip_group_check=True)
                ins.then_inc(down_mm, 1)

            for n in range(NCH * N0 + 2):
                if n < NCH * N0:
                    ck, m = divmod(n, N0)
                    xs = (XHI0[:, ck % 2, :], XLO0[:, ck % 2, :])
                    if m == 0:
                        pe.wait_ge(x0_lo, ck + 1)
                    if n >= 2:
                        pe.wait_ge(silu_done, n - 1)
                    split_product(PS[n % 2][:, :], (GWH0[:, m, :], GWL0[:, m, :]), xs).then_inc(g_mm, 1)
                    if n >= 2:
                        pe.wait_ge(mult_done, n - 1)
                    split_product(PS[2 + n % 2][:, :], (UWH0[:, m, :], UWL0[:, m, :]), xs).then_inc(u_mm, 1)
                if n >= 2:
                    down0_step(n - 2)
                if n == RT_BACK_AT[1]:
                    router0_back(1)
                if Z_AT <= n < Z_AT + 4:
                    i = n - Z_AT
                    if i == 0:
                        pe.wait_ge(ld_filt, 80)
                        pe.wait_ge(ld_pe, 16)
                        pe.wait_ge(rt_out, 2)
                    if i >= 2:
                        pe.wait_ge(z_out, i - 1)
                    mm(PS[6 + i % 2][0:FH, :], W1S, PET[:, CH * i:CH * (i + 1)], start=True, stop=True)\
                      .then_inc(z_mm, 1)

            pe.wait_ge(silu_done, NCH * N0)
            pe.wait_ge(mult_done, NCH * N0)
            pe.wait_ge(x_added, NCH)
            pe.wait_ge(sin_done, 1)
            pe.wait_ge(ones_row, 1)
            for j in range(NI // 2):
                if j >= 4:
                    pe.wait_ge(h_dec, j - 3)
                for i in range(2):
                    t = 2 * j + i
                    ins = mm(PS[4 + j % 4][:, 2 * D * i:2 * D * (i + 1)], SINT[:, P * t:P * (t + 1)], W2S,
                             start=True, stop=True)
                ins.then_inc(h_mm, 1)

            def block_dft(t, src):
                def transposes(j):
                    J = 8 * t + j
                    if t >= 2 and j % 4 == 0:
                        pe.wait_ge(gated, 8 * (t - 2) + j + 4)
                    if J >= 2:
                        pe.wait_ge(ft_in, J - 1)
                    for n in range(4):
                        g = 4 * j + n
                        ins = nc.tensor.transpose(PS[6 + J % 2][:, P * n:P * (n + 1)], src[:, g], IDENT)
                    ins.then_inc(f0_mm, 1)

                def rows(j):
                    J = 8 * t + j
                    pe.wait_ge(ft_in, J + 1)
                    for h in range(2):
                        K = 2 * J + h
                        if t >= 2 and j == 1:
                            pe.wait_ge(gated, 8 * (t - 1))
                        if K >= 4:
                            pe.wait_ge(a_in[K % 2], (K - 4) // 2 + 1)
                        for n in range(2):
                            m = 2 * h + n
                            ins = mm(a_bank(K)[:, 256 * n:256 * (n + 1)], FT[:, J % 2, P * m:P * (m + 1)],
                                     DFTB, start=True, stop=True)
                        ins.then_inc(f1_mm, 1)

                transposes(0)
                for j in range(8):
                    if j < 7:
                        transposes(j + 1)
                    rows(j)
                pe.wait_ge(a_in[0], 8 * (t + 1))
                pe.wait_ge(a_in[1], 8 * (t + 1))

            def inner_dft(k, n):
                o = bank(n, 2, 2 * D)
                s, rows = z_slots(k)
                if rows == 1:
                    mm(o[:, 0, :], MF[:, k, 0, :], a_rows(s, 1), start=True, stop=True)
                    return mm(o[:, 1, :], MF[:, k, 1, :], a_rows(s, 1), start=True, stop=True)
                mm(PS[n][:, :], MF[:, k, 0, :], a_rows(s, 2), start=True, stop=False, skip_group_check=True)
                mm(o[:, 1, :], MF[:, k, 1, :], a_rows(s, 1), start=False, stop=False, skip_group_check=True)
                return mm(o[:, 0, :], MF[:, k, 2, :], a_rows(s + 1, 1), start=False, stop=True, skip_group_check=True)

            def inner_idft(k, n, ys):
                o = bank(n, 2, 2 * D)
                if z_slots(k)[1] == 1:
                    mm(o[:, 0, :], MI[:, k, 0, :], ys[:, 0, :], start=True, stop=False)
                    return mm(o[:, 0, :], MI[:, k, 1, :], ys[:, 1, :], start=False, stop=True)
                mm(PS[n][:, :], MI[:, k, 0, :], ys, start=True, stop=False, skip_group_check=True)
                mm(o[:, 0, :], MI[:, k, 1, :], ys[:, 1, :], start=False, stop=False, skip_group_check=True)
                return mm(o[:, 1, :], MI[:, k, 2, :], ys[:, 0, :], start=False, stop=True, skip_group_check=True)

            pe.wait_ge(h_ready, NI // 2)
            pe.wait_ge(h_dec, NI // 2)
            block_dft(0, HT)
            pe.wait_ge(ld_dft, 16)
            for k in range(NK):
                if k >= 3:
                    pe.wait_ge(spec_act if (k - 3) % 2 else spec_dve, (k - 3) // 2 + 1)
                inner_dft(k, k % 3).then_inc(f2_mm, 1)
            pe.wait_ge(spec_act, NK // 2)
            pe.wait_ge(spec_dve, NK - NK // 2)
            pe.wait_ge(ld_idft, 16)
            for c in range(2):
                block_dft(c + 1, VG)
                for k in range(NK + 2):
                    if k < NK:
                        q = NK * c + k
                        if q >= 3:
                            pe.wait_ge(prod_in, q - 2)
                        inner_dft(k, q % 3).then_inc(f2_mm, 1)
                    if k >= 2:
                        q = NK * c + k - 2
                        pe.wait_ge(y_in, q + 1)
                        if q >= 3:
                            pe.wait_ge(z_in, q - 2)
                        inner_idft(k - 2, 3 + q % 3, YS[:, q % 2]).then_inc(i1_mm, 1)
                pe.wait_ge(z_in, NK * (c + 1))
                for p in range(18):
                    if p < 16:
                        q = 16 * c + p
                        if q >= 4:
                            pe.wait_ge(zt_in, q - 3)
                        for n in range(4):
                            ins = nc.tensor.transpose(PS[4 + q % 4][:, P * n:P * (n + 1)], A[:, 4 * p + n], IDENT)
                        ins.then_inc(i2_mm, 1)
                    if p >= 2:
                        q = 16 * c + p - 2
                        pe.wait_ge(zt_in, q + 1)
                        R = q // 2
                        if q % 2 == 0 and R >= 4:
                            pe.wait_ge(gated, R - 3)
                        for n in range(4):
                            ins = mm(PS[R % 4][:, 256 * (q % 2) + 64 * n:256 * (q % 2) + 64 * (n + 1)],
                                     ZT[:, q % 4, P * n:P * (n + 1)], IDFTB, start=True, stop=True)
                        ins.then_inc(i3_mm, 1)
            def gates(ck, t):
                if ck:
                    pe.wait_ge(sq_in, TPC * ck + t)
                elif t >= 2:
                    pe.wait_ge(sq_in, t - 1)
                if t == 0:
                    pe.wait_ge(x_lo, ck + 1)
                at = slice(P * t, P * (t + 1))
                split_product(PS[gate_bank(ck, t)][:, :], (XHI[:, ck % 2, at], XLO[:, ck % 2, at]),
                              (WAH[:, :, :], WAL[:, :, :])).then_inc(gh_mm, 1)

            def weights_back(ck):
                pe.wait_ge(w1_in, ck + 1)
                nc.tensor.transpose(PS[router_bank(ck)][0:TPC * 8, 0:P], WGT1, IDENT).then_inc(wt1_mm, 1)

            for st in range(STEPS):
                if st < NCH:
                    if st % (NCH // B) == 0:
                        pe.wait_ge(gated, 8 + st + 4)
                    if st:
                        pe.wait_ge(vt_in, st)
                    for t in range(TPC):
                        ins = nc.tensor.transpose(PS[6][:, P * t:P * (t + 1)], V[:, TPC * st + t, :], IDENT)
                    ins.then_inc(vt_mm, 1)
                if 1 <= st <= NCH:
                    j = st - 1
                    pe.wait_ge(vt_in, j + 1)
                    if j:
                        pe.wait_ge(o_added, j)
                    for t in range(TPC):
                        ins = mm(PS[7][:, D * t:D * (t + 1)], VT[:, j % 2, P * t:P * (t + 1)], WOUT,
                                 start=True, stop=True)
                    ins.then_inc(o_mm, 1)
                if 4 <= st < NCH + 4:
                    if st == 4:
                        pe.wait_ge(ld_w1, N_W1)
                    pe.wait_ge(xnt1_in, st - 3)
                    for j in (2 * (st - 4), 2 * (st - 4) + 1):
                        if j >= 2:
                            pe.wait_ge(kv_bias, j - 1)
                        for i in range(2):
                            t = 2 * j + i
                            ins = mm(PS[1 + j % 2][:, 256 * i:256 * (i + 1)], XNT1[:, P * t:P * (t + 1)], WKV,
                                     start=True, stop=True)
                        ins.then_inc(kv_mm, 1)
                if 3 <= st < NCH + 3:
                    j = st - 3
                    pe.wait_ge(ln1_xn, j + 1)
                    if j:
                        pe.wait_ge(xnt1_in, j)
                    else:
                        pe.wait_ge(gated, 16)
                    for t in range(TPC):
                        ins = nc.tensor.transpose(PS[0][:, P * t:P * (t + 1)], XNR[:, j % 2, t, :], IDENT)
                    ins.then_inc(xnt1_mm, 1)
                if 5 <= st < NCH + 5:
                    for i in (2 * (st - 5), 2 * (st - 5) + 1):
                        pe.wait_ge(k_fm, i + 1)
                        for h in range(2):
                            t = 2 * i + h
                            mm(PS[5][:, 256 * (t // NI):256 * (t // NI) + P + 1], KVS[:, i % 3, h, 0:P], KVS[:, i % 3, h, P:2 * P + 1],
                               start=(t % NI == 0), stop=(t % NI == NI - 1)).then_inc(kvs_mm, 1)
                if st == PREP_AT:
                    pe.wait_ge(wa_lo, 1)
                    for t in range(TPC):
                        gates(0, t)
                if COMP_AT <= st < COMP_AT + PAIRS:
                    q = st - COMP_AT
                    if q:
                        pe.wait_ge(gw_lo, q)
                    else:
                        pe.wait_ge(sq_in, TPC)
                    for n in range(2):
                        ins = mm(bank(4, 4, P)[:, 2 * n:2 * n + 2, :], WAT[:, q, :],
                                 WB1[:, 4 * q + 2 * n:4 * q + 2 * n + 2, :], start=True, stop=True)
                    ins.then_inc(comp_mm, 1)
                if st == PREP_AT + 6:
                    weights_back(0)

            def down1_step(n):
                q, m = divmod(n, 2)
                if m == 0 and q >= 2:
                    pe.wait_ge(scaled, q - 1)
                pe.wait_ge(am_lo, n + 1)
                w, s = n % M1, n % 4
                split_product(PS[4 + q % 2][:, :], (DNH[:, w, :], DNL[:, w, :]), (AMH[:, s, :], AML[:, s, :]),
                              start=(m == 0), stop=(m == 1)).then_inc(down1_mm, 1)

            def attention_out(ck):
                pe.wait_ge(att_in, ck + 1)
                mm(PS[7][:, :], WO, ATT, start=True, stop=True).then_inc(wo_mm, 1)

            def back(ck):
                pe.wait_ge(ot_in, ck + 1)
                for t in range(TPC):
                    ins = nc.tensor.transpose(PS[7][:, P * t:P * (t + 1)], OT1[:, P * t:P * (t + 1)], IDENT)
                ins.then_inc(y_mm, 1)

            pe.wait_ge(kv_mask, B)
            pe.wait_ge(wt1_in, 1)
            pe.wait_ge(gw_lo, PAIRS)
            pe.wait_ge(up_lo, W_PARTS)
            pe.wait_ge(dn_lo, W_PARTS)
            for n in range(NCH * M1 + LAG):
                ck, m = divmod(n, M1)
                if n < NCH * M1:
                    x = (XHI[:, ck % 2, :], XLO[:, ck % 2, :])
                    if n >= 2:
                        pe.wait_ge(silu1, n - 1)
                    split_product(PS[n % 2][:, :], (GWH[:, m, :], GWL[:, m, :]), x).then_inc(g1_mm, 1)
                    if n >= 2:
                        pe.wait_ge(mult1, n - 1)
                    split_product(PS[2 + n % 2][:, :], (UPH[:, m, :], UPL[:, m, :]), x).then_inc(u1_mm, 1)
                if n >= LAG:
                    down1_step(n - LAG)
                if ck and m == WO_AT:
                    attention_out(ck - 1)
                if 0 < ck < NCH and m == BACK_AT:
                    back(ck - 1)
                if ck + 1 < NCH:
                    if GH_AT <= m < GH_AT + TPC:
                        gates(ck + 1, m - GH_AT)
                    if m == WT_AT:
                        weights_back(ck + 1)
                if ck < NCH:
                    if m == Q_AT:
                        pe.wait_ge(sq_in, TPC * min(ck + 2, NCH))
                        mm(PS[6][:, :], WQ, XNT1[:, CH * ck:CH * (ck + 1)], start=True, stop=True).then_inc(q_mm, 1)
                    if m == ND_AT:
                        b = ck // (NCH // B)
                        pe.wait_ge(q_fm, ck + 1)
                        pe.wait_ge(wt1_in, min(ck + 2, NCH))
                        mm(PS[6][:, :], KVB[:, b, :], QPS, start=True, stop=True)
                        mm(PS[7][:, :], KSB[:, b, :], QPS, start=True, stop=True).then_inc(nd_mm, 1)
            back(NCH - 1)


_OUT = ((B, L, D), "float32")


def _constants():
    f32 = np.float32
    a, k2, i = np.arange(P), np.arange(P), np.arange(NI)
    mf = np.zeros((P, NK, 3, P))
    for k in range(NK):
        th = 2 * np.pi * (np.outer(a, k + K1 * k2) % (K1 * P)) / (K1 * P)
        mf[:, k, 0], mf[:, k, 1], mf[:, k, 2] = np.cos(th), -np.sin(th), np.sin(th)
    mi = mf.transpose(3, 1, 2, 0)
    slots = [(0, 0), (NK - 1, 0)] + [(k, r) for k in range(1, NK - 1) for r in range(2)]
    fw, iv = np.zeros((NI, 8, 2, K1, 4)), np.zeros((K1, 4, NI, 4))
    for s, (k, r) in enumerate(slots):
        th = 2 * np.pi * ((i * k) % K1) / K1
        row = -np.sin(th) if r else np.cos(th)
        weight = (1 if k in (0, NK - 1) else 2) / (K1 * P) / L
        for c in range(8):
            fw[:, c, c // 4, s, c % 4] = row
        for c in range(4):
            iv[s, c, :, c] = row * weight
    t = np.linspace(0.0, 1.0, L).astype(f32)
    bands = np.linspace(0.0, EMB - 1.0, EMB).astype(f32)
    pe = np.sin((t[:, None] * bands[None, :]).astype(f32) * f32(10.0)).astype(f32)
    ch = np.arange(D)
    edges = np.zeros((P, 2))
    edges[0, 0] = edges[P - 1, 1] = 1
    before = np.broadcast_to((np.arange(8)[None, :] < np.arange(8)[:, None]), (P, 8, 8))
    tables = {
        "dft_f": mf, "dft_i": mi, "dft_b": fw.reshape(P, K1 * 8), "idft_b": iv.reshape(P, NI * 4),
        "negt": -t.reshape(NI, P).T, "ident": np.eye(P), "before": before, "heads": (ch[:, None] // 8 == ch[None, :] // 8),
        "edges": edges, "peT": pe.T,
    }
    return {k: np.ascontiguousarray(v, dtype=f32) for k, v in tables.items()}


def kernel(**inputs):
    import concourse.bacc as _bacc
    from concourse.bass_utils import run_bass_kernel_spmd as _run

    a = {k: np.asarray(v) for k, v in inputs.items()}
    g = lambda n: a["L0_attn_" + n]
    f = lambda n: a["L0_ffn_" + n]
    h = lambda n: a["L1_attn_" + n]
    w = lambda n: a["L1_ffn_" + n]
    c = _constants()

    def pairs(m):
        return m.transpose(1, 0, 2).reshape(D, M0, P)

    arrays = {
        "x": g("u"), "w_inT": g("w_in").T, "conv_w": g("conv_w").T, "conv_b": g("conv_b"), "b_in": g("b_in"),
        "peT": c["peT"], "w1T": g("w1").T, "b1": g("b1")[:, None], "w2b": np.concatenate([g("w2").T, g("b2")[None]]),
        "fdec": g("filt_decay").reshape(-1), "fbias": g("filt_bias").reshape(-1), "w_outT": g("w_out").T,
        "b_out": g("b_out"), "rout_w": f("router_w"), "rout_b": f("router_bias").reshape(1),
        "gate0": np.concatenate([pairs(f("gate_w")), f("s_gate_w").reshape(D, 2, P)], axis=1),
        "up0": np.concatenate([pairs(f("up_w")), f("s_up_w").reshape(D, 2, P)], axis=1),
        "down0": np.concatenate([f("down_w").reshape(M0, P, D), f("s_down_w").reshape(2, P, D)]).transpose(1, 0, 2),
        "wq": h("wq"), "wkv": np.concatenate([h("wk"), h("wv")], axis=1),
        "bkv": np.concatenate([h("bk"), h("bv")]), "bq": h("bq")[:, None], "wo": h("wo"), "bo": h("bo")[:, None],
        "w_a": w("W_A").transpose(2, 0, 1).reshape(D, PAIRS, P),
        "w_at": w("W_A").reshape(PAIRS, P, D).transpose(1, 0, 2),
        "w_b": w("W_B").transpose(0, 2, 1).reshape(E1, R1, 2, P),
        "w_up": w("W_up").transpose(2, 0, 1).reshape(D, M1, P),
        "w_dn": w("W_down").transpose(0, 2, 1).reshape(M1, P, D).transpose(1, 0, 2),
    }
    for k in ("dft_f", "dft_i", "dft_b", "idft_b", "negt", "ident", "before", "heads", "edges"):
        arrays[k] = c[k]
    nc = _bacc.Bacc("TRN2", target_bir_lowering=False, num_devices=1)
    fed, args = {}, []
    for name, v in arrays.items():
        v = np.ascontiguousarray(v)
        fed[f"in_{name}"] = v
        args.append(nc.dram_tensor(f"in_{name}", v.shape, mybir.dt.from_np(v.dtype), kind="ExternalInput").ap())
    args.append(nc.dram_tensor("out_0", _OUT[0], F32, kind="ExternalOutput").ap())
    hyena_moe_program(nc, *args)
    r = _run(nc, [fed], core_ids=[0])
    return r.results[0]["out_0"]
```

```python
import math

import numpy as np

import concourse.bass as bass
from concourse import mybir
from contextlib import ExitStack

F32 = mybir.dt.float32
F32R = mybir.dt.float32r
ALU = mybir.AluOpType
ACT = mybir.ActivationFunctionType
AX = mybir.AxisListType

P = 128
B, L, D = 2, 2048, 128
NI = L // P
T = B * NI
TOK = B * L
CH = 512
NCH = TOK // CH
TPC = CH // P
OD = 3 * D
K1 = 2 * NI
NK = K1 // 2 + 1
EMB, FH = 33, 64
E0, I0, IS = 8, 64, 256
M0 = E0 * I0 // P
N0 = M0 + IS // P
E1, R1, F1W = 8, 64, 256
M1 = E1 * F1W // P
PAIRS = E1 // 2
EPS = 1e-5
XS_AT, GH_AT, RANK_AT, SUB_AT, EXP_AT, RW_AT, WT_AT = 0, 3, 8, 10, 11, 12, 14
Q_AT, QF_AT, ND_AT, WO_AT, OT_AT, BACK_AT, FIN_AT = 9, 13, 15, 3, 5, 7, 8
LAG = 3
XS0_AT, UP_AT, DN_AT, PREP_AT, COMP_AT = 4, 5, 11, 6, 7
W_PARTS = 4
STEPS = NCH + 5
RESULT_AT = (11, 13, 15)
EARLY = len(RESULT_AT)
ARENA_WORDS = 53000
ARENA_AT = 16640
Z_AT = 5
RT_STEPS = ((17, 19, 20, 21, 23, 24, 26, 28, 30), (0, 2, 3, 4, 5, 6, 7, 8, 10))
RT_EXP_AT, RT_BACK_AT = 1, (30, 9)
MAGIC = 12582912.0
PI2_HI = 6.28125
PI2_LO = 2 * math.pi - PI2_HI
PI_IN = 3.1415925


def hyena_moe_program(nc, x, w_inT, conv_w, conv_b, b_in, peT, w1T, b1, w2b, fdec, fbias, w_outT, b_out,
                      rout_w, rout_b, gate0, up0, down0, wq, wkv, bkv, bq, wo, bo, w_a, w_at, w_b, w_up, w_dn,
                      dft_f, dft_i, dft_b, idft_b, negt, ident, before, heads, edges,
                      out):
    wexp = [nc.dram_tensor(f"expert_weights_{n}", (T, 8, P), F32, kind="Internal").ap() for n in range(2)]
    ctx = ExitStack()
    with ctx:
        words = [0]
        arena = nc.alloc_sbuf_tensor_at("arena", [P, ARENA_WORDS], F32, offset=ARENA_AT)

        def region(n):
            at = words[0]
            words[0] += -(-n // 8) * 8
            assert words[0] <= ARENA_WORDS, words[0]
            return at

        def view(at, *dims, parts=P):
            n = int(np.prod(dims))
            v = arena[0:parts, at:at + n]
            if len(dims) == 1:
                return v
            names = "abcd"[:len(dims)]
            return v.rearrange("p (%s) -> p %s" % (" ".join(names), " ".join(names)),
                               **{c: d for c, d in zip(names, dims)})

        def split_part(name, at, *dims):
            n = int(np.prod(dims))
            names = "abcd"[:len(dims)]
            t = nc.alloc_sbuf_tensor_at(name, [P, n], F32R, offset=ARENA_AT + 4 * at)
            if len(dims) == 1:
                return t[:, :]
            return t[:, :].rearrange("p (%s) -> p %s" % (" ".join(names), " ".join(names)),
                                     **{c: d for c, d in zip(names, dims)})

        def split_view(name, at, *dims):
            return split_part(name + "_hi", at, *dims), split_part(name + "_lo", at + int(np.prod(dims)), *dims)

        IDENT = view(region(P), P)
        DFTB = view(region(K1 * 8), K1 * 8)
        IDFTB = view(region(NI * 4), NI * 4)
        NEGT = view(region(NI), NI)
        BEFORE = view(region(64), 8, 8)
        HEADS = view(region(P), P)
        EDGES = view(region(2), 2)
        ROUTB = view(region(1), 1)
        B1 = view(region(1), 1, parts=FH)
        BQ = view(region(1), 1)
        NBQ = view(region(1), 1)
        BO = view(region(1), 1)
        BOUT = view(region(D), D)
        MV = view(region(2 * T), T, 2)
        RSTD = view(region(T), T)
        STAT = view(region(6 * T), T, 6)
        HALF = view(region(16), 2, 8)

        rX = region(T * D)
        rG = region(T * 2 * D)
        rV = region(T * D)
        rH = region(NK * 2 * 2 * D)
        rA = region(K1 * 2 * D + 8)
        rY = region(4096)
        rF = region(NK * 3 * P)
        rI = region(NK * 3 * P)

        X = view(rX, T, D)
        G = view(rG, T, 2, D)
        V = view(rV, T, D)
        VG = view(rV, B * 16, NI, 8)
        H = view(rH, NK, 2, 2 * D)
        A = view(rA, 2 * D // 4, K1, 4)
        XNTH, XNTL = split_part("xnt_hi", rA, TOK + 2), split_part("xnt_lo", rI, TOK + 2)
        XN = view(rY, T, D)
        MF = view(rF, NK, 3, P)
        MI = view(rI, NK, 3, P)
        FT = view(rY, 2, CH)
        ZT = view(rY, 4, CH)
        T1 = view(rY + 1024, 2, 2, 2 * D)
        T2 = view(rY + 2048, 2, 2, 2 * D)
        YS = view(rY + 3072, 2, 2, 2 * D)
        WRES = view(rH + 4096, 3 * OD + E0)
        rB = rH + 4096 + 3 * (OD + E0)
        RBIAS = view(rB, 3, OD)
        CWB = view(rB + 3 * OD, 3, OD)
        BINB = view(rB + 6 * OD, OD)
        CBB = view(rB + 7 * OD, OD)
        WIN = view(rH + 3712, OD)
        assert rB + 8 * OD <= rA
        PET = view(rH, L, parts=EMB)
        SINT = view(rH + L, L, parts=FH + 1)
        SIN64 = view(rH + L, L, parts=FH)
        DEC = view(rH + 2 * L, NI, 2 * D)
        ZF = SIN64
        HT = view(rY, 2 * D // 8, NI, 8)
        r0 = rA + TOK + 8
        SG0 = view(r0, 2, CH)
        AM0 = view(r0 + 2 * CH, 3, CH)
        WRESH, WRESL = split_view("projection", r0, 3 * OD + E0)
        assert 2 * (3 * OD + E0) <= 5 * CH
        DW0 = view(r0 + 5 * CH, N0, P)
        WB0 = view(r0 + 5 * CH + N0 * P, M0, CH)
        UWH0, UWL0 = split_view("up_weights0", r0 + (5 + M0) * CH + N0 * P, N0, P)
        ZN = view(r0 + (5 + M0) * CH + 3 * N0 * P, L // 2, parts=FH)
        assert r0 + (5 + M0) * CH + 3 * N0 * P + L // 2 <= rF
        GWH0, GWL0 = split_view("gate_weights0", rI + TOK + 8, N0, P)
        SHIFTH, SHIFTL = split_view("shift", rI + TOK + 8 + 2 * N0 * P, 2, P)
        assert TOK + 8 + 2 * N0 * P + 4 * P <= NK * 3 * P
        GW0 = view(rF + 4096, N0, P)
        UW0 = view(rF + 4096 + N0 * P, N0, P)
        small = region(2 * 2 * D + FH + 2 * D + D)
        FDB = view(small, 2 * D)
        FBB = view(small + 2 * D, 2 * D)
        W1S = view(small + 4 * D, FH, parts=EMB)
        W2S = view(small + 4 * D + FH, 2 * D, parts=FH + 1)
        WOUT = view(small + 6 * D + FH, D)

        def router_scratch(at):
            return (view(at, T, 8), view(at + 256, T, 8), view(at + 512, T, 8), view(at + 768, T, 8),
                    view(at + 1024, T * 8), view(at + 1024, T, 8), view(at + 1280, 2, P), view(at + 1536, T),
                    view(at + 1536 + T, T))

        LOG, SCO, COR, RNK, WGT, WGT3, WTT, RED, RED2 = router_scratch(rF)
        CMP0 = (view(rF + 2048, NI, 8, 8), view(rF + 3072, NI, 8, 8))
        VT = view(rY + 3072, 2, CH)
        assert rY + 4096 == rF
        XNR = view(rY + 2048, 2, TPC, D)
        KVS = view(rG + TOK + 4 * CH, 3, 2, 2 * P + 1)
        KEX = view(rH + 7168, 3, 2, P)
        KVB = view(rH + 2400, B, P)
        KSB = view(rH + 2656, B, P)
        KSC = view(rH + 2912, B, 1)
        XNT1 = view(rG, TOK)
        XHI, XLO = split_view("x", rG + TOK, 2, CH)
        ACC1 = view(rG + TOK + 4 * CH, 2, CH)
        TMP1 = view(rG + TOK + 6 * CH, 2, CH)
        GWH, GWL = split_view("gate_weights", rH + 3072, M1, P)
        assert rH + 3072 + 2 * M1 * P <= rA
        WBC1 = view(rA, E1, CH)
        SQ1 = view(rA + 4096, TPC, E1, R1)
        q0 = rA + 6144
        LOG1, SCO1, COR1, RNK1 = (view(q0 + 32 * n, TPC, 8) for n in range(4))
        WGT1, WGT13 = view(q0 + 128, TPC * 8), view(q0 + 128, TPC, 8)
        WTT1 = view(q0 + 160, P, parts=TPC * 8)
        RED11, RED12 = view(q0 + 288, TPC), view(q0 + 292, TPC)
        CMP1 = (view(q0 + 320, TPC, 8, 8), view(q0 + 576, TPC, 8, 8))
        QEX, QPS, DEN, ATT = (view(rV + CH * n, CH) for n in range(4))
        rW = rF
        WA1 = view(rW, PAIRS, P)
        WAT = view(rW + 512, PAIRS, P)
        WB1 = view(rW + 1024, M1, P)
        UP1 = view(rW + 3072, M1, P)
        DN1 = view(rW + 5120, M1, P)
        UPH, UPL = split_view("up_weights", rW + 7168, M1, P)
        w0 = rW + 7168 + 2 * M1 * P
        WQ = view(w0, P)
        WKV = view(w0 + P, 2 * P)
        WO = view(w0 + 3 * P, P)
        BKV = view(w0 + 4 * P, 2 * P)
        WAH, WAL = split_view("router_weights", w0 + 6 * P, PAIRS, P)
        assert w0 + 14 * P <= rI + NK * 3 * P
        DNH, DNL = split_view("down_weights", rW + 1024, M1, P)
        SG1 = view(rY, 2, CH)
        AM1 = view(rY + 1024, 2, CH)
        AML = split_part("activations_lo", rY + 2048, 4, CH)
        AMH = split_part("activations_hi", rH, 4, CH)
        OT1 = view(rV + 4 * CH, CH)
        ST1 = view(q0 + 832, 2, TPC, D)
        assert q0 + 832 + 2 * CH <= rY

        PS = [ctx.enter_context(nc.psum_tensor(f"bank{n}", [P, CH], F32)) for n in range(8)]

        def bank(n, *dims, at=0):
            n_words = int(np.prod(dims))
            v = PS[n][:, at:at + n_words]
            names = "abcd"[:len(dims)]
            return v if len(dims) == 1 else v.rearrange(
                "p (%s) -> p %s" % (" ".join(names), " ".join(names)), **{c: d for c, d in zip(names, dims)})

        def sem(name):
            return ctx.enter_context(nc.semaphore(name))

        ld_const = sem("ld_const")
        ld_ident = sem("ld_ident")
        wo_mm = sem("wo_mm")
        ld_x = [sem(f"ld_x{n}") for n in range(4)]
        ld_res = sem("ld_res")
        ld_w0 = sem("ld_w0")
        ld_filt = sem("ld_filt")
        ld_pe = sem("ld_pe")
        ld_dft = sem("ld_dft")
        ld_idft = sem("ld_idft")
        ld_w1 = sem("ld_w1")
        ld_wexp0 = [sem(f"ld_wexp0_{m}") for m in range(M0)]
        ld_wexp1 = [sem(f"ld_wexp1_{e}") for e in range(E1)]
        st_wexp = sem("st_wexp")
        st_out = [sem("st_out_even"), sem("st_out_odd")]
        half_set = sem("half_set")
        ln_var = sem("ln_var")
        ln_rstd = sem("ln_rstd")
        ln_xn = sem("ln_xn")
        gw0_hi = sem("gw0_hi")
        gw0_lo = sem("gw0_lo")
        wres_hi = sem("wres_hi")
        wres_lo = sem("wres_lo")
        lnt_done = sem("lnt_done")
        xnt_lo = sem("xnt_lo")
        xnt_hi = sem("xnt_hi")
        rt_sub = sem("rt_sub")
        rt_exp = sem("rt_exp")
        rt_w = sem("rt_w")
        rt_tr = sem("rt_tr")
        rt_out = sem("rt_out")
        dve_chain = sem("dve_chain")
        pool_chain = sem("pool_chain")
        edge_set = sem("edge_set")
        res_mm = sem("res_mm")
        res_out = sem("res_out")
        bout_in = sem("bout_in")
        g_mm = sem("g_mm")
        u_mm = sem("u_mm")
        silu_done = sem("silu_done")
        mult_done = sem("mult_done")
        weighted = sem("weighted")
        down_mm = sem("down_mm")
        x_added = sem("x_added")
        z_mm = sem("z_mm")
        z_out = sem("z_out")
        z_wrapped = sem("z_wrapped")
        sin_done = sem("sin_done")
        ones_row = sem("ones_row")
        dec_exp = sem("dec_exp")
        h_mm = sem("h_mm")
        h_dec = sem("h_dec")
        h_ready = [sem("h_ready_even"), sem("h_ready_odd")]
        spec_act = sem("spec_act")
        spec_dve = sem("spec_dve")
        f0_mm = sem("f0_mm")
        ft_in = sem("ft_in")
        f1_mm = sem("f1_mm")
        a_in = [sem("a_in_dve"), sem("a_in_act")]
        f2_mm = sem("f2_mm")
        prod_in = sem("prod_in")
        y_in = sem("y_in")
        i1_mm = sem("i1_mm")
        z_in = sem("z_in")
        i2_mm = sem("i2_mm")
        zt_in = sem("zt_in")
        i3_mm = sem("i3_mm")
        gated = sem("gated")
        vt_mm = sem("vt_mm")
        vt_in = sem("vt_in")
        o_mm = sem("o_mm")
        o_added = sem("o_added")
        ln1_var = sem("ln1_var")
        ln1_rstd = sem("ln1_rstd")
        ln1_xn = sem("ln1_xn")
        xnt1_mm = sem("xnt1_mm")
        xnt1_in = sem("xnt1_in")
        log1_in = sem("log1_in")
        sqrt1 = sem("sqrt1")
        sub1 = sem("sub1")
        exp1 = sem("exp1")
        w1_in = sem("w1_in")
        wt1_mm = sem("wt1_mm")
        wt1_in = sem("wt1_in")
        st_wexp1 = sem("st_wexp1")
        wb_zero = sem("wb_zero")
        one_set = sem("one_set")
        kv_mm = sem("kv_mm")
        kv_bias = sem("kv_bias")
        q_neg = sem("q_neg")
        k_exp = sem("k_exp")
        k_fm = sem("k_fm")
        k_neg = sem("k_neg")
        kvs_mm = sem("kvs_mm")
        kv_mask = sem("kv_mask")
        gh_mm = sem("gh_mm")
        sq_in = sem("sq_in")
        comp_mm = sem("comp_mm")
        gw_hi = sem("gw_hi")
        gw_lo = sem("gw_lo")
        up_hi = sem("up_hi")
        up_lo = sem("up_lo")
        dn_hi = sem("dn_hi")
        dn_lo = sem("dn_lo")
        wa_hi = sem("wa_hi")
        wa_lo = sem("wa_lo")
        summed = sem("summed")
        scaled = sem("scaled")
        am_lo = sem("am_lo")
        x_hi = sem("x_hi")
        x_lo = sem("x_lo")
        q_mm = sem("q_mm")
        q_exp = sem("q_exp")
        q_fm = sem("q_fm")
        nd_mm = sem("nd_mm")
        att_in = sem("att_in")
        den_in = sem("den_in")
        g1_mm = sem("g1_mm")
        u1_mm = sem("u1_mm")
        silu1 = sem("silu1")
        mult1 = sem("mult1")
        down1_mm = sem("down1_mm")
        ot_in = sem("ot_in")
        y_mm = sem("y_mm")
        y_sum = sem("y_sum")

        N_CONST = 12 * 16
        N_W1 = 16 * 16
        block = ctx.enter_context(nc.Block())

        F1_BANKS = (4, 5, 0, 1)

        def a_bank(K):
            return PS[F1_BANKS[K % 4]][:, :]

        def a_slot(n):
            return arena[:, rA + CH * n:rA + CH * (n + 1)]

        def a_rows(s, n):
            return A[:, :, s:s + n, :].rearrange("p g s c -> p s g c")

        def h_blocks(j):
            return HT[:, :, 2 * j:2 * j + 2, :].rearrange("p g i c -> p i g c")

        def tap(v, d, n=OD):
            at = OD * (0, 2, 1)[d]
            return v[:, at:at + n]

        def filter_bias(engine, j):
            hv = h_blocks(j)
            return engine.tensor_tensor(out=hv, in0=hv, in1=FBB.rearrange("p (g c) -> p g c", c=8).unsqueeze(1)
                                        .broadcast_to((P, 2, 2 * D // 8, 8)), op=ALU.add)

        def z_slots(k):
            return (0, 1) if k == 0 else (1, 1) if k == NK - 1 else (2 * k, 2)

        def add_down(dve, ck):
            dve.wait_ge(down_mm, N0 * (ck + 1))
            xs = X[:, TPC * ck:TPC * (ck + 1), :]
            nc.vector.tensor_tensor(out=xs, in0=bank(4 + ck % 2, TPC, D), in1=xs, op=ALU.add).then_inc(x_added, 1)

        outv = out.rearrange("b (i a) c -> a (b i) c", a=P)

        def store(sp, ck):
            sp.wait_ge(y_sum, ck + 1)
            sp.dma_start(outv[:, TPC * ck:TPC * (ck + 1), :], ST1[:, ck % 2]).then_inc(st_out[ck % 2], 16)

        def gate_bank(ck, t):
            return 6 if ck else 3 + t % 2

        def gate_square(act, ck, t):
            act.wait_ge(gh_mm, TPC * ck + t + 1)
            if ck and t == 0:
                act.wait_ge(log1_in, TPC * ck)
            nc.scalar.activation(SQ1[:, t, :, :], bank(gate_bank(ck, t), E1, R1), ACT.Square).then_inc(sq_in, 1)

        def split_hi(act, ck):
            if ck >= 2:
                act.wait_ge(u1_mm, M1 * (ck - 1))
            else:
                act.wait_ge(xnt1_in, ck + 1)
            nc.scalar.activation(XHI[:, ck % 2, :], XNT1[:, CH * ck:CH * (ck + 1)], ACT.Copy).then_inc(x_hi, 1)

        def split_lo(pool, ck):
            pool.wait_ge(x_hi, ck + 1)
            nc.gpsimd.tensor_tensor(out=XLO[:, ck % 2, :], in0=XNT1[:, CH * ck:CH * (ck + 1)],
                                    in1=XHI[:, ck % 2, :].bitcast(F32), op=ALU.subtract).then_inc(x_lo, 1)

        def router_root(pool, ck, t):
            pool.wait_ge(log1_in, TPC * ck + t + 1)
            nc.gpsimd.tensor_tensor(out=SCO1[:, t, :], in0=LOG1[:, t, :], in1=HALF[:, 1, :], op=ALU.pow)\
              .then_inc(sqrt1, 1)

        def router_exp(act, ck):
            act.wait_ge(sub1, ck + 1)
            nc.scalar.activation(SCO1, SCO1, ACT.Exp).then_inc(exp1, 1)

        @block.sync
        def _(sp):
            xv = x.rearrange("b (i a) c -> a (b i) c", a=P)
            sp.dma_start(IDENT, ident).then_inc(ld_ident, 16)
            for n in range(4):
                sp.dma_start(X[:, 8 * n:8 * n + 8, :], xv[:, 8 * n:8 * n + 8, :]).then_inc(ld_x[n], 16)
            for dst, src in ((WRES[:, 3 * OD:3 * OD + E0], rout_w), (ROUTB, rout_b.partition_broadcast(P)),
                             (BEFORE, before), (EDGES, edges), (BOUT, b_out.partition_broadcast(P)), (DFTB, dft_b),
                             (IDFTB, idft_b), (NEGT, negt), (HEADS, heads), (B1, b1), (BQ, bq),
                             (BO, bo)):
                sp.dma_start(dst, src).then_inc(ld_const, 16)
            for dst, src in ((W1S, w1T), (W2S, w2b), (FDB, fdec.partition_broadcast(P)),
                             (FBB, fbias.partition_broadcast(P)), (WOUT, w_outT)):
                sp.dma_start(dst, src).then_inc(ld_filt, 16)
            sp.dma_start(PET, peT).then_inc(ld_pe, 16)
            sp.wait_ge(lnt_done, NCH)
            for dst, src in ((GW0, gate0), (UW0, up0), (DW0, down0)):
                sp.dma_start(dst, src).then_inc(ld_w0, 16)
            def expert_weights(n):
                sp.wait_ge(rt_out, n + 1)
                sp.dma_start(wexp[0].rearrange("(n t) e a -> (t e) n a", n=2)[:, n, :], WTT[:, n, :])\
                  .then_inc(st_wexp, 16)
                sp.wait_ge(st_wexp, 16 * (n + 1))

            expert_weights(0)
            for ck in range(NCH):
                for m in range(M0):
                    if ck:
                        sp.wait_ge(weighted, M0 * (ck - 1) + m + 1)
                    for e2 in range(2):
                        src = wexp[0][TPC * ck:TPC * (ck + 1), 2 * m + e2, :]
                        sp.dma_start(WB0[64 * e2:64 * e2 + 64, m, :].rearrange("p (t a) -> p t a", a=P),
                                     src.partition_broadcast(64)).then_inc(ld_wexp0[m], 16)
                if ck == 1:
                    expert_weights(1)
                if ck >= 1:
                    ks = slice(3 * (ck - 1), min(3 * ck, NK))
                    if ks.start < NK:
                        sp.dma_start(MF[:, ks], dft_f[:, ks]).then_inc(ld_dft, 16)
            sp.wait_ge(u_mm, NCH * N0)
            sp.dma_start(MI, dft_i).then_inc(ld_idft, 16)
            sp.wait_ge(i1_mm, 2 * NK)
            sp.wait_ge(wb_zero, 1)
            for e in range(E1):
                h0 = 64 * (e % 2)
                sp.dma_start(WB1[h0:h0 + 64, 2 * e:2 * e + 2, :], w_b[e]).then_inc(ld_w1, 16)
            for dst, src in ((WA1, w_a), (WAT, w_at), (UP1, w_up), (DN1, w_dn), (WQ, wq), (WKV, wkv), (WO, wo),
                             (BKV, bkv.partition_broadcast(P))):
                sp.dma_start(dst, src).then_inc(ld_w1, 16)
            for ck in range(NCH):
                sp.wait_ge(wt1_in, ck + 1)
                sp.dma_start(wexp[1][TPC * ck:TPC * (ck + 1)].rearrange("t e a -> (t e) a"), WTT1)\
                  .then_inc(st_wexp1, 16)
                sp.wait_ge(st_wexp1, 16 * (ck + 1))
                for e in range(E1):
                    if ck:
                        sp.wait_ge(scaled, E1 * (ck - 1) + e + 1)
                    sp.dma_start(WBC1[:, e, :].rearrange("p (t a) -> p t a", a=P),
                                 wexp[1][TPC * ck:TPC * (ck + 1), e, :].partition_broadcast(P))\
                      .then_inc(ld_wexp1[e], 16)
                if ck >= 2:
                    store(sp, ck - 2)
            store(sp, NCH - 2)
            store(sp, NCH - 1)
            sp.wait_ge(st_out[0], 16 * NCH // 2)
            sp.wait_ge(st_out[1], 16 * NCH // 2)

        @block.gpsimd
        def _(pool):
            done = [0]

            def link(ins):
                done[0] += 1
                ins.then_inc(pool_chain, 1)
                pool.wait_ge(pool_chain, done[0])

            def fold(step):
                if step < 3:
                    link(nc.gpsimd.tensor_tensor(out=tap(WRES, step), in0=WIN, in1=CWB[:, step, :], op=ALU.mult))
                elif step < 6:
                    cw = CWB[:, step - 3, :]
                    link(nc.gpsimd.tensor_tensor(out=cw, in0=BINB, in1=cw, op=ALU.mult))
                elif step < 9:
                    link(nc.gpsimd.tensor_tensor(out=RBIAS[:, 0, :], in0=CWB[:, 0, :] if step == 6 else RBIAS[:, 0, :],
                                                 in1=CBB if step == 8 else CWB[:, step - 5, :], op=ALU.add))

            for n in range(4):
                pool.wait_ge(ln_var, n + 1)
                if n == 0:
                    pool.wait_ge(half_set, 2)
                rs = RSTD[:, 8 * n:8 * n + 8]
                nc.gpsimd.tensor_tensor(out=rs, in0=rs, in1=HALF[:, 0, :], op=ALU.pow).then_inc(ln_rstd, 1)
                if n == 1:
                    pool.wait_ge(ld_res, 64)
                if n == 2:
                    pool.wait_ge(wres_hi, 1)
                    nc.gpsimd.tensor_tensor(out=WRESL, in0=WRES, in1=WRESH.bitcast(F32),
                                            op=ALU.subtract).then_inc(wres_lo, 1)
                for step in ((), range(0, 3), range(3, 6), range(6, 9))[n]:
                    fold(step)
            pool.wait_ge(ld_const, N_CONST)
            for n, d in ((1, 0), (2, 2)):
                link(nc.gpsimd.tensor_scalar(out=CWB[:, d, :], in0=CWB[:, d, :], scalar1=EDGES[:, n - 1:n],
                                             scalar2=None, op0=ALU.mult))
                link(nc.gpsimd.tensor_tensor(out=RBIAS[:, n, :], in0=RBIAS[:, 0, :], in1=CWB[:, d, :],
                                             op=ALU.subtract))
            nc.gpsimd.memset(arena[FH:FH + 1, rH + L:rH + 2 * L], 1.0).then_inc(ones_row, 1)
            pool.wait_ge(ones_row, 1)
            nc.gpsimd.tensor_scalar(out=NBQ, in0=BQ, scalar1=-1.0, scalar2=None, op0=ALU.mult)
            for n, (whole, hi, lo) in enumerate(((GW0, GWH0, GWL0), (UW0, UWH0, UWL0))):
                pool.wait_ge(gw0_hi, n + 1)
                nc.gpsimd.tensor_tensor(out=lo[:, :, :], in0=whole, in1=hi[:, :, :].bitcast(F32), op=ALU.subtract)\
                  .then_inc(gw0_lo, 1)

            pool.wait_ge(ln_xn, 8)
            for n in range(NCH):
                ins = nc.gpsimd.tensor_tensor(out=X[:, TPC * n:TPC * (n + 1), :], in0=X[:, TPC * n:TPC * (n + 1), :],
                                              in1=BOUT.unsqueeze(1).broadcast_to((P, TPC, D)), op=ALU.add)
            ins.then_inc(bout_in, 1)

            for ck in range(NCH):
                for m in range(M0):
                    n = N0 * ck + m
                    pool.wait_ge(mult_done, n + 1)
                    pool.wait_ge(ld_wexp0[m], 32 * (ck + 1))
                    nc.gpsimd.tensor_tensor(out=AM0[:, n % 3, :], in0=AM0[:, n % 3, :], in1=WB0[:, m, :],
                                            op=ALU.mult).then_inc(weighted, 1)
            for j in range(0, NI // 2, 2):
                pool.wait_ge(h_dec, j + 1)
                filter_bias(nc.gpsimd, j).then_inc(h_ready[0], 1)
            for c in range(2):
                for k in range(NK):
                    q = NK * c + k
                    pool.wait_ge(prod_in, q + 1)
                    if q >= 2:
                        pool.wait_ge(i1_mm, q - 1)
                    s = q % 2
                    nc.gpsimd.tensor_tensor(out=YS[:, s, 0, :], in0=T1[:, s, 0, :], in1=T2[:, s, 1, :],
                                            op=ALU.subtract)
                    nc.gpsimd.tensor_tensor(out=YS[:, s, 1, :], in0=T1[:, s, 1, :], in1=T2[:, s, 0, :],
                                            op=ALU.add).then_inc(y_in, 1)
            pool.wait_ge(i1_mm, 2 * NK)
            nc.gpsimd.memset(WB1[:, :, :], 0.0).then_inc(wb_zero, 1)
            nc.gpsimd.memset(KVS[:, :, :, 2 * P:2 * P + 1], 1.0).then_inc(one_set, 1)
            for st in range(max(STEPS, DN_AT + W_PARTS)):
                if 1 <= st <= NCH:
                    pool.wait_ge(ln1_var, st)
                    rs = RSTD[:, TPC * (st - 1):TPC * st]
                    nc.gpsimd.tensor_tensor(out=rs, in0=rs, in1=HALF[:, 0, 0:TPC], op=ALU.pow).then_inc(ln1_rstd, 1)
                if 4 <= st < NCH + 4:
                    for j in (2 * (st - 4), 2 * (st - 4) + 1):
                        pool.wait_ge(k_exp, j + 1)
                        k = KVS[:, j % 3, :, 0:P]
                        nc.gpsimd.tensor_tensor(out=k, in0=k, in1=KEX[:, j % 3], op=ALU.add).then_inc(k_fm, 1)
                if st == XS0_AT:
                    pool.wait_ge(wa_hi, 1)
                    nc.gpsimd.tensor_tensor(out=WAL[:, :, :], in0=WA1, in1=WAH[:, :, :].bitcast(F32),
                                            op=ALU.subtract).then_inc(wa_lo, 1)
                    split_lo(pool, 0)
                if st in (PREP_AT + 1, PREP_AT + 2):
                    for t in (2 * (st - PREP_AT - 1), 2 * (st - PREP_AT - 1) + 1):
                        router_root(pool, 0, t)
                for at, whole, hi, lo, hi_in, lo_in in ((UP_AT, UP1, UPH, UPL, up_hi, up_lo),
                                                        (DN_AT, DN1, DNH, DNL, dn_hi, dn_lo)):
                    if at <= st < at + W_PARTS:
                        ms = slice(M1 // W_PARTS * (st - at), M1 // W_PARTS * (st - at + 1))
                        pool.wait_ge(hi_in, 1)
                        nc.gpsimd.tensor_tensor(out=lo[:, ms, :], in0=whole[:, ms, :], in1=hi[:, ms, :].bitcast(F32),
                                                op=ALU.subtract).then_inc(lo_in, 1)

            def accumulate(q):
                ck, e = divmod(q, E1)
                if e:
                    pool.wait_ge(scaled, q + 1)
                    acc = ACC1[:, ck % 2, :]
                    if e >= 2:
                        pool.wait_ge(summed, (E1 - 1) * ck + e - 1)
                    nc.gpsimd.tensor_tensor(out=acc, in0=acc, in1=TMP1[:, q % 2, :], op=ALU.add).then_inc(summed, 1)

            for n in range(NCH * M1 + LAG + 3):
                ck, m = divmod(n, M1)
                if n < NCH * M1:
                    pool.wait_ge(mult1, n + 1)
                    if n >= 4:
                        pool.wait_ge(down1_mm, n - 3)
                    nc.gpsimd.tensor_tensor(out=AML[:, n % 4, :], in0=AM1[:, n % 2, :],
                                            in1=AMH[:, n % 4, :].bitcast(F32), op=ALU.subtract).then_inc(am_lo, 1)
                if n >= LAG + 3 and (n - LAG - 3) % 2 == 0:
                    accumulate((n - LAG - 3) // 2)
                if ck + 1 < NCH:
                    if m == XS_AT:
                        split_lo(pool, ck + 1)
                    if GH_AT < m <= GH_AT + TPC:
                        router_root(pool, ck + 1, m - GH_AT - 1)

        @block.scalar
        def _(act):
            for dst, src in ((WIN, w_inT), (CWB, conv_w.rearrange("k o -> (k o)").partition_broadcast(P)
                                            .rearrange("p (k o) -> p k o", k=3)),
                             (BINB, b_in.partition_broadcast(P)), (CBB, conv_b.partition_broadcast(P))):
                act.dma_start(dst, src).then_inc(ld_res, 16)
            for j in range(NCH):
                act.wait_ge(lnt_done, j + 1)
                nc.scalar.activation(XNTH[:, 1 + CH * j:1 + CH * (j + 1)], PS[4 + j % 4][:, :], ACT.Copy)\
                  .then_inc(xnt_hi, 1)
                if j == 1:
                    act.wait_ge(pool_chain, 3)
                    act.wait_ge(ld_const, N_CONST)
                    nc.scalar.activation(WRESH, WRES, ACT.Copy).then_inc(wres_hi, 1)
            act.wait_ge(ld_w0, 48)
            nc.scalar.activation(GWH0[:, :, :], GW0, ACT.Copy).then_inc(gw0_hi, 1)
            nc.scalar.activation(UWH0[:, :, :], UW0, ACT.Copy).then_inc(gw0_hi, 1)

            def router0_exp(n):
                act.wait_ge(rt_sub, n + 1)
                sc = SCO[:, NI * n:NI * (n + 1), :]
                nc.scalar.activation(sc, sc, ACT.Exp).then_inc(rt_exp, 1)

            act.wait_ge(z_wrapped, 2)
            nc.scalar.activation(SIN64, ZF, ACT.Sin).then_inc(sin_done, 1)
            router0_exp(0)
            for n in range(NCH * N0):
                act.wait_ge(g_mm, n + 1)
                if n >= 2:
                    act.wait_ge(mult_done, n - 1)
                nc.scalar.activation(SG0[:, n % 2, :], PS[n % 2][:, :], ACT.Silu).then_inc(silu_done, 1)
                if n == RT_EXP_AT:
                    router0_exp(1)
                    nc.scalar.activation(FDB, FDB, ACT.Exp).then_inc(dec_exp, 1)
            act.wait_ge(dec_exp, 1)
            for i in range(NI):
                nc.scalar.activation(DEC[:, i, :], FDB, ACT.Exp, scale=NEGT[:, i:i + 1]).then_inc(dec_exp, 1)

            def block_copies(t):
                def ft(j):
                    J = 8 * t + j
                    act.wait_ge(f0_mm, J + 1)
                    if J >= 2:
                        act.wait_ge(f1_mm, 2 * (J - 1))
                    if t and j < 2:
                        act.wait_ge(i3_mm, 16 * (t - 1))
                    nc.scalar.activation(FT[:, J % 2, :], PS[6 + J % 2][:, :], ACT.Copy).then_inc(ft_in, 1)

                def a(j):
                    K = 16 * t + 2 * j + 1
                    act.wait_ge(f1_mm, K + 1)
                    nc.scalar.activation(a_slot(2 * j + 1), a_bank(K), ACT.Copy).then_inc(a_in[1], 1)

                ft(0)
                for j in range(8):
                    if j < 7:
                        ft(j + 1)
                    a(j)

            block_copies(0)
            for k in range(1, NK, 2):
                act.wait_ge(f2_mm, k + 1)
                nc.scalar.activation(H[:, k], bank(k % 3, 2, 2 * D), ACT.Copy).then_inc(spec_act, 1)
            def result_copy(st):
                if st < NCH:
                    act.wait_ge(vt_mm, st + 1)
                    if st >= 2:
                        act.wait_ge(o_mm, st - 1)
                    nc.scalar.activation(VT[:, st % 2, :], PS[6][:, :], ACT.Copy).then_inc(vt_in, 1)

            for c in range(2):
                block_copies(c + 1)
                for k in range(NK):
                    q = NK * c + k
                    act.wait_ge(i1_mm, q + 1)
                    s, n = z_slots(k)
                    nc.scalar.activation(a_rows(s, n), bank(3 + q % 3, n, 2 * D // 4, 4), ACT.Copy).then_inc(z_in, 1)
                for p in range(16):
                    q = 16 * c + p
                    act.wait_ge(i2_mm, q + 1)
                    if q >= 4:
                        act.wait_ge(i3_mm, q - 3)
                    nc.scalar.activation(ZT[:, q % 4, :], PS[4 + q % 2][:, :], ACT.Copy).then_inc(zt_in, 1)
                    if c == 1 and p in RESULT_AT:
                        result_copy(RESULT_AT.index(p))
            for st in range(EARLY, STEPS):
                result_copy(st)
                if 3 <= st < NCH + 3:
                    j = st - 3
                    act.wait_ge(xnt1_mm, j + 1)
                    nc.scalar.activation(XNT1[:, CH * j:CH * (j + 1)], PS[0][:, :], ACT.Copy).then_inc(xnt1_in, 1)
                if 4 <= st < NCH + 4:
                    for j in (2 * (st - 4), 2 * (st - 4) + 1):
                        act.wait_ge(kv_bias, j + 1)
                        if j >= 3:
                            act.wait_ge(k_fm, j - 2)
                        k = KVS[:, j % 3, :, 0:P]
                        nc.scalar.activation(KEX[:, j % 3], k, ACT.Relu, scale=-1.0).then_inc(k_neg, 1)
                        act.wait_ge(k_neg, j + 1)
                        nc.scalar.activation(k, k, ACT.Relu)
                        nc.scalar.activation(KEX[:, j % 3], KEX[:, j % 3], ACT.Exp, scale=-1.0).then_inc(k_exp, 1)
                if st == XS0_AT:
                    act.wait_ge(ld_w1, N_W1)
                    nc.scalar.activation(WAH[:, :, :], WA1, ACT.Copy).then_inc(wa_hi, 1)
                    split_hi(act, 0)
                if st == DN_AT:
                    act.wait_ge(comp_mm, PAIRS)
                    act.wait_ge(up_lo, W_PARTS)
                    nc.scalar.activation(DNH[:, :, :], DN1[:, :, :], ACT.Copy).then_inc(dn_hi, 1)
                if st == UP_AT:
                    nc.scalar.activation(UPH[:, :, :], UP1[:, :, :], ACT.Copy).then_inc(up_hi, 1)
                if st == PREP_AT:
                    for t in range(TPC):
                        gate_square(act, 0, t)
                if COMP_AT <= st < COMP_AT + PAIRS:
                    q = st - COMP_AT
                    act.wait_ge(comp_mm, q + 1)
                    nc.scalar.activation(GWH[:, 4 * q:4 * q + 4, :], bank(4, 4, P), ACT.Copy).then_inc(gw_hi, 1)
                if st == PREP_AT + 5:
                    router_exp(act, 0)

            for ck in range(NCH):
                for m in range(M1):
                    n = M1 * ck + m
                    act.wait_ge(g1_mm, n + 1)
                    if n >= 2:
                        act.wait_ge(mult1, n - 1)
                    nc.scalar.activation(SG1[:, n % 2, :], PS[n % 2][:, :], ACT.Silu).then_inc(silu1, 1)
                    if ck + 1 < NCH:
                        if m == XS_AT:
                            split_hi(act, ck + 1)
                        if GH_AT <= m < GH_AT + TPC:
                            gate_square(act, ck + 1, m - GH_AT)
                        if m == EXP_AT:
                            router_exp(act, ck + 1)
                    if m == Q_AT + 1:
                        act.wait_ge(q_mm, ck + 1)
                        if ck:
                            act.wait_ge(nd_mm, ck)
                        nc.scalar.activation(QEX, PS[6][:, :], ACT.Relu, bias=NBQ, scale=-1.0).then_inc(q_neg, 1)
                        nc.scalar.activation(QPS, PS[6][:, :], ACT.Relu, bias=BQ)
                    if m == EXP_AT:
                        act.wait_ge(q_neg, ck + 1)
                        nc.scalar.activation(QEX, QEX, ACT.Exp, scale=-1.0).then_inc(q_exp, 1)

        @block.vector
        def _(dve):
            done = [0]

            def link(ins):
                done[0] += 1
                ins.then_inc(dve_chain, 1)
                dve.wait_ge(dve_chain, done[0])

            def stats(t0, n):
                for t in range(t0, t0 + n):
                    ins = nc.vector.bn_stats(out=STAT[:, t, :], in_=X[:, t, :])
                link(ins)
                for t in range(t0, t0 + n):
                    ins = nc.vector.bn_aggr(out=MV[:, t, :], in_=STAT[:, t, :])
                link(ins)
                return nc.vector.tensor_scalar(out=RSTD[:, t0:t0 + n], in0=MV[:, t0:t0 + n, 1], scalar1=EPS,
                                               scalar2=None, op0=ALU.add)

            def normed(t, dst):
                return nc.vector.tensor_scalar(out=dst, in0=X[:, t, :], scalar1=MV[:, t, 0:1],
                                               scalar2=RSTD[:, t:t + 1], op0=ALU.subtract, op1=ALU.mult)

            def pairs_of(values, n):
                return (values.unsqueeze(2).broadcast_to((P, n, 8, 8)), values.unsqueeze(3).broadcast_to((P, n, 8, 8)))

            def rank_ties(values, ge, n):
                vj, ve = pairs_of(values, n)
                link(nc.vector.tensor_tensor(out=ge, in0=vj, in1=ve, op=ALU.is_ge))
                link(nc.vector.tensor_tensor(out=ge, in0=ge, in1=BEFORE.unsqueeze(1).broadcast_to((P, n, 8, 8)),
                                             op=ALU.mult))

            def rank_larger(values, ge, gt, n):
                vj, ve = pairs_of(values, n)
                link(nc.vector.tensor_tensor(out=gt, in0=vj, in1=ve, op=ALU.is_gt))
                link(nc.vector.tensor_tensor(out=ge, in0=ge, in1=gt, op=ALU.max))

            def chosen(ge, rnk, k):
                link(nc.vector.tensor_reduce(out=rnk, in_=ge, axis=AX.X, op=ALU.add))
                link(nc.vector.tensor_scalar(out=rnk, in0=rnk, scalar1=float(k), scalar2=None, op0=ALU.is_lt))

            def per_tile(v, n):
                return v.unsqueeze(2).broadcast_to((P, n, 8))

            def normalise(dst, src, red, inv, tiny, n):
                link(nc.vector.tensor_reduce(out=red, in_=src, axis=AX.X, op=ALU.add))
                if tiny:
                    link(nc.vector.tensor_scalar(out=red, in0=red, scalar1=tiny, scalar2=None, op0=ALU.add))
                link(nc.vector.reciprocal(inv, red))
                return nc.vector.tensor_tensor(out=dst, in0=src, in1=per_tile(inv, n), op=ALU.mult)

            nc.vector.memset(HALF[:, 0, :], -0.5).then_inc(half_set, 1)
            nc.vector.memset(HALF[:, 1, :], 0.5).then_inc(half_set, 1)
            dve.wait_ge(half_set, 2)
            for at in (XNTH[:, 0:1], XNTL[:, 0:1], XNTH[:, TOK + 1:TOK + 2], XNTL[:, TOK + 1:TOK + 2],
                       SHIFTH[:, 0, 0:1], SHIFTL[:, 0, 0:1], SHIFTH[:, 1, P - 1:P], SHIFTL[:, 1, P - 1:P]):
                nc.vector.tensor_scalar(out=at, in0=HALF[:, 1, 0:1], scalar1=0.0, scalar2=None, op0=ALU.mult)

            def transposed_lo(j):
                dve.wait_ge(xnt_hi, j + 1)
                at = slice(1 + CH * j, 1 + CH * (j + 1))
                nc.vector.tensor_tensor(out=XNTL[:, at], in0=PS[4 + j % 4][:, :], in1=XNTH[:, at].bitcast(F32),
                                        op=ALU.subtract).then_inc(xnt_lo, 1)

            for q in range(5):
                if q < 4:
                    dve.wait_ge(ld_x[q], 16)
                    stats(8 * q, 8).then_inc(ln_var, 1)
                if q:
                    dve.wait_ge(ln_rstd, q)
                    for t in range(8 * (q - 1), 8 * q):
                        ins = normed(t, XN[:, t, :])
                        if t % TPC == TPC - 1:
                            ins.then_inc(ln_xn, 1)
                if q >= 2:
                    transposed_lo(2 * (q - 2))
                    transposed_lo(2 * (q - 2) + 1)
            transposed_lo(6)
            transposed_lo(7)
            dve.wait_ge(xnt_lo, NCH)
            for sh, xn in ((SHIFTH, XNTH), (SHIFTL, XNTL)):
                nc.vector.tensor_copy(sh[:, 0, 1:P], xn[:, 1 + L:L + P].bitcast(F32))
                ins = nc.vector.tensor_copy(sh[:, 1, 0:P - 1], xn[:, L - P + 2:L + 1].bitcast(F32))
            ins.then_inc(edge_set, 1)

            def router0(n, step):
                half = slice(NI * n, NI * (n + 1))
                log, sco, cor, rnk, wgt = (v[:, half, :] for v in (LOG, SCO, COR, RNK, WGT3))
                red, red2 = RED[:, half], RED2[:, half]
                ge, gt = CMP0
                vj, ve = pairs_of(cor, NI)
                if step == 0:
                    link(nc.vector.tensor_reduce(out=red, in_=log, axis=AX.X, op=ALU.max))
                    nc.vector.tensor_tensor(out=sco, in0=log, in1=per_tile(red, NI), op=ALU.subtract)\
                      .then_inc(rt_sub, 1)
                if step == 1:
                    dve.wait_ge(rt_exp, n + 1)
                    link(normalise(wgt, sco, red, red2, None, NI))
                    link(nc.vector.tensor_scalar(out=cor, in0=wgt, scalar1=ROUTB, scalar2=None, op0=ALU.add))
                if step == 2:
                    link(nc.vector.tensor_tensor(out=ge, in0=vj, in1=ve, op=ALU.is_ge))
                if step == 3:
                    link(nc.vector.tensor_tensor(out=ge, in0=ge, in1=BEFORE.unsqueeze(1).broadcast_to((P, NI, 8, 8)),
                                                 op=ALU.mult))
                if step == 4:
                    link(nc.vector.tensor_tensor(out=gt, in0=vj, in1=ve, op=ALU.is_gt))
                if step == 5:
                    link(nc.vector.tensor_tensor(out=ge, in0=ge, in1=gt, op=ALU.max))
                if step == 6:
                    chosen(ge, rnk, 4)
                    link(nc.vector.tensor_tensor(out=cor, in0=rnk, in1=wgt, op=ALU.mult))
                if step == 7:
                    normalise(wgt, cor, red, red2, 1e-20, NI).then_inc(rt_w, 1)
                if step == 8:
                    dve.wait_ge(rt_tr, n + 1)
                    nc.vector.tensor_copy(WTT[:, n, :], PS[6 + n][:, 0:P]).then_inc(rt_out, 1)

            dve.wait_ge(pool_chain, 13)
            for t in range(T):
                dve.wait_ge(res_mm, t + 1)
                kind = 1 if t % NI == 0 else 2 if t % NI == NI - 1 else 0
                nc.vector.tensor_tensor(out=G[:, t, :, :], in0=bank(t % 4, 2, D),
                                        in1=RBIAS[:, kind, 0:2 * D].rearrange("p (g c) -> p g c", g=2), op=ALU.add)
                nc.vector.tensor_tensor(out=VG[:, 16 * (t // NI):16 * (t // NI) + 16, t % NI, :],
                                        in0=bank(t % 4, 16, 8, at=2 * D),
                                        in1=RBIAS[:, kind, 2 * D:OD].rearrange("p (g c) -> p g c", c=8),
                                        op=ALU.add)
                nc.vector.tensor_copy(LOG[:, t, :], PS[t % 4][:, OD:OD + E0]).then_inc(res_out, 1)
                if Z_AT <= t < Z_AT + 4:
                    i = t - Z_AT
                    dve.wait_ge(z_mm, i + 1)
                    nc.vector.tensor_scalar(out=ZF[:, CH * i:CH * (i + 1)], in0=PS[4 + i % 2][0:FH, :],
                                            scalar1=B1, scalar2=10.0, op0=ALU.add, op1=ALU.mult)\
                      .then_inc(z_out, 1)
                if t == Z_AT + 3:
                    dve.wait_ge(z_out, 4)
                if Z_AT + 4 <= t < Z_AT + 12:
                    half, step = divmod(t - Z_AT - 4, 4)
                    zf, zn = ZF[:, L // 2 * half:L // 2 * (half + 1)], ZN
                    if step == 0:
                        link(nc.vector.tensor_scalar(out=zn, in0=zf, scalar1=1 / (2 * math.pi), scalar2=MAGIC,
                                                     op0=ALU.mult, op1=ALU.add))
                        link(nc.vector.tensor_scalar(out=zn, in0=zn, scalar1=-MAGIC, scalar2=None, op0=ALU.add))
                    if step == 1:
                        link(nc.vector.scalar_tensor_tensor(out=zf, in0=zn, scalar=-PI2_HI, in1=zf, op0=ALU.mult,
                                                            op1=ALU.add))
                    if step == 2:
                        link(nc.vector.scalar_tensor_tensor(out=zf, in0=zn, scalar=-PI2_LO, in1=zf, op0=ALU.mult,
                                                            op1=ALU.add))
                    if step == 3:
                        nc.vector.tensor_scalar(out=zf, in0=zf, scalar1=PI_IN, scalar2=-PI_IN, op0=ALU.min,
                                                op1=ALU.max).then_inc(z_wrapped, 1)
                if t == RT_STEPS[0][0] or t == T - 1:
                    dve.wait_ge(res_out, t + 1)
                if t in RT_STEPS[0]:
                    router0(0, RT_STEPS[0].index(t))
            dve.wait_ge(bout_in, 1)
            for ck in range(NCH):
                for m in range(N0):
                    n = N0 * ck + m
                    dve.wait_ge(silu_done, n + 1)
                    dve.wait_ge(u_mm, n + 1)
                    if n >= 3:
                        dve.wait_ge(down_mm, n - 2)
                    nc.vector.tensor_tensor(out=AM0[:, n % 3, :], in0=PS[2 + n % 2][:, :], in1=SG0[:, n % 2, :],
                                            op=ALU.mult).then_inc(mult_done, 1)
                    if ck and m == 2:
                        add_down(dve, ck - 1)
                    if n in RT_STEPS[1]:
                        router0(1, RT_STEPS[1].index(n))
            add_down(dve, NCH - 1)
            for j in range(NI // 2):
                dve.wait_ge(dec_exp, 1 + 2 * (j + 1))
                dve.wait_ge(h_mm, j + 1)
                nc.vector.tensor_tensor(out=h_blocks(j), in0=bank(4 + j % 4, 2, 2 * D // 8, 8),
                                        in1=DEC[:, 2 * j:2 * j + 2, :].rearrange("p i (g c) -> p i g c", c=8),
                                        op=ALU.mult).then_inc(h_dec, 1)
                if j % 2:
                    dve.wait_ge(h_dec, j + 1)
                    filter_bias(nc.vector, j).then_inc(h_ready[1], 1)

            def block_copies(t):
                for j in range(8):
                    K = 16 * t + 2 * j
                    dve.wait_ge(f1_mm, K + 1)
                    nc.vector.tensor_copy(a_slot(2 * j), a_bank(K)).then_inc(a_in[0], 1)

            block_copies(0)
            for k in range(0, NK, 2):
                dve.wait_ge(f2_mm, k + 1)
                nc.vector.tensor_copy(H[:, k], bank(k % 3, 2, 2 * D)).then_inc(spec_dve, 1)
            def residual(j):
                dve.wait_ge(o_mm, j + 1)
                xs = X[:, TPC * j:TPC * (j + 1), :]
                nc.vector.tensor_tensor(out=xs, in0=bank(7, TPC, D), in1=xs, op=ALU.add).then_inc(o_added, 1)
                dve.wait_ge(o_added, j + 1)
                stats(TPC * j, TPC).then_inc(ln1_var, 1)

            def normalise1(j):
                dve.wait_ge(ln1_rstd, j + 1)
                if j >= 2:
                    dve.wait_ge(xnt1_mm, j - 1)
                for t in range(TPC):
                    ins = normed(TPC * j + t, XNR[:, j % 2, t, :])
                ins.then_inc(ln1_xn, 1)

            for c in range(2):
                block_copies(c + 1)
                if c == 0:
                    dve.wait_ge(spec_act, NK // 2)
                    dve.wait_ge(spec_dve, NK - NK // 2)
                for k in range(NK):
                    q = NK * c + k
                    dve.wait_ge(f2_mm, NK + q + 1)
                    if q >= 2:
                        dve.wait_ge(y_in, q - 1)
                    xs = bank(q % 3, 2, B, D)
                    for part, dst in ((0, T1), (1, T2)):
                        h = H[:, k, part, D * c:D * (c + 1)].unsqueeze(1).unsqueeze(1).broadcast_to((P, 2, B, D))
                        ins = nc.vector.tensor_tensor(out=dst[:, q % 2].rearrange("p r (b c) -> p r b c", b=B),
                                                      in0=xs, in1=h, op=ALU.mult)
                    ins.then_inc(prod_in, 1)
                for r in range(8):
                    R = 8 * c + r
                    dve.wait_ge(i3_mm, 2 * (R + 1))
                    b, c0 = r // 4, 32 * (r % 4)
                    gate = G[:, NI * b:NI * (b + 1), c, c0:c0 + 32].rearrange("p i (g s) -> p g i s", s=4)
                    if c:
                        dst = V[:, NI * b:NI * (b + 1), c0:c0 + 32].rearrange("p i (g s) -> p g i s", s=4)
                        nc.vector.tensor_tensor(out=dst, in0=bank(R % 4, 8, NI, 4), in1=gate, op=ALU.mult)\
                          .then_inc(gated, 1)
                        if r >= 6:
                            residual(r - 6)
                        if r == 7:
                            normalise1(0)
                        continue
                    for h in range(2):
                        dst = VG[:, 16 * b + 4 * (r % 4):16 * b + 4 * (r % 4) + 4, :, 4 * h:4 * h + 4]
                        ins = nc.vector.tensor_tensor(out=dst, in0=bank(R % 4, 8, NI, 4)[:, h:8:2],
                                                      in1=gate[:, h:8:2], op=ALU.mult)
                    ins.then_inc(gated, 1)
            def norm_sum(ck, t):
                dve.wait_ge(sq_in, TPC * ck + t + 1)
                nc.vector.tensor_reduce(out=LOG1[:, t, :], in_=SQ1[:, t, :, :], axis=AX.X, op=ALU.add)\
                  .then_inc(log1_in, 1)

            def router_rank(ck):
                dve.wait_ge(log1_in, TPC * (ck + 1))
                rank_ties(LOG1, CMP1[0], TPC)

            def router_rank_more():
                rank_larger(LOG1, *CMP1, TPC)

            def router_sub(ck):
                chosen(CMP1[0], RNK1, 2)
                dve.wait_ge(sqrt1, TPC * (ck + 1))
                link(nc.vector.tensor_reduce(out=RED11, in_=SCO1, axis=AX.X, op=ALU.max))
                nc.vector.tensor_tensor(out=SCO1, in0=SCO1, in1=per_tile(RED11, TPC), op=ALU.subtract)\
                  .then_inc(sub1, 1)

            def router_weights(ck):
                dve.wait_ge(exp1, ck + 1)
                link(nc.vector.tensor_tensor(out=COR1, in0=RNK1, in1=SCO1, op=ALU.mult))
                normalise(WGT13, COR1, RED11, RED12, None, TPC).then_inc(w1_in, 1)

            def weights_out(ck):
                dve.wait_ge(wt1_mm, ck + 1)
                if ck:
                    dve.wait_ge(st_wexp1, 16 * ck)
                nc.vector.tensor_copy(WTT1, PS[7][0:TPC * 8, 0:P]).then_inc(wt1_in, 1)

            dve.wait_ge(one_set, 1)
            for st in range(EARLY, STEPS):
                if st <= NCH:
                    residual(st - 1)
                if COMP_AT < st <= COMP_AT + PAIRS:
                    q = st - COMP_AT - 1
                    dve.wait_ge(gw_hi, q + 1)
                    ms = slice(4 * q, 4 * q + 4)
                    nc.vector.tensor_tensor(out=GWL[:, ms, :], in0=bank(4, 4, P), in1=GWH[:, ms, :].bitcast(F32),
                                            op=ALU.subtract).then_inc(gw_lo, 1)
                if 4 <= st < NCH + 4:
                    for j in (2 * (st - 4), 2 * (st - 4) + 1):
                        dve.wait_ge(kv_mm, j + 1)
                        if j >= 3:
                            dve.wait_ge(kvs_mm, 2 * (j - 2))
                        nc.vector.tensor_tensor(out=KVS[:, j % 3, :, 0:2 * P], in0=bank(1 + j % 2, 2, 2 * P),
                                                in1=BKV.unsqueeze(1).broadcast_to((P, 2, 2 * P)), op=ALU.add)\
                          .then_inc(kv_bias, 1)
                if st < NCH + 2:
                    normalise1(st - 2)
                if st in (PREP_AT + 1, PREP_AT + 2):
                    for t in (2 * (st - PREP_AT - 1), 2 * (st - PREP_AT - 1) + 1):
                        norm_sum(0, t)
                if st == PREP_AT + 3:
                    router_rank(0)
                    router_rank_more()
                if st == PREP_AT + 4:
                    router_sub(0)
                if st == PREP_AT + 5:
                    router_weights(0)
            def denominator(n):
                at = slice(P * n, P * (n + 1))
                nc.vector.reciprocal(DEN[:, at], DEN[:, at]).then_inc(den_in, 1)

            def scale(q):
                ck, e = divmod(q, E1)
                dve.wait_ge(down1_mm, 2 * (q + 1))
                dve.wait_ge(ld_wexp1[e], 16 * (ck + 1))
                if e == 0 and ck >= 2:
                    dve.wait_ge(ot_in, ck - 1)
                if e and q >= 2:
                    dve.wait_ge(summed, (E1 - 1) * ck + max(e - 2, 0))
                nc.vector.tensor_tensor(out=TMP1[:, q % 2, :] if e else ACC1[:, ck % 2, :], in0=PS[4 + q % 2][:, :],
                                        in1=WBC1[:, e, :], op=ALU.mult).then_inc(scaled, 1)

            def total(ck):
                dve.wait_ge(wo_mm, ck + 1)
                dve.wait_ge(summed, (E1 - 1) * (ck + 1))
                if ck:
                    dve.wait_ge(y_mm, ck)
                nc.vector.scalar_tensor_tensor(out=OT1, in0=PS[7][:, :], scalar=BO, in1=ACC1[:, ck % 2, :],
                                               op0=ALU.add, op1=ALU.add).then_inc(ot_in, 1)

            def finish(ck):
                dve.wait_ge(y_mm, ck + 1)
                if ck >= 2:
                    dve.wait_ge(st_out[ck % 2], 16 * (ck // 2))
                nc.vector.tensor_tensor(out=ST1[:, ck % 2], in0=bank(7, TPC, D),
                                        in1=X[:, TPC * ck:TPC * (ck + 1), :], op=ALU.add).then_inc(y_sum, 1)

            for n in range(NCH * M1 + LAG + 2):
                ck, m = divmod(n, M1)
                if ck < NCH:
                    dve.wait_ge(silu1, n + 1)
                    dve.wait_ge(u1_mm, n + 1)
                    if n >= 2:
                        dve.wait_ge(am_lo, n - 1)
                    nc.vector.tensor_tensor(out=AM1[:, n % 2, :], in0=PS[2 + n % 2][:, :], in1=SG1[:, n % 2, :],
                                            op=ALU.mult)
                    if n >= 4:
                        dve.wait_ge(down1_mm, n - 3)
                    nc.vector.tensor_tensor(out=AMH[:, n % 4, :], in0=PS[2 + n % 2][:, :], in1=SG1[:, n % 2, :],
                                            op=ALU.mult).then_inc(mult1, 1)
                if n == 0:
                    weights_out(0)
                if n == 1:
                    dve.wait_ge(kvs_mm, T)
                    for b in range(B):
                        nc.vector.tensor_tensor(out=KVB[:, b, :], in0=PS[5][:, 256 * b:256 * b + P], in1=HEADS, op=ALU.mult)
                        link(nc.vector.tensor_copy(KSC[:, b, :], PS[5][:, 256 * b + P:256 * b + P + 1]))
                        nc.vector.tensor_scalar(out=KSB[:, b, :], in0=HEADS, scalar1=KSC[:, b, :], scalar2=None,
                                                op0=ALU.mult).then_inc(kv_mask, 1)
                if n >= LAG + 2 and (n - LAG - 2) % 2 == 0:
                    scale((n - LAG - 2) // 2)
                if ck and m == OT_AT:
                    total(ck - 1)
                if ck and m == FIN_AT:
                    finish(ck - 1)
                if ck + 1 < NCH:
                    if GH_AT < m <= GH_AT + TPC:
                        norm_sum(ck + 1, m - GH_AT - 1)
                    if m == RANK_AT:
                        router_rank(ck + 1)
                    if m == RANK_AT + 1:
                        router_rank_more()
                    if m == SUB_AT:
                        router_sub(ck + 1)
                    if m == RW_AT:
                        router_weights(ck + 1)
                    if m == WT_AT:
                        weights_out(ck + 1)
                if ck < NCH:
                    if m == QF_AT:
                        dve.wait_ge(q_exp, ck + 1)
                        nc.vector.tensor_tensor(out=QPS, in0=QPS, in1=QEX, op=ALU.add).then_inc(q_fm, 1)
                    if m == ND_AT:
                        dve.wait_ge(nd_mm, ck + 1)
                        link(nc.vector.tensor_scalar(out=DEN, in0=PS[7][:, :], scalar1=1e-6, scalar2=None,
                                                     op0=ALU.add))
                        denominator(0)
                        denominator(1)
                if ck and m < 2:
                    denominator(m + 2)
                if ck and m == 1:
                    dve.wait_ge(den_in, TPC * ck)
                    if ck >= 2:
                        dve.wait_ge(wo_mm, ck - 1)
                    nc.vector.tensor_tensor(out=ATT, in0=PS[6][:, :], in1=DEN, op=ALU.mult).then_inc(att_in, 1)
            total(NCH - 1)
            finish(NCH - 1)

        @block.tensor
        def _(pe):
            mm = nc.tensor.matmul

            def router0_back(n):
                pe.wait_ge(rt_w, n + 1)
                nc.tensor.transpose(PS[6 + n][:, 0:P], WGT[:, P * n:P * (n + 1)], IDENT).then_inc(rt_tr, 1)

            def split_product(o, left, right, start=True, stop=True):
                (lh, ll), (rh, rl) = left, right
                mm(o, lh, rh, start=start, stop=False, skip_group_check=True)
                mm(o, lh, rl, start=False, stop=False, skip_group_check=True)
                return mm(o, ll, rh, start=False, stop=stop, skip_group_check=True)

            def project(t):
                c = min(t + 1, T - 1) // TPC
                pe.wait_ge(xnt_lo, c + 1)
                if t == NI - 1:
                    pe.wait_ge(edge_set, 1)
                if t >= 4:
                    pe.wait_ge(res_out, t - 3)
                for d in (1, 0, 2):
                    xt = [part[:, P * t + d:P * (t + 1) + d] for part in (XNTH, XNTL)]
                    if t == NI and d == 0:
                        xt = (SHIFTH[:, 0, :], SHIFTL[:, 0, :])
                    if t == NI - 1 and d == 2:
                        xt = (SHIFTH[:, 1, :], SHIFTL[:, 1, :])
                    n = OD + E0 if d == 1 else OD
                    ins = split_product(PS[t % 4][:, 0:n], xt, (tap(WRESH, d, n), tap(WRESL, d, n)),
                                        start=(d == 1), stop=(d == 2))
                ins.then_inc(res_mm, 1)

            pe.wait_ge(ld_ident, 16)
            for j in range(NCH):
                pe.wait_ge(ln_xn, j + 1)
                if j >= 4:
                    pe.wait_ge(xnt_lo, j - 3)
                for t in range(TPC):
                    ins = nc.tensor.transpose(PS[4 + j % 4][:, P * t:P * (t + 1)], XN[:, TPC * j + t, :], IDENT)
                ins.then_inc(lnt_done, 1)
                if j == 3:
                    pe.wait_ge(wres_lo, 1)
                if j in (3, 5):
                    project(j - 3)
                    project(j - 2)
            for t in range(4, T):
                project(t)
                if Z_AT - 1 <= t < Z_AT + 3:
                    i = t - Z_AT + 1
                    if i == 0:
                        pe.wait_ge(ld_filt, 80)
                        pe.wait_ge(ld_pe, 16)
                        pe.wait_ge(xnt_lo, NCH)
                    if i >= 2:
                        pe.wait_ge(z_out, i - 1)
                    mm(PS[4 + i % 2][0:FH, :], W1S, PET[:, CH * i:CH * (i + 1)], start=True, stop=True)\
                      .then_inc(z_mm, 1)
                if t == RT_BACK_AT[0]:
                    router0_back(0)
            pe.wait_ge(gw0_lo, 2)
            pe.wait_ge(res_out, T)

            def down0_step(n):
                ck, m = divmod(n, N0)
                if m < M0:
                    pe.wait_ge(weighted, M0 * ck + m + 1)
                else:
                    pe.wait_ge(mult_done, n + 1)
                if m == 0 and ck >= 2:
                    pe.wait_ge(x_added, ck - 1)
                for t in range(TPC):
                    ins = mm(PS[4 + ck % 2][:, D * t:D * (t + 1)], AM0[:, n % 3, P * t:P * (t + 1)],
                             DW0[:, m, :], start=(m == 0 and t == 0), stop=(m == N0 - 1), skip_group_check=True)
                ins.then_inc(down_mm, 1)

            for n in range(NCH * N0 + 2):
                if n < NCH * N0:
                    ck, m = divmod(n, N0)
                    xs = [part[:, 1 + CH * ck:1 + CH * (ck + 1)] for part in (XNTH, XNTL)]
                    if n >= 2:
                        pe.wait_ge(silu_done, n - 1)
                    split_product(PS[n % 2][:, :], (GWH0[:, m, :], GWL0[:, m, :]), xs).then_inc(g_mm, 1)
                    if n >= 2:
                        pe.wait_ge(mult_done, n - 1)
                    split_product(PS[2 + n % 2][:, :], (UWH0[:, m, :], UWL0[:, m, :]), xs).then_inc(u_mm, 1)
                if n >= 2:
                    down0_step(n - 2)
                if n == RT_BACK_AT[1]:
                    router0_back(1)

            pe.wait_ge(silu_done, NCH * N0)
            pe.wait_ge(mult_done, NCH * N0)
            pe.wait_ge(x_added, NCH)
            pe.wait_ge(sin_done, 1)
            pe.wait_ge(ones_row, 1)
            for j in range(NI // 2):
                if j >= 4:
                    pe.wait_ge(h_dec, j - 3)
                for i in range(2):
                    t = 2 * j + i
                    ins = mm(PS[4 + j % 4][:, 2 * D * i:2 * D * (i + 1)], SINT[:, P * t:P * (t + 1)], W2S,
                             start=True, stop=True)
                ins.then_inc(h_mm, 1)

            def block_dft(t, src):
                def transposes(j):
                    J = 8 * t + j
                    if t >= 2 and j % 4 == 0:
                        pe.wait_ge(gated, 8 * (t - 2) + j + 4)
                    if J >= 2:
                        pe.wait_ge(ft_in, J - 1)
                    for n in range(4):
                        g = 4 * j + n
                        ins = nc.tensor.transpose(PS[6 + J % 2][:, P * n:P * (n + 1)], src[:, g], IDENT)
                    ins.then_inc(f0_mm, 1)

                def rows(j):
                    J = 8 * t + j
                    pe.wait_ge(ft_in, J + 1)
                    for h in range(2):
                        K = 2 * J + h
                        if t >= 2 and j == 1:
                            pe.wait_ge(gated, 8 * (t - 1))
                        if K >= 4:
                            pe.wait_ge(a_in[K % 2], (K - 4) // 2 + 1)
                        for n in range(2):
                            m = 2 * h + n
                            ins = mm(a_bank(K)[:, 256 * n:256 * (n + 1)], FT[:, J % 2, P * m:P * (m + 1)],
                                     DFTB, start=True, stop=True)
                        ins.then_inc(f1_mm, 1)

                transposes(0)
                for j in range(8):
                    if j < 7:
                        transposes(j + 1)
                    rows(j)
                pe.wait_ge(a_in[0], 8 * (t + 1))
                pe.wait_ge(a_in[1], 8 * (t + 1))

            def inner_dft(k, n):
                o = bank(n, 2, 2 * D)
                s, rows = z_slots(k)
                if rows == 1:
                    mm(o[:, 0, :], MF[:, k, 0, :], a_rows(s, 1), start=True, stop=True)
                    return mm(o[:, 1, :], MF[:, k, 1, :], a_rows(s, 1), start=True, stop=True)
                mm(PS[n][:, :], MF[:, k, 0, :], a_rows(s, 2), start=True, stop=False, skip_group_check=True)
                mm(o[:, 1, :], MF[:, k, 1, :], a_rows(s, 1), start=False, stop=False, skip_group_check=True)
                return mm(o[:, 0, :], MF[:, k, 2, :], a_rows(s + 1, 1), start=False, stop=True, skip_group_check=True)

            def inner_idft(k, n, ys):
                o = bank(n, 2, 2 * D)
                if z_slots(k)[1] == 1:
                    mm(o[:, 0, :], MI[:, k, 0, :], ys[:, 0, :], start=True, stop=False)
                    return mm(o[:, 0, :], MI[:, k, 1, :], ys[:, 1, :], start=False, stop=True)
                mm(PS[n][:, :], MI[:, k, 0, :], ys, start=True, stop=False, skip_group_check=True)
                mm(o[:, 0, :], MI[:, k, 1, :], ys[:, 1, :], start=False, stop=False, skip_group_check=True)
                return mm(o[:, 1, :], MI[:, k, 2, :], ys[:, 0, :], start=False, stop=True, skip_group_check=True)

            pe.wait_ge(h_ready[0], NI // 4)
            pe.wait_ge(h_ready[1], NI // 4)
            pe.wait_ge(h_dec, NI // 2)
            block_dft(0, HT)
            pe.wait_ge(ld_dft, 16 * -(-NK // 3))
            for k in range(NK):
                if k >= 3:
                    pe.wait_ge(spec_act if (k - 3) % 2 else spec_dve, (k - 3) // 2 + 1)
                inner_dft(k, k % 3).then_inc(f2_mm, 1)
            pe.wait_ge(spec_act, NK // 2)
            pe.wait_ge(spec_dve, NK - NK // 2)
            pe.wait_ge(ld_idft, 16)
            def result(st):
                if st < NCH:
                    if st % (NCH // B) == 0:
                        pe.wait_ge(gated, 8 + st + 4)
                    if st:
                        pe.wait_ge(vt_in, st)
                    for t in range(TPC):
                        ins = nc.tensor.transpose(PS[6][:, P * t:P * (t + 1)], V[:, TPC * st + t, :], IDENT)
                    ins.then_inc(vt_mm, 1)
                if 1 <= st <= NCH:
                    j = st - 1
                    pe.wait_ge(vt_in, j + 1)
                    if j:
                        pe.wait_ge(o_added, j)
                    for t in range(TPC):
                        ins = mm(PS[7][:, D * t:D * (t + 1)], VT[:, j % 2, P * t:P * (t + 1)], WOUT,
                                 start=True, stop=True)
                    ins.then_inc(o_mm, 1)

            for c in range(2):
                block_dft(c + 1, VG)
                for k in range(NK + 2):
                    if k < NK:
                        q = NK * c + k
                        if q >= 3:
                            pe.wait_ge(prod_in, q - 2)
                        inner_dft(k, q % 3).then_inc(f2_mm, 1)
                    if k >= 2:
                        q = NK * c + k - 2
                        pe.wait_ge(y_in, q + 1)
                        if q >= 3:
                            pe.wait_ge(z_in, q - 2)
                        inner_idft(k - 2, 3 + q % 3, YS[:, q % 2]).then_inc(i1_mm, 1)
                pe.wait_ge(z_in, NK * (c + 1))
                for p in range(18):
                    if p < 16:
                        q = 16 * c + p
                        if q >= 2:
                            pe.wait_ge(zt_in, q - 1)
                        for n in range(4):
                            ins = nc.tensor.transpose(PS[4 + q % 2][:, P * n:P * (n + 1)], A[:, 4 * p + n], IDENT)
                        ins.then_inc(i2_mm, 1)
                    if p >= 2:
                        q = 16 * c + p - 2
                        pe.wait_ge(zt_in, q + 1)
                        R = q // 2
                        if q % 2 == 0 and R >= 4:
                            pe.wait_ge(gated, R - 3)
                        for n in range(4):
                            ins = mm(PS[R % 4][:, 256 * (q % 2) + 64 * n:256 * (q % 2) + 64 * (n + 1)],
                                     ZT[:, q % 4, P * n:P * (n + 1)], IDFTB, start=True, stop=True)
                        ins.then_inc(i3_mm, 1)
                    if c == 1 and p in RESULT_AT:
                        result(RESULT_AT.index(p))

            def gates(ck, t):
                if ck >= 2 and t == 0:
                    pe.wait_ge(att_in, ck - 1)
                elif ck:
                    pe.wait_ge(sq_in, TPC * ck + t)
                elif t >= 2:
                    pe.wait_ge(sq_in, t - 1)
                if t == 0:
                    pe.wait_ge(x_lo, ck + 1)
                at = slice(P * t, P * (t + 1))
                split_product(PS[gate_bank(ck, t)][:, :], (XHI[:, ck % 2, at], XLO[:, ck % 2, at]),
                              (WAH[:, :, :], WAL[:, :, :])).then_inc(gh_mm, 1)

            def weights_back(ck):
                pe.wait_ge(w1_in, ck + 1)
                nc.tensor.transpose(PS[7][0:TPC * 8, 0:P], WGT1, IDENT).then_inc(wt1_mm, 1)

            def key_value_sum(i):
                pe.wait_ge(k_fm, i + 1)
                for h in range(2):
                    t = 2 * i + h
                    mm(PS[5][:, 256 * (t // NI):256 * (t // NI) + P + 1], KVS[:, i % 3, h, 0:P],
                       KVS[:, i % 3, h, P:2 * P + 1], start=(t % NI == 0), stop=(t % NI == NI - 1)).then_inc(kvs_mm, 1)

            for st in range(EARLY, STEPS):
                result(st)
                if 4 <= st < NCH + 4:
                    if st == 4:
                        pe.wait_ge(ld_w1, N_W1)
                    pe.wait_ge(xnt1_in, st - 3)
                    for j in (2 * (st - 4), 2 * (st - 4) + 1):
                        if j >= 2:
                            pe.wait_ge(kv_bias, j - 1)
                        for i in range(2):
                            t = 2 * j + i
                            ins = mm(PS[1 + j % 2][:, 256 * i:256 * (i + 1)], XNT1[:, P * t:P * (t + 1)], WKV,
                                     start=True, stop=True)
                        ins.then_inc(kv_mm, 1)
                if 3 <= st < NCH + 3:
                    j = st - 3
                    pe.wait_ge(ln1_xn, j + 1)
                    if j:
                        pe.wait_ge(xnt1_in, j)
                    else:
                        pe.wait_ge(gated, 16)
                    for t in range(TPC):
                        ins = nc.tensor.transpose(PS[0][:, P * t:P * (t + 1)], XNR[:, j % 2, t, :], IDENT)
                    ins.then_inc(xnt1_mm, 1)
                if 5 <= st < NCH + 4:
                    key_value_sum(2 * (st - 5))
                    key_value_sum(2 * (st - 5) + 1)
                if st == PREP_AT:
                    pe.wait_ge(wa_lo, 1)
                    for t in range(TPC):
                        gates(0, t)
                if COMP_AT <= st < COMP_AT + PAIRS:
                    q = st - COMP_AT
                    if q:
                        pe.wait_ge(gw_lo, q)
                    else:
                        pe.wait_ge(sq_in, TPC)
                    for n in range(2):
                        ins = mm(bank(4, 4, P)[:, 2 * n:2 * n + 2, :], WAT[:, q, :],
                                 WB1[:, 4 * q + 2 * n:4 * q + 2 * n + 2, :], start=True, stop=True)
                    ins.then_inc(comp_mm, 1)

            def down1_step(n):
                q, m = divmod(n, 2)
                if n < M1 and n % 4 == 0:
                    pe.wait_ge(dn_lo, n // 4 + 1)
                if m == 0 and q >= 2:
                    pe.wait_ge(scaled, q - 1)
                pe.wait_ge(am_lo, n + 1)
                w, s = n % M1, n % 4
                split_product(PS[4 + q % 2][:, :], (DNH[:, w, :], DNL[:, w, :]), (AMH[:, s, :], AML[:, s, :]),
                              start=(m == 0), stop=(m == 1)).then_inc(down1_mm, 1)

            def attention_out(ck):
                pe.wait_ge(att_in, ck + 1)
                mm(PS[7][:, :], WO, ATT, start=True, stop=True).then_inc(wo_mm, 1)

            def back(ck):
                pe.wait_ge(ot_in, ck + 1)
                for t in range(TPC):
                    ins = nc.tensor.transpose(PS[7][:, P * t:P * (t + 1)], OT1[:, P * t:P * (t + 1)], IDENT)
                ins.then_inc(y_mm, 1)

            for n in range(NCH * M1 + max(LAG, WO_AT + 1)):
                ck, m = divmod(n, M1)
                if n < NCH * M1:
                    x = (XHI[:, ck % 2, :], XLO[:, ck % 2, :])
                    if ck == 0 and m % 4 == 0:
                        pe.wait_ge(gw_lo, m // 4 + 1)
                        pe.wait_ge(up_lo, m // 4 + 1)
                    if n == 0:
                        pe.wait_ge(sq_in, TPC)
                        pe.wait_ge(xnt1_in, NCH)
                        pe.wait_ge(kv_bias, 2 * NCH)
                    if n == 2:
                        pe.wait_ge(gw_lo, PAIRS)
                    if n == 4:
                        pe.wait_ge(kv_mask, B)
                    if n >= 2:
                        pe.wait_ge(silu1, n - 1)
                    split_product(PS[n % 2][:, :], (GWH[:, m, :], GWL[:, m, :]), x).then_inc(g1_mm, 1)
                    if n >= 2:
                        pe.wait_ge(mult1, n - 1)
                    split_product(PS[2 + n % 2][:, :], (UPH[:, m, :], UPL[:, m, :]), x).then_inc(u1_mm, 1)
                if n == 0:
                    key_value_sum(T // 2 - 2)
                    key_value_sum(T // 2 - 1)
                    weights_back(0)
                if LAG <= n < NCH * M1 + LAG:
                    down1_step(n - LAG)
                if ck and m == WO_AT:
                    attention_out(ck - 1)
                if 0 < ck < NCH and m == BACK_AT:
                    back(ck - 1)
                if ck + 1 < NCH:
                    if GH_AT <= m < GH_AT + TPC:
                        gates(ck + 1, m - GH_AT)
                    if m == WT_AT:
                        weights_back(ck + 1)
                if ck < NCH:
                    if m == Q_AT:
                        pe.wait_ge(sq_in, TPC * min(ck + 2, NCH))
                        mm(PS[6][:, :], WQ, XNT1[:, CH * ck:CH * (ck + 1)], start=True, stop=True).then_inc(q_mm, 1)
                    if m == ND_AT:
                        b = ck // (NCH // B)
                        pe.wait_ge(q_fm, ck + 1)
                        mm(PS[6][:, :], KVB[:, b, :], QPS, start=True, stop=True)
                        pe.wait_ge(wt1_in, min(ck + 2, NCH))
                        mm(PS[7][:, :], KSB[:, b, :], QPS, start=True, stop=True).then_inc(nd_mm, 1)
            back(NCH - 1)


_OUT = ((B, L, D), "float32")


def _constants():
    f32 = np.float32
    a, k2, i = np.arange(P), np.arange(P), np.arange(NI)
    mf = np.zeros((P, NK, 3, P))
    for k in range(NK):
        th = 2 * np.pi * (np.outer(a, k + K1 * k2) % (K1 * P)) / (K1 * P)
        mf[:, k, 0], mf[:, k, 1], mf[:, k, 2] = np.cos(th), -np.sin(th), np.sin(th)
    mi = mf.transpose(3, 1, 2, 0)
    slots = [(0, 0), (NK - 1, 0)] + [(k, r) for k in range(1, NK - 1) for r in range(2)]
    fw, iv = np.zeros((NI, 8, 2, K1, 4)), np.zeros((K1, 4, NI, 4))
    for s, (k, r) in enumerate(slots):
        th = 2 * np.pi * ((i * k) % K1) / K1
        row = -np.sin(th) if r else np.cos(th)
        weight = (1 if k in (0, NK - 1) else 2) / (K1 * P) / L
        for c in range(8):
            fw[:, c, c // 4, s, c % 4] = row
        for c in range(4):
            iv[s, c, :, c] = row * weight
    t = np.linspace(0.0, 1.0, L).astype(f32)
    bands = np.linspace(0.0, EMB - 1.0, EMB).astype(f32)
    pe = np.sin((t[:, None] * bands[None, :]).astype(f32) * f32(10.0)).astype(f32)
    ch = np.arange(D)
    edges = np.zeros((P, 2))
    edges[0, 0] = edges[P - 1, 1] = 1
    before = np.broadcast_to((np.arange(8)[None, :] < np.arange(8)[:, None]), (P, 8, 8))
    tables = {
        "dft_f": mf, "dft_i": mi, "dft_b": fw.reshape(P, K1 * 8), "idft_b": iv.reshape(P, NI * 4),
        "negt": -t.reshape(NI, P).T, "ident": np.eye(P), "before": before, "heads": (ch[:, None] // 8 == ch[None, :] // 8),
        "edges": edges, "peT": pe.T,
    }
    return {k: np.ascontiguousarray(v, dtype=f32) for k, v in tables.items()}


def kernel(**inputs):
    import concourse.bacc as _bacc
    from concourse.bass_utils import run_bass_kernel_spmd as _run

    a = {k: np.asarray(v) for k, v in inputs.items()}
    g = lambda n: a["L0_attn_" + n]
    f = lambda n: a["L0_ffn_" + n]
    h = lambda n: a["L1_attn_" + n]
    w = lambda n: a["L1_ffn_" + n]
    c = _constants()

    def pairs(m):
        return m.transpose(1, 0, 2).reshape(D, M0, P)

    arrays = {
        "x": g("u"), "w_inT": g("w_in").T, "conv_w": g("conv_w").T, "conv_b": g("conv_b"), "b_in": g("b_in"),
        "peT": c["peT"], "w1T": g("w1").T, "b1": g("b1")[:, None], "w2b": np.concatenate([g("w2").T, g("b2")[None]]),
        "fdec": g("filt_decay").reshape(-1), "fbias": g("filt_bias").reshape(-1), "w_outT": g("w_out").T,
        "b_out": g("b_out"), "rout_w": f("router_w"), "rout_b": f("router_bias").reshape(1),
        "gate0": np.concatenate([pairs(f("gate_w")), f("s_gate_w").reshape(D, 2, P)], axis=1),
        "up0": np.concatenate([pairs(f("up_w")), f("s_up_w").reshape(D, 2, P)], axis=1),
        "down0": np.concatenate([f("down_w").reshape(M0, P, D), f("s_down_w").reshape(2, P, D)]).transpose(1, 0, 2),
        "wq": h("wq"), "wkv": np.concatenate([h("wk"), h("wv")], axis=1),
        "bkv": np.concatenate([h("bk"), h("bv")]), "bq": h("bq")[:, None], "wo": h("wo"), "bo": h("bo")[:, None],
        "w_a": w("W_A").transpose(2, 0, 1).reshape(D, PAIRS, P),
        "w_at": w("W_A").reshape(PAIRS, P, D).transpose(1, 0, 2),
        "w_b": w("W_B").transpose(0, 2, 1).reshape(E1, R1, 2, P),
        "w_up": w("W_up").transpose(2, 0, 1).reshape(D, M1, P),
        "w_dn": w("W_down").transpose(0, 2, 1).reshape(M1, P, D).transpose(1, 0, 2),
    }
    for k in ("dft_f", "dft_i", "dft_b", "idft_b", "negt", "ident", "before", "heads", "edges"):
        arrays[k] = c[k]
    nc = _bacc.Bacc("TRN2", target_bir_lowering=False, num_devices=1)
    fed, args = {}, []
    for name, v in arrays.items():
        v = np.ascontiguousarray(v)
        fed[f"in_{name}"] = v
        args.append(nc.dram_tensor(f"in_{name}", v.shape, mybir.dt.from_np(v.dtype), kind="ExternalInput").ap())
    args.append(nc.dram_tensor("out_0", _OUT[0], F32, kind="ExternalOutput").ap())
    hyena_moe_program(nc, *args)
    r = _run(nc, [fed], core_ids=[0])
    return r.results[0]["out_0"]
```
